# Optimizing a Trainium2 kernel written in Bass

```python
import numpy as np
import jax
import jax.numpy as jnp

def _softmax(x, axis=-1):
    return jax.nn.softmax(x, axis=axis)

def _gelu(x):
    return jax.nn.gelu(x, approximate=True)

def _silu(x):
    return jax.nn.silu(x)

def _sigmoid(x):
    return jax.nn.sigmoid(x)

def _layernorm(x, axis=-1, eps=1e-05):
    m = jnp.mean(x, axis=axis, keepdims=True)
    v = jnp.var(x, axis=axis, keepdims=True)
    return (x - m) / jnp.sqrt(v + eps)

def _scatter_add(tgt, idx, src, axis=0):
    return tgt.at[idx].add(src)

def _segment_sum(src, seg, n):
    return jax.ops.segment_sum(src, seg, n)
kernel_name = 'mk_decoder_preln_d1_seqx_r8_83f4bb'

def setup_inputs(seed: int=0):
    np.random.seed(seed)
    _w = jnp.asarray

    def _rec_inputs():
        import jax
        import jax.numpy as jnp
        _rk = jax.random.key(seed)
        x = -0.0003929 + 0.9999 * jax.random.normal(jax.random.fold_in(_rk, 1), (64, 64, 128), jnp.float32)
        _lenS = 64 - jax.random.randint(jax.random.fold_in(_rk, 7), (64,), 0, max(1, 64 // 4) + 1, jnp.int32)
        _lenS2 = 64 - jax.random.randint(jax.random.fold_in(_rk, 8), (64,), 0, max(1, 64 // 4) + 1, jnp.int32)
        _ctx_768P = jax.random.normal(jax.random.fold_in(_rk, 11), (64, 16, 96), jnp.float32)
        _ctx_768c = jax.random.dirichlet(jax.random.fold_in(_rk, 511), 0.3 * jnp.ones((16,), jnp.float32), (64, 64))
        _ctx_768t = jnp.einsum('bsk,bkd->bsd', _ctx_768c, _ctx_768P)
        _ctx_768t = _ctx_768t * jax.lax.rsqrt(jnp.mean(jnp.square(_ctx_768t)) + 1e-12) * 0.953939
        ctx_768 = -0.00055796 + 0.999787 * (_ctx_768t + 0.3 * jax.random.normal(jax.random.fold_in(_rk, 611), (64, 64, 96), jnp.float32))
        return (x, ctx_768)
    x, ctx_768 = _rec_inputs()

    def _L0_attn_setup():
        import jax, jax.numpy as jnp
        import numpy as np
        import math
        B, T, E, H = (4, 256, 128, 16)
        D = E // H
        rng = jax.random.key(seed)
        k1, k2, k3, k4, k5 = jax.random.split(rng, 5)
        scale_w = 1.0 / math.sqrt(E)
        return {'query': jax.random.normal(k1, (B, T, E), jnp.float32), 'key': jax.random.normal(k2, (B, T, E), jnp.float32), 'value': jax.random.normal(k3, (B, T, E), jnp.float32), 'in_proj_weight': jax.random.normal(k4, (3 * E, E), jnp.float32) * scale_w, 'out_proj_weight': jax.random.normal(k5, (E, E), jnp.float32) * scale_w}
    _L0_attn_all = _L0_attn_setup()
    _L0_attn_in = {k: v for k, v in _L0_attn_all.items() if k in ('key', 'value', 'in_proj_weight', 'out_proj_weight')}
    del _L0_attn_all

    def _L0_xattn_setup():
        import jax, jax.numpy as jnp
        import numpy as np
        IMAGE_DIM = 128
        TEXT_DIM = 96
        NUM_HEADS = 16
        HEAD_DIM = IMAGE_DIM // NUM_HEADS
        key = jax.random.key(seed)
        ks = jax.random.split(key, 14)
        B, N, M = (4, 512, 64)
        s_img = 1.0 / np.sqrt(IMAGE_DIM)
        s_txt = 1.0 / np.sqrt(TEXT_DIM)
        s_ff = 1.0 / np.sqrt(2 * IMAGE_DIM)
        return {'x': jax.random.normal(ks[0], (B, N, IMAGE_DIM), jnp.float32), 'y': jax.random.normal(ks[1], (B, M, TEXT_DIM), jnp.float32), 'Wq': jax.random.normal(ks[2], (IMAGE_DIM, IMAGE_DIM), jnp.float32) * s_img, 'bq': jax.random.normal(ks[3], (IMAGE_DIM,), jnp.float32) * s_img, 'Wk': jax.random.normal(ks[4], (TEXT_DIM, IMAGE_DIM), jnp.float32) * s_txt, 'bk': jax.random.normal(ks[5], (IMAGE_DIM,), jnp.float32) * s_txt, 'Wv': jax.random.normal(ks[6], (TEXT_DIM, IMAGE_DIM), jnp.float32) * s_txt, 'bv': jax.random.normal(ks[7], (IMAGE_DIM,), jnp.float32) * s_txt, 'W1': jax.random.normal(ks[8], (IMAGE_DIM, 2 * IMAGE_DIM), jnp.float32) * s_img, 'b1': jax.random.normal(ks[9], (2 * IMAGE_DIM,), jnp.float32) * s_img, 'W2': jax.random.normal(ks[10], (2 * IMAGE_DIM, IMAGE_DIM), jnp.float32) * s_ff, 'b2': jax.random.normal(ks[11], (IMAGE_DIM,), jnp.float32) * s_ff}
    _L0_xattn_all = _L0_xattn_setup()
    _L0_xattn_in = {k: v for k, v in _L0_xattn_all.items() if k in ('Wq', 'bq', 'Wk', 'bk', 'Wv', 'bv', 'W1', 'b1', 'W2', 'b2')}
    del _L0_xattn_all

    def _L0_ffn_setup():
        import jax, jax.numpy as jnp
        import numpy as np
        EMBED = 128
        HEADS = 16
        HEAD_DIM = EMBED // HEADS
        NUM_EXPERTS = 8
        TOP_K = 2
        HIDDEN = (int(2 * (4 * EMBED) / 3) + 63) // 64 * 64
        SEQ = 256
        BATCH = 2
        ROPE_BASE = 10000.0
        EPS = 1e-06

        def _rope_tables(seq_len, dim):
            inv_freq = 1.0 / ROPE_BASE ** (np.arange(0, dim, 2, dtype=np.float32) / dim)
            t = np.arange(seq_len, dtype=np.float32)
            freqs = np.einsum('i,j->ij', t, inv_freq)
            emb = np.concatenate([freqs, freqs], axis=-1)
            return (jnp.asarray(np.cos(emb)), jnp.asarray(np.sin(emb)))

        def _rotate_half(x):
            x1, x2 = jnp.split(x, 2, axis=-1)
            return jnp.concatenate([-x2, x1], axis=-1)

        def _rmsnorm(x, w):
            return x * jax.lax.rsqrt(jnp.mean(x * x, axis=-1, keepdims=True) + EPS) * w

        def _attention(x, wq, wk, wv, wo):
            B, S, _ = x.shape
            q = (x @ wq).reshape(B, S, HEADS, HEAD_DIM).transpose(0, 2, 1, 3)
            k = (x @ wk).reshape(B, S, HEADS, HEAD_DIM).transpose(0, 2, 1, 3)
            v = (x @ wv).reshape(B, S, HEADS, HEAD_DIM).transpose(0, 2, 1, 3)
            cos, sin = _rope_tables(S, HEAD_DIM)
            cos = cos[None, None]
            sin = sin[None, None]
            q = q * cos + _rotate_half(q) * sin
            k = k * cos + _rotate_half(k) * sin
            scale = HEAD_DIM ** (-0.5)
            scores = jnp.einsum('bhqd,bhkd->bhqk', q, k) * scale
            causal = jnp.triu(jnp.ones((S, S), bool), k=1)
            scores = jnp.where(causal, -jnp.inf, scores)
            attn = jax.nn.softmax(scores, axis=-1)
            out = jnp.einsum('bhqk,bhkd->bhqd', attn, v)
            out = out.transpose(0, 2, 1, 3).reshape(B, S, EMBED)
            return out @ wo

        def _moe(x, w_router, wg, wu, wd):
            B, S, E = x.shape
            xf = x.reshape(-1, E)
            logits = xf @ w_router
            probs = jax.nn.softmax(logits, axis=-1)
            topw, topi = jax.lax.top_k(probs, TOP_K)
            topw = topw / jnp.sum(topw, axis=-1, keepdims=True)
            combine = jnp.sum(jax.nn.one_hot(topi, NUM_EXPERTS, dtype=xf.dtype) * topw[..., None], axis=1)
            g = jax.nn.silu(jnp.einsum('td,xdh->txh', xf, wg))
            u = jnp.einsum('td,xdh->txh', xf, wu)
            eo = jnp.einsum('txh,xhd->txd', g * u, wd)
            out = jnp.einsum('txd,tx->td', eo, combine)
            return out.reshape(B, S, E)
        key = jax.random.key(seed)
        ks = jax.random.split(key, 12)
        s = 0.02
        return {'x': jax.random.normal(ks[0], (BATCH, SEQ, EMBED), jnp.float32), 'wq': jax.random.normal(ks[1], (EMBED, EMBED), jnp.float32) * s, 'wk': jax.random.normal(ks[2], (EMBED, EMBED), jnp.float32) * s, 'wv': jax.random.normal(ks[3], (EMBED, EMBED), jnp.float32) * s, 'wo': jax.random.normal(ks[4], (EMBED, EMBED), jnp.float32) * s, 'w_router': jax.random.normal(ks[5], (EMBED, NUM_EXPERTS), jnp.float32) * s, 'wg': jax.random.normal(ks[6], (NUM_EXPERTS, EMBED, HIDDEN), jnp.float32) * s, 'wu': jax.random.normal(ks[7], (NUM_EXPERTS, EMBED, HIDDEN), jnp.float32) * s, 'wd': jax.random.normal(ks[8], (NUM_EXPERTS, HIDDEN, EMBED), jnp.float32) * s, 'g1': jnp.ones((EMBED,), jnp.float32), 'g2': jnp.ones((EMBED,), jnp.float32)}
    _L0_ffn_all = _L0_ffn_setup()
    _L0_ffn_in = {k: v for k, v in _L0_ffn_all.items() if k in ('wq', 'wk', 'wv', 'wo', 'w_router', 'wg', 'wu', 'wd', 'g1', 'g2')}
    del _L0_ffn_all
    return {'x': x, 'ctx_768': ctx_768, 'L0_attn_key': _L0_attn_in['key'], 'L0_attn_value': _L0_attn_in['value'], 'L0_attn_in_proj_weight': _L0_attn_in['in_proj_weight'], 'L0_attn_out_proj_weight': _L0_attn_in['out_proj_weight'], 'L0_xattn_Wq': _L0_xattn_in['Wq'], 'L0_xattn_bq': _L0_xattn_in['bq'], 'L0_xattn_Wk': _L0_xattn_in['Wk'], 'L0_xattn_bk': _L0_xattn_in['bk'], 'L0_xattn_Wv': _L0_xattn_in['Wv'], 'L0_xattn_bv': _L0_xattn_in['bv'], 'L0_xattn_W1': _L0_xattn_in['W1'], 'L0_xattn_b1': _L0_xattn_in['b1'], 'L0_xattn_W2': _L0_xattn_in['W2'], 'L0_xattn_b2': _L0_xattn_in['b2'], 'L0_ffn_wq': _L0_ffn_in['wq'], 'L0_ffn_wk': _L0_ffn_in['wk'], 'L0_ffn_wv': _L0_ffn_in['wv'], 'L0_ffn_wo': _L0_ffn_in['wo'], 'L0_ffn_w_router': _L0_ffn_in['w_router'], 'L0_ffn_wg': _L0_ffn_in['wg'], 'L0_ffn_wu': _L0_ffn_in['wu'], 'L0_ffn_wd': _L0_ffn_in['wd'], 'L0_ffn_g1': _L0_ffn_in['g1'], 'L0_ffn_g2': _L0_ffn_in['g2']}

def reference(x, ctx_768, L0_attn_key, L0_attn_value, L0_attn_in_proj_weight, L0_attn_out_proj_weight, L0_xattn_Wq, L0_xattn_bq, L0_xattn_Wk, L0_xattn_bk, L0_xattn_Wv, L0_xattn_bv, L0_xattn_W1, L0_xattn_b1, L0_xattn_W2, L0_xattn_b2, L0_ffn_wq, L0_ffn_wk, L0_ffn_wv, L0_ffn_wo, L0_ffn_w_router, L0_ffn_wg, L0_ffn_wu, L0_ffn_wd, L0_ffn_g1, L0_ffn_g2):
    import jax
    import jax.numpy as jnp

    def _L0_attn_ref(query, key, value, in_proj_weight, out_proj_weight):
        import jax, jax.numpy as jnp
        import numpy as np
        import math
        B, T, E, H = (4, 256, 128, 16)
        D = E // H
        b, t, e = query.shape
        qkv = jnp.einsum('bte,fe->btf', query, in_proj_weight).reshape(b, t, 3, H, D)
        q = jnp.transpose(qkv[:, :, 0], (0, 2, 1, 3))
        k = jnp.transpose(qkv[:, :, 1], (0, 2, 1, 3))
        v = jnp.transpose(qkv[:, :, 2], (0, 2, 1, 3))
        q = q / math.sqrt(D)
        scores = jnp.einsum('bhqd,bhkd->bhqk', q, k)
        pos = jnp.arange(t)
        causal = pos[:, None] >= pos[None, :]
        scores = jnp.where(causal[None, None], scores, jnp.float32(-jnp.inf))
        attn = jax.nn.softmax(scores, axis=-1)
        out = jnp.einsum('bhqk,bhkd->bhqd', attn, v)
        out = jnp.transpose(out, (0, 2, 1, 3)).reshape(b, t, e)
        out = jnp.einsum('bte,fe->btf', out, out_proj_weight)
        return out

    def _L0_xattn_ref(x, y, Wq, bq, Wk, bk, Wv, bv, W1, b1, W2, b2):
        import jax, jax.numpy as jnp
        import numpy as np
        IMAGE_DIM = 128
        TEXT_DIM = 96
        NUM_HEADS = 16
        HEAD_DIM = IMAGE_DIM // NUM_HEADS
        B, N, _ = x.shape
        M = y.shape[1]
        q = (x @ Wq + bq).reshape(B, N, NUM_HEADS, HEAD_DIM)
        k = (y @ Wk + bk).reshape(B, M, NUM_HEADS, HEAD_DIM)
        v = (y @ Wv + bv).reshape(B, M, NUM_HEADS, HEAD_DIM)
        scale = 1.0 / np.sqrt(HEAD_DIM)
        scores = jnp.einsum('bnhd,bmhd->bhnm', q, k) * scale
        attn = jax.nn.softmax(scores, axis=-1)
        out = jnp.einsum('bhnm,bmhd->bnhd', attn, v).reshape(B, N, IMAGE_DIM)
        h = jax.nn.relu(out @ W1 + b1)
        return h @ W2 + b2

    def _L0_ffn_ref(x, wq, wk, wv, wo, w_router, wg, wu, wd, g1, g2):
        import jax, jax.numpy as jnp
        import numpy as np
        EMBED = 128
        HEADS = 16
        HEAD_DIM = EMBED // HEADS
        NUM_EXPERTS = 8
        TOP_K = 2
        HIDDEN = (int(2 * (4 * EMBED) / 3) + 63) // 64 * 64
        SEQ = 256
        BATCH = 2
        ROPE_BASE = 10000.0
        EPS = 1e-06

        def _rope_tables(seq_len, dim):
            inv_freq = 1.0 / ROPE_BASE ** (np.arange(0, dim, 2, dtype=np.float32) / dim)
            t = np.arange(seq_len, dtype=np.float32)
            freqs = np.einsum('i,j->ij', t, inv_freq)
            emb = np.concatenate([freqs, freqs], axis=-1)
            return (jnp.asarray(np.cos(emb)), jnp.asarray(np.sin(emb)))

        def _rotate_half(x):
            x1, x2 = jnp.split(x, 2, axis=-1)
            return jnp.concatenate([-x2, x1], axis=-1)

        def _rmsnorm(x, w):
            return x * jax.lax.rsqrt(jnp.mean(x * x, axis=-1, keepdims=True) + EPS) * w

        def _attention(x, wq, wk, wv, wo):
            B, S, _ = x.shape
            q = (x @ wq).reshape(B, S, HEADS, HEAD_DIM).transpose(0, 2, 1, 3)
            k = (x @ wk).reshape(B, S, HEADS, HEAD_DIM).transpose(0, 2, 1, 3)
            v = (x @ wv).reshape(B, S, HEADS, HEAD_DIM).transpose(0, 2, 1, 3)
            cos, sin = _rope_tables(S, HEAD_DIM)
            cos = cos[None, None]
            sin = sin[None, None]
            q = q * cos + _rotate_half(q) * sin
            k = k * cos + _rotate_half(k) * sin
            scale = HEAD_DIM ** (-0.5)
            scores = jnp.einsum('bhqd,bhkd->bhqk', q, k) * scale
            causal = jnp.triu(jnp.ones((S, S), bool), k=1)
            scores = jnp.where(causal, -jnp.inf, scores)
            attn = jax.nn.softmax(scores, axis=-1)
            out = jnp.einsum('bhqk,bhkd->bhqd', attn, v)
            out = out.transpose(0, 2, 1, 3).reshape(B, S, EMBED)
            return out @ wo

        def _moe(x, w_router, wg, wu, wd):
            B, S, E = x.shape
            xf = x.reshape(-1, E)
            logits = xf @ w_router
            probs = jax.nn.softmax(logits, axis=-1)
            topw, topi = jax.lax.top_k(probs, TOP_K)
            topw = topw / jnp.sum(topw, axis=-1, keepdims=True)
            combine = jnp.sum(jax.nn.one_hot(topi, NUM_EXPERTS, dtype=xf.dtype) * topw[..., None], axis=1)
            g = jax.nn.silu(jnp.einsum('td,xdh->txh', xf, wg))
            u = jnp.einsum('td,xdh->txh', xf, wu)
            eo = jnp.einsum('txh,xhd->txd', g * u, wd)
            out = jnp.einsum('txd,tx->td', eo, combine)
            return out.reshape(B, S, E)
        h = x + _attention(_rmsnorm(x, g1), wq, wk, wv, wo)
        y = h + _moe(_rmsnorm(h, g2), w_router, wg, wu, wd)
        return y
    x = x + _L0_attn_ref(_layernorm(x, axis=-1), L0_attn_key, L0_attn_value, L0_attn_in_proj_weight, L0_attn_out_proj_weight)
    x = x + _L0_xattn_ref(_layernorm(x, axis=-1), ctx_768, L0_xattn_Wq, L0_xattn_bq, L0_xattn_Wk, L0_xattn_bk, L0_xattn_Wv, L0_xattn_bv, L0_xattn_W1, L0_xattn_b1, L0_xattn_W2, L0_xattn_b2)
    x = x + _L0_ffn_ref(_layernorm(x, axis=-1), L0_ffn_wq, L0_ffn_wk, L0_ffn_wv, L0_ffn_wo, L0_ffn_w_router, L0_ffn_wg, L0_ffn_wu, L0_ffn_wd, L0_ffn_g1, L0_ffn_g2)
    return x

_drawn_inputs = setup_inputs


def setup_inputs(seed=0):
    import zlib

    import numpy as np

    out = dict(_drawn_inputs(seed))
    spreads = {'L0_ffn_g1': (1.0, 0.6), 'L0_ffn_g2': (1.0, 0.6)}
    factors = {'L0_xattn_bq': 3.936,
     'L0_xattn_bk': 8.0,
     'L0_ffn_wq': 8.0,
     'L0_ffn_wk': 8.0,
     'L0_ffn_wv': 4.884,
     'L0_ffn_wo': 4.858,
     'L0_ffn_w_router': 8.0,
     'L0_ffn_wg': 8.0,
     'L0_ffn_wu': 8.0,
     'L0_ffn_wd': 8.0}
    for name, (base, spread) in spreads.items():
        noise = np.random.default_rng([zlib.crc32(name.encode()), seed]).standard_normal(out[name].shape)
        drawn = base * np.exp(spread * noise) if base else spread * noise
        out[name] = jnp.asarray(drawn.astype(out[name].dtype))
    for name, factor in factors.items():
        out[name] = (out[name] * factor).astype(out[name].dtype)
    return out
```

```python
from contextlib import ExitStack

import numpy as np

import concourse.bass as bass
from concourse import mybir

F32 = mybir.dt.float32
BF16 = mybir.dt.bfloat16
I32 = mybir.dt.int32
U32 = mybir.dt.uint32
ALU = mybir.AluOpType
ACT = mybir.ActivationFunctionType
AX = mybir.AxisListType

P = 128
BATCH, SEQ, E, CE = 64, 64, 128, 96
HEADS, D = 16, 8
TOKENS = BATCH * SEQ
TILE, SUB = 512, 4
TILES = TOKENS // TILE
SUBS = TOKENS // P
EXPERTS, HIDDEN = 8, 384
HC = HIDDEN // P
FF = 256
BLOCKS = (2 * TOKENS + EXPERTS * (P - 1)) // P + 1
SCALE = float(D) ** -0.5
VW = HEADS * (D + 1)
PAD = 48

JOBS = 6
ITERS = TILES // 2

C_ID, C_ROT, C_LOW, C_COS, C_SIN, C_MASK, C_IOTA, C_BLK = 0, 128, 256, 384, 448, 512, 576, 584
C_ALL = C_BLK + BLOCKS
N_LOADS = 23
EXPORT = 3 * 16


def constants():
    c = np.zeros((P, C_ALL), np.float32)
    c[:, C_ID:C_ID + P] = np.eye(P)
    half = D // 2
    for o in range(P):
        d = o % D
        if d < half:
            c[o + half, C_ROT + o] = -1.0
        else:
            c[o - half, C_ROT + o] = 1.0
    c[:, C_LOW:C_LOW + P] = np.triu(np.ones((P, P)), 1)
    inv = 1.0 / 10000.0 ** (np.arange(0, D, 2, dtype=np.float32) / D)
    freqs = np.einsum("i,j->ij", np.arange(SEQ, dtype=np.float32), inv)
    emb = np.concatenate([freqs, freqs], axis=-1)
    c[:, C_COS:C_COS + SEQ] = np.tile(np.cos(emb).T, (HEADS, 1))
    c[:, C_SIN:C_SIN + SEQ] = np.tile(np.sin(emb).T, (HEADS, 1))
    q, k = np.arange(P)[:, None] % SEQ, np.arange(SEQ)[None, :]
    c[:, C_MASK:C_MASK + SEQ] = np.where(k > q, -1e30, 0.0)
    c[:, C_IOTA:C_IOTA + EXPERTS] = np.arange(EXPERTS)
    c[:, C_BLK:C_BLK + BLOCKS] = np.arange(BLOCKS)
    return c


SLOT_FIRST = (("xT", "k"), ("q",), ("v0", "v1"), ())
SLOT_A = (("oT", "wo", "cT"), ("k", "v0", "v1"), ("xT", "q"), ())
SLOT_B = (("oT", "h0", "h1", "ff"), (), ("xT", "k", "kr"), ("q", "qr", "v0", "v1"))
SLOT_C = (("oT", "wo"), ("xT", "k"), ("q", "v0", "v1"), ("hT", "lg"))
SLOTS = {1: SLOT_A, 2: SLOT_A, 3: SLOT_B, 4: SLOT_B, 5: SLOT_C, 6: SLOT_C}
PRE0 = ("xT", "k", "q", "v0", "v1")
POST = {0: ("oT", "wo"), 1: ("oT", "h0", "h1", "ff"), 2: ("oT", "wo", "hT", "lg")}
N_SLOT = {j: sum(len(c) for c in SLOTS[j]) for j in SLOTS}
N_ITER = sum(N_SLOT.values())
N_FIRST = len(PRE0) + sum(len(c) for c in SLOT_FIRST)
NORMS = {1: 1, 2: 1, 3: 1, 4: 1, 5: 2, 6: 2}
NORMS_ITER, NORMS_FIRST = sum(NORMS.values()), 2


def glue_before(i, j):
    if j == 0:
        return len(PRE0)
    return N_FIRST + i * N_ITER + sum(N_SLOT[x] for x in range(1, j))


def norms_before(i, j):
    return NORMS_FIRST + i * NORMS_ITER + sum(NORMS[x] for x in range(1, j))


def kind_of(j):
    return (j % JOBS) // 2


def wait(eng, sem, value):
    if not (isinstance(value, int) and value <= 0):
        eng.wait_ge(sem, value)


def build(nc, a, out):
    with ExitStack() as ctx:
        _build(nc, ctx, a, out)


def _build(nc, ctx, a, out):
    def sb(name, shape, dt=F32):
        return ctx.enter_context(nc.sbuf_tensor(name, shape, dt))

    def sem(name):
        return ctx.enter_context(nc.semaphore(name))

    const = sb("const", [P, C_ALL])
    ident = const[:, C_ID:C_ID + P]
    identb = sb("identb", [P, P], BF16)
    maskb = sb("maskb", [P, SEQ], BF16)
    raw = sb("raw", [P, 4, P])
    rawf = sb("rawf", [P, 2, P])
    rawT = sb("rawT", [P, 2, P])
    w_a = sb("w_a", [P, 4, P])
    w_x = sb("w_x", [P, 3, P])
    w1 = sb("w1", [P, FF])
    w2 = sb("w2", [P, 2, P])
    w_f = sb("w_f", [P, 6, P])
    w_r = sb("w_r", [P, EXPERTS])
    cols = sb("cols", [P, 8])
    b2 = sb("b2", [P, E])
    w_gu = sb("w_gu", [P, EXPERTS * 2 * HIDDEN])
    w_d = sb("w_d", [P, HC, EXPERTS * P])
    small = sb("small", [P, 12])
    xin = [sb(f"xin{r}", [P, SUB, E]) for r in range(2)]
    cin = [sb(f"cin{r}", [P, SUB, CE]) for r in range(2)]
    xres = [sb(f"xres{r}", [P, SUB, E]) for r in range(2)]
    fres = [sb(f"fres{r}", [P, SUB, E]) for r in range(2)]
    xh = sb("xh", [P, SUB, E])
    hn = sb("hn", [P, SUB, E])
    hres = sb("hres", [P, SUB, E])
    base = sb("base", [P, SUB, E])
    lgs = sb("lgs", [P, SUB, EXPERTS])
    stats = sb("stats", [P, SUB, 6])
    mv = sb("mv", [P, SUB, 2])
    rstd = sb("rstd", [P, SUB])
    rboth = sb("rboth", [P, SUB])
    pt = sb("pt", [P, 4, SUB])
    xT = sb("xT", [P, TILE])
    cT = sb("cT", [CE, TILE])
    oT = sb("oT", [P, TILE])
    h1T = sb("h1T", [P, 2, TILE])
    hT = sb("hT", [P, TILE])
    rope = sb("rope", [P, 2, TILE])
    qT = [sb(f"qT{r}", [P, TILE]) for r in range(2)]
    kS = [sb(f"kS{r}", [P, TILE]) for r in range(2)]
    kbd = [sb(f"kbd{r}", [P, HEADS, TILE]) for r in range(2)]
    vbd = [sb(f"vbd{r}", [P, (2 * SUB + 1) * VW]) for r in range(2)]
    probs = [sb(f"probs{r}", [P, HEADS, SEQ]) for r in range(2)]
    probsT = [sb(f"probsT{r}", [P, HEADS // 2, P]) for r in range(2)]
    rmax = [sb(f"rmax{r}", [P, HEADS]) for r in range(2)]
    rden = sb("rden", [P, HEADS])
    att = [sb(f"att{r}", [P, SUB, E]) for r in range(2)]
    lg_all = sb("lg_all", [P, SUBS, EXPERTS])
    ones = sb("ones", [P, P])
    zrow = sb("zrow", [P, E])
    turn = sb("turn", [P, 1])
    big = EXPERTS * SUBS
    route = kbd[1][:].rearrange("p h t -> p (h t)")
    spare = kbd[0][:].rearrange("p h t -> p (h t)")

    def grid(k):
        return route[:, k * big:(k + 1) * big].rearrange("p (s e) -> p s e", e=EXPERTS)

    oh0, oh1, sel3, less, keyed, second, scan0, scan1, rank = [grid(k) for k in range(9)]
    sel = route[:, 2 * big:3 * big]
    line = [route[:, 9 * big + k * SUBS:9 * big + (k + 1) * SUBS] for k in range(9)]
    top0, top1, idx0, idx1, gap, w1st, wsum, posf0, posf1 = line
    weight0, weight1 = sb("weight0", [P, SUBS]), sb("weight1", [P, SUBS])
    pos0, pos1 = sb("pos0", [P, SUBS], I32), sb("pos1", [P, SUBS], I32)
    counts_i = sb("counts_i", [P, EXPERTS], I32)
    blocks_i = sb("blocks_i", [P, EXPERTS], I32)
    blocks_f = sb("blocks_f", [P, 3, EXPERTS])
    first_row = sb("first_row", [P, EXPERTS])
    expert_of = sb("expert_of", [1, BLOCKS], I32)
    past = route[0:1, 12 * big:12 * big + BLOCKS * EXPERTS].rearrange("p (j e) -> p j e", e=EXPERTS)
    past_sum = route[0:1, 15 * big:15 * big + BLOCKS]

    def spare_pair(at, n):
        return [spare[:, at + r * n:at + (r + 1) * n] for r in range(2)]

    xb, xbT = spare_pair(0, P), spare_pair(2 * P, P)
    th, hh = spare_pair(512, HIDDEN), spare_pair(512 + 2 * HIDDEN, HIDDEN)
    hbT = spare_pair(512 + 4 * HIDDEN, HIDDEN)
    yb = spare_pair(512 + 6 * HIDDEN, P)
    RING = 4
    gy = [[spare[:, 4096 + (2 * r + k) * E:4096 + (2 * r + k + 1) * E] for k in range(2)] for r in range(RING)]
    hn_all = route[:, 16 * big:].rearrange("p (s e) -> p s e", e=E)
    hn_dram = nc.dram_tensor("hn_dram", [P, SUBS, E], F32).ap()
    base_dram = nc.dram_tensor("base_dram", [P, SUBS, E], F32).ap()
    xs_dram = nc.dram_tensor("xs_dram", [BLOCKS * P, E], F32).ap()
    ys_dram = nc.dram_tensor("ys_dram", [BLOCKS * P, E], F32).ap()

    ps_s = [ctx.enter_context(nc.psum_tensor(f"ps_s{r}", [P, HEADS, SEQ], F32)) for r in range(2)]
    ps_t = [ctx.enter_context(nc.psum_tensor(f"ps_t{r}", [P, 4, P], F32)) for r in range(2)]
    ps_o = ctx.enter_context(nc.psum_tensor("ps_o", [P, 512], F32))
    ps_g = ctx.enter_context(nc.psum_tensor("ps_g", [P, 512], F32))

    weights_loaded = sem("weights_loaded")
    gate_up_loaded = sem("gate_up_loaded")
    pool_clear = sem("pool_clear")
    pool_const = sem("pool_const")
    const_ready = sem("const_ready")
    setup_filled = sem("setup_filled")
    setup_drained = sem("setup_drained")
    x_loaded = [sem(f"x_loaded{r}") for r in range(2)]
    ctx_loaded = [sem(f"ctx_loaded{r}") for r in range(2)]
    kbd_loaded = [sem(f"kbd_loaded{r}") for r in range(2)]
    scores_ready = sem("scores_ready")
    rmax_ready = sem("rmax_ready")
    centered = sem("centered")
    probs_ready = sem("probs_ready")
    probsT_filled = sem("probsT_filled")
    probsT_copied = sem("probsT_copied")
    out_ready = sem("out_ready")
    rden_ready = sem("rden_ready")
    heads_ready = sem("heads_ready")
    glue_filled = sem("glue_filled")
    glue_drained = sem("glue_drained")
    stats_ready = sem("stats_ready")
    mv_ready = sem("mv_ready")
    pool_step = sem("pool_step")
    normed = sem("normed")
    b2_added = sem("b2_added")
    roped = sem("roped")
    exported = sem("exported")
    export_ready = sem("export_ready")
    dve_chain = sem("dve_chain")
    sel_ready = sem("sel_ready")
    ranks_ready = sem("ranks_ready")
    gap_ready = sem("gap_ready")
    weight_ready = sem("weight_ready")
    xs_cleared = sem("xs_cleared")
    pos_ready = sem("pos_ready")
    scattered = sem("scattered")
    hn_loaded = sem("hn_loaded")
    gate_up_ready = sem("gate_up_ready")
    xb_loaded = [sem(f"xb_loaded{r}") for r in range(2)]
    ys_stored = [sem(f"ys_stored{r}") for r in range(2)]
    xbT_filled, xbT_copied = sem("xbT_filled"), sem("xbT_copied")
    gu_filled, tanh_ready, gated, h_ready = sem("gu_filled"), sem("tanh_ready"), sem("gated"), sem("h_ready")
    hbT_filled, hbT_copied = sem("hbT_filled"), sem("hbT_copied")
    y_filled, y_copied = sem("y_filled"), sem("y_copied")
    base_loaded = sem("base_loaded")
    fetched = [sem(f"fetched{r}") for r in range(RING)]
    first_added = sem("first_added")
    summed = sem("summed")
    stored = sem("stored")

    steps = {1: 2, 2: 2, 3: 7, 4: 7, 5: 6, 6: 6}

    def steps_before(i, j):
        return 4 + i * sum(steps.values()) + sum(steps[x] for x in range(1, j))

    def pair_no(i, j, p):
        return i * (JOBS * SUB) + j * SUB + p

    def tile_no(i, j):
        return 2 * i + 2 * (j // JOBS) + j % 2

    def tile_turn(i, j):
        return i + j // JOBS

    def job_turn(i, j):
        return 3 * i + j // 2

    def norm_index(i, j, which):
        if which == "pre":
            return j + 1 if isinstance(i, int) and i == 0 and j <= 1 else norms_before(i, j - 1) + 1
        if isinstance(i, int) and i == ITERS - 1:
            return norms_before(i, JOBS - 1) + (1 if j == JOBS - 2 else 2)
        return norms_before(i, j + 1) + 2

    def key_uses(i, j):
        if isinstance(i, int) and i == 0 and j <= 1:
            return glue_before(0, 0) * j + 2
        flat = sum(SLOTS[j - 1], ())
        return glue_before(i, j - 1) + flat.index("kr" if kind_of(j) == 2 else "k") + 1

    def is_last(i, j):
        return isinstance(i, int) and i == ITERS - 1 and j == JOBS - 1

    def walk(eng, slot):
        slot(0, 0)
        with eng.Fori(0, ITERS - 1) as i:
            for j in range(1, JOBS + 1):
                slot(i, j)
        for j in range(1, JOBS):
            slot(ITERS - 1, j)

    def glue_uses(i, j, p):
        chunks = SLOT_FIRST if j == 0 else SLOTS[j]
        post = () if j == 0 else POST[kind_of(j - 1)]
        if is_last(i, j):
            chunks = [[name for name in c if name in post] for c in chunks]
        n = glue_before(i, j) + sum(len(c) for c in chunks[:p])
        for k, name in enumerate(chunks[p]):
            yield n + k, name, j - 1 if name in post else j + 1

    def tail_uses():
        n = glue_before(ITERS - 1, JOBS - 1) + len(POST[2])
        for k, name in enumerate(POST[2]):
            yield n + k, name, JOBS - 1

    def route_dve(dve):
        V = nc.vector
        n = [0]

        def step(ins):
            n[0] += 1
            ins.then_inc(dve_chain, 1)
            dve.wait_ge(dve_chain, n[0])

        iota = const[:, C_IOTA:C_IOTA + EXPERTS].unsqueeze(1).broadcast_to([P, SUBS, EXPERTS])

        def wide(x):
            return x.unsqueeze(2).broadcast_to([P, SUBS, EXPERTS])

        dve.wait_ge(exported, EXPORT * (TILES + 1))
        for src, top, idx, oh in ((lg_all[:], top0, idx0, oh0), (second, top1, idx1, oh1)):
            step(V.reduce_max(top, src, AX.X))
            step(V.tensor_tensor(less, src, wide(top), ALU.is_lt))
            step(V.scalar_tensor_tensor(keyed, less, float(EXPERTS), iota, ALU.mult, ALU.add))
            step(V.tensor_reduce(idx, keyed, AX.X, ALU.min))
            step(V.tensor_tensor(oh, iota, wide(idx), ALU.is_equal))
            if src is not second:
                step(V.scalar_tensor_tensor(second, oh, -1e30, src, ALU.mult, ALU.add))
        V.tensor_tensor(sel3, oh0, oh1, ALU.add).then_inc(sel_ready, 1)
        V.tensor_tensor(gap, top1, top0, ALU.subtract).then_inc(gap_ready, 1)
        dve.wait_ge(ranks_ready, 1)
        within = ps_g[:, 0:big].rearrange("p (s e) -> p s e", e=EXPERTS)
        total = ps_g[:, big:2 * big].rearrange("p (s e) -> p s e", e=EXPERTS)
        step(V.tensor_copy(scan0, total))
        src, dst = scan0, scan1
        for k in (1, 2, 4, 8, 16):
            V.tensor_copy(dst[:, 0:k, :], src[:, 0:k, :])
            step(V.tensor_tensor(dst[:, k:, :], src[:, k:, :], src[:, 0:SUBS - k, :], ALU.add))
            src, dst = dst, src
        step(V.tensor_scalar(counts_i[:], src[:, SUBS - 1, :], float(P - 1), None, ALU.add))
        step(V.tensor_scalar(blocks_i[:], counts_i[:], 7, None, ALU.logical_shift_right))
        step(V.tensor_copy(blocks_f[:, 0, :], blocks_i[:]))
        a0, b0 = 0, 1
        for k in (1, 2, 4):
            V.tensor_copy(blocks_f[:, b0, 0:k], blocks_f[:, a0, 0:k])
            step(V.tensor_tensor(blocks_f[:, b0, k:], blocks_f[:, a0, k:], blocks_f[:, a0, 0:EXPERTS - k], ALU.add))
            a0, b0 = b0, (2 if k == 1 else a0)
        ends = blocks_f[:, a0, :]
        step(V.tensor_copy(blocks_f[:, b0, :], blocks_i[:]))
        step(V.tensor_tensor(first_row[:], ends, blocks_f[:, b0, :], ALU.subtract))
        step(V.tensor_scalar(first_row[:], first_row[:], float(P), None, ALU.mult))
        step(V.tensor_tensor(rank, src, total, ALU.subtract))
        step(V.tensor_tensor(rank, rank, within, ALU.add))
        step(V.tensor_tensor(rank, rank, first_row[:].unsqueeze(1).broadcast_to([P, SUBS, EXPERTS]), ALU.add))
        for oh, posf, pos in ((oh0, posf0, pos0), (oh1, posf1, pos1)):
            step(V.tensor_tensor(keyed, oh, rank, ALU.mult))
            step(V.reduce_sum(posf, keyed, AX.X))
            V.tensor_copy(pos[:], posf).then_inc(pos_ready, 1)
        step(V.tensor_tensor(past, const[0:1, C_BLK:C_BLK + BLOCKS].unsqueeze(2).broadcast_to([1, BLOCKS, EXPERTS]),
                             ends[0:1, :].unsqueeze(1).broadcast_to([1, BLOCKS, EXPERTS]), ALU.is_ge))
        step(V.reduce_sum(past_sum, past, AX.X))
        V.tensor_scalar(expert_of[:], past_sum, float(EXPERTS - 1), None, ALU.min).then_inc(pos_ready, 1)
        dve.wait_ge(weight_ready, 1)
        step(V.tensor_scalar(wsum, w1st, 1.0, None, ALU.add))
        step(V.reciprocal(weight0[:], wsum))
        step(V.tensor_tensor(weight1[:], w1st, weight0[:], ALU.mult))

    def dispatch_pool(pool):
        pool.wait_ge(xs_cleared, 16)
        pool.wait_ge(pos_ready, 2)
        pool.wait_ge(hn_loaded, 16)
        for s in range(SUBS):
            for pos in (pos0, pos1):
                nc.gpsimd.indirect_dma_start(
                    out=xs_dram, out_offset=bass.IndirectOffsetOnAxis(ap=pos[:, s:s + 1], axis=0),
                    in_=hn_all[:, s, :], in_offset=None).then_inc(scattered, 16)

    def blocks(eng, step):
        for j in range(3):
            step(j, j % 2)
        with eng.Fori(0, (BLOCKS - 6) // 2) as i:
            step(i * 2 + 3, 1)
            step(i * 2 + 4, 0)
        for j in range(BLOCKS - 3, BLOCKS):
            step(j, j % 2)

    def there(j):
        return not isinstance(j, int) or 0 <= j < BLOCKS

    g_bank = [ps_s[0][:].rearrange("p h k -> p (h k)")[:, 512 * r:512 * r + HIDDEN] for r in range(2)]
    u_bank = [ps_s[1][:].rearrange("p h k -> p (h k)")[:, 512 * r:512 * r + HIDDEN] for r in range(2)]
    h_bank = [ps_t[r][:].rearrange("p a b -> p (a b)")[:, 0:HIDDEN] for r in range(2)]
    x_bank, y_bank = ps_o[:, 0:P], ps_g[:, 0:E]

    def experts_sp(sp):
        sp.wait_ge(scattered, 16 * 2 * SUBS)
        xs_b = xs_dram.rearrange("(b p) e -> b p e", p=P)
        ys_b = ys_dram.rearrange("(b p) e -> b p e", p=P)

        def one(ap, j):
            return ap[j] if isinstance(j, int) else ap[bass.ds(j, 1)].rearrange("o p e -> (o p) e")

        def load(j, r):
            sp.dma_start(xb[r], one(xs_b, j)).then_inc(xb_loaded[r], 16)

        load(0, 0)
        load(1, 1)

        def step(j, r):
            if there(j + 2):
                sp.wait_ge(xbT_filled, j + 1)
                load(j + 2, r)
            if there(j - 1):
                sp.wait_ge(y_copied, j)
                sp.dma_start(one(ys_b, j - 1), yb[1 - r]).then_inc(ys_stored[1 - r], 16)

        blocks(sp, step)
        sp.wait_ge(y_copied, BLOCKS)
        sp.dma_start(one(ys_b, BLOCKS - 1), yb[(BLOCKS - 1) % 2]).then_inc(ys_stored[(BLOCKS - 1) % 2], 16)
        sp.dma_start(hn_all, base_dram).then_inc(base_loaded, 16)
        for t in range(TILES):
            sp.wait_ge(summed, (t + 1) * SUB)
            sp.dma_start(out_t[t], hn_all[:, t * SUB:(t + 1) * SUB, :]).then_inc(stored, 16)
        sp.wait_ge(stored, 16 * TILES)

    def experts_pe(pe):
        mm = nc.tensor.matmul
        pe.wait_ge(pos_ready, 3)
        pe.wait_ge(gate_up_ready, 1)
        pe.wait_ge(gate_up_loaded, 16 * (2 + HC))

        def expert(j):
            at = expert_of[0:1, j:j + 1] if isinstance(j, int) else expert_of[0:1, bass.ds(j, 1)]
            return pe.value_load(at, min_val=0, max_val=EXPERTS - 1)

        def rows_T(j, r, half):
            pe.wait_ge(xb_loaded[r], half * 16 + 16)
            wait(pe, xbT_copied, j)
            nc.tensor.transpose(x_bank, xb[r], ident).then_inc(xbT_filled, 1)

        def gate_up(j, r):
            pe.wait_ge(xbT_copied, j + 1)
            wait(pe, h_ready, j - 1)
            e = expert(j)
            for k, bank in ((0, g_bank), (1, u_bank)):
                w = w_gu[:, bass.ds(e * (2 * HIDDEN) + k * HIDDEN, HIDDEN)]
                last = mm(bank[r], xbT[r], w, start=True, stop=True)
            last.then_inc(gu_filled, 1)

        def hidden_T(j, r):
            pe.wait_ge(h_ready, j + 1)
            wait(pe, hbT_copied, j - 1)
            for c in range(HC):
                last = nc.tensor.transpose(h_bank[r][:, c * P:(c + 1) * P], hh[r][:, c * P:(c + 1) * P], ident)
            last.then_inc(hbT_filled, 1)

        def down(j, r):
            pe.wait_ge(hbT_copied, j + 1)
            wait(pe, y_copied, j)
            e = expert(j)
            for c in range(HC):
                last = mm(y_bank, hbT[r][:, c * P:(c + 1) * P], w_d[:, c, bass.ds(e * P, P)],
                          start=(c == 0), stop=(c == HC - 1))
            last.then_inc(y_filled, 1)

        rows_T(0, 0, 0)
        rows_T(1, 1, 0)
        gate_up(0, 0)

        def step(j, r):
            if there(j + 1):
                gate_up(j + 1, 1 - r)
            if there(j - 1):
                down(j - 1, 1 - r)
            if there(j + 2):
                rows_T(j + 2, r, (j + 2 - r) // 2 if isinstance(j, int) else half_of(j, r) + 1)
            hidden_T(j, r)

        blocks(pe, step)
        down(BLOCKS - 1, (BLOCKS - 1) % 2)

    def half_of(j, r):
        return (j - r) // 2

    def experts_act(act):
        def rows_out(j, r):
            act.wait_ge(xbT_filled, j + 1)
            wait(act, gu_filled, j - 1)
            nc.scalar.activation(xbT[r], x_bank, ACT.Copy).then_inc(xbT_copied, 1)

        rows_out(0, 0)
        rows_out(1, 1)

        def step(j, r):
            act.wait_ge(gu_filled, j + 1)
            wait(act, h_ready, j - 1)
            nc.scalar.activation(th[r], g_bank[r], ACT.Tanh, scale=0.5).then_inc(tanh_ready, 1)
            if there(j + 2):
                rows_out(j + 2, r)
            act.wait_ge(hbT_filled, j + 1)
            wait(act, y_filled, j - 1)
            nc.scalar.activation(hbT[r], h_bank[r], ACT.Copy, scale=0.5).then_inc(hbT_copied, 1)

        blocks(act, step)

    def experts_dve(dve):
        V = nc.vector

        def copy_y(j, r, half):
            dve.wait_ge(y_filled, j + 1)
            wait(dve, ys_stored[r], half * 16)
            V.tensor_scalar(yb[r], y_bank, 1.0, None, ALU.mult).then_inc(y_copied, 1)

        def step(j, r):
            dve.wait_ge(tanh_ready, j + 1)
            V.scalar_tensor_tensor(th[r], th[r], 1.0, g_bank[r], ALU.add, ALU.mult).then_inc(gated, 1)
            wait(dve, hbT_filled, j - 1)
            dve.wait_ge(gated, j + 1)
            V.tensor_tensor(hh[r], th[r], u_bank[r], ALU.mult).then_inc(h_ready, 1)
            if there(j - 1):
                copy_y(j - 1, 1 - r, half_of(j - 1, 1 - r))

        blocks(dve, step)
        copy_y(BLOCKS - 1, (BLOCKS - 1) % 2, (BLOCKS - 1) // 2)

    def gather_pool(pool):
        pool.wait_ge(ys_stored[0], 16 * (BLOCKS // 2))
        pool.wait_ge(ys_stored[1], 16 * (BLOCKS // 2))
        for s in range(SUBS):
            if s >= RING:
                pool.wait_ge(summed, s - RING + 1)
            for k, pos in enumerate((pos0, pos1)):
                nc.gpsimd.indirect_dma_start(
                    out=gy[s % RING][k], out_offset=None, in_=ys_dram,
                    in_offset=bass.IndirectOffsetOnAxis(ap=pos[:, s:s + 1], axis=0)).then_inc(fetched[s % RING], 16)

    def combine_dve(dve):
        V = nc.vector
        dve.wait_ge(base_loaded, 16)
        for s in range(SUBS):
            y0, y1 = gy[s % RING]
            dve.wait_ge(fetched[s % RING], 32 * (s // RING + 1))
            V.scalar_tensor_tensor(y0, y0, weight0[:, s:s + 1], hn_all[:, s, :], ALU.mult, ALU.add)\
             .then_inc(first_added, 1)
            dve.wait_ge(first_added, s + 1)
            V.scalar_tensor_tensor(hn_all[:, s, :], y1, weight1[:, s:s + 1], y0, ALU.mult, ALU.add)\
             .then_inc(summed, 1)

    block = ctx.enter_context(nc.Block())

    x_t = a["x"].rearrange("b q e -> (b q) e").rearrange("(t s p) e -> t p s e", s=SUB, p=P)
    c_t = a["ctx_768"].rearrange("b q e -> (b q) e").rearrange("(t s p) e -> t p s e", s=SUB, p=P)
    out_t = out.rearrange("b q e -> (b q) e").rearrange("(t s p) e -> t p s e", s=SUB, p=P)

    def dyn(ap, t):
        if isinstance(t, int):
            return ap[t]
        return ap[bass.ds(t, 1)].rearrange("o p s e -> (o p) s e")

    def column(name, lo=0):
        return a[name][lo:lo + P].rearrange("(p o) -> p o", o=1)

    @block.sync
    def _(sp):
        def load_tile(t, r):
            sp.dma_start(xin[r][:], dyn(x_t, t)).then_inc(x_loaded[r], 16)
            sp.dma_start(cin[r][:], dyn(c_t, t)).then_inc(ctx_loaded[r], 16)

        loads = [(const[:], a["const"])]
        loads += [(raw[:, k, :], a["L0_attn_in_proj_weight"][k * P:(k + 1) * P, :]) for k in range(3)]
        loads += [(raw[:, 3, :], a["L0_attn_out_proj_weight"])]
        loads += [(rawf[:, 0, :], a["L0_ffn_wq"]), (rawf[:, 1, :], a["L0_ffn_wk"]),
                  (w_f[:, 2, :], a["L0_ffn_wv"]), (w_f[:, 5, :], a["L0_ffn_wo"])]
        loads += [(cols[:, 5:6], column("L0_ffn_g1")), (cols[:, 6:7], column("L0_ffn_g2"))]
        loads += [(w_x[:, 0, :], a["L0_xattn_Wq"]), (w_x[0:CE, 1, :], a["L0_xattn_Wk"]),
                  (w_x[0:CE, 2, :], a["L0_xattn_Wv"]), (w1[:], a["L0_xattn_W1"]),
                  (w2[:], a["L0_xattn_W2"].rearrange("(k p) e -> p k e", p=P))]
        loads += [(cols[:, 0:1], column("L0_xattn_bq")), (cols[:, 1:2], column("L0_xattn_bk")),
                  (cols[:, 2:3], column("L0_xattn_bv")), (cols[:, 3:4], column("L0_xattn_b1")),
                  (cols[:, 4:5], column("L0_xattn_b1", P)),
                  (b2[:], a["L0_xattn_b2"].rearrange("(o e) -> o e", o=1).broadcast_to([P, E])),
                  (w_r[:], a["L0_ffn_w_router"])]
        assert len(loads) == N_LOADS
        for dst, src in loads:
            sp.dma_start(dst, src).then_inc(weights_loaded, 16)
        load_tile(0, 0)
        load_tile(1, 1)
        gu = w_gu[:].rearrange("p (e k h) -> p e k h", e=EXPERTS, k=2)
        sp.dma_start(gu[:, :, 0, :], a["L0_ffn_wg"].rearrange("x p h -> p x h")).then_inc(gate_up_loaded, 16)
        sp.dma_start(gu[:, :, 1, :], a["L0_ffn_wu"].rearrange("x p h -> p x h")).then_inc(gate_up_loaded, 16)
        wd_v = w_d[:].rearrange("p c (x e) -> p c x e", x=EXPERTS)
        for c in range(HC):
            sp.dma_start(wd_v[:, c], a["L0_ffn_wd"][:, c * P:(c + 1) * P, :].rearrange("x p e -> p x e"))\
              .then_inc(gate_up_loaded, 16)

        def spread_keys(i, j):
            r = j % 2
            sp.wait_ge(glue_drained, key_uses(i, j))
            for h in range(HEADS):
                sp.dma_start(kbd[r][D * h:D * h + D, h, :], kS[r][D * h:D * h + D, :]).then_inc(kbd_loaded[r], 16)

        def export(i, j):
            t = tile_no(i, j)
            wait(sp, export_ready, t + 1)
            sl = slice(t * SUB, t * SUB + SUB) if isinstance(t, int) else bass.ds(t * SUB, SUB)
            sp.dma_start(hn_dram[:, sl, :], hn[:]).then_inc(exported, 16)
            sp.dma_start(base_dram[:, sl, :], base[:]).then_inc(exported, 16)
            sp.dma_start(lg_all[:, sl, :], lgs[:]).then_inc(exported, 16)

        sp.wait_ge(pool_const, 1)
        sp.sem_inc(exported, EXPORT)
        sp.dma_start(xs_dram.rearrange("(b p) e -> p b e", p=P),
                     zrow[:].unsqueeze(1).broadcast_to([P, BLOCKS, E])).then_inc(xs_cleared, 16)
        spread_keys(0, 0)

        def slot(i, j):
            if j in (3, 4) and not (isinstance(i, int) and i == ITERS - 1):
                wait(sp, glue_drained, glue_before(i, j))
                load_tile(2 * i + 2 + (j - 3), j - 3)
            if not is_last(i, j):
                spread_keys(i, j + 1)
            if j in (5, 6):
                export(i, j - 1)

        walk(sp, slot)
        export(ITERS - 1, JOBS - 1)
        sp.wait_ge(exported, EXPORT * (TILES + 1))
        sp.wait_ge(scores_ready, TILES * 3 * SUB)
        sp.dma_start(hn_all, hn_dram).then_inc(hn_loaded, 16)
        experts_sp(sp)

    @block.tensor
    def _(pe):
        mm = nc.tensor.matmul

        def setup():
            pe.wait_ge(weights_loaded, 16 * N_LOADS)
            for k in range(4):
                last = nc.tensor.transpose(ps_g[:, k * P:(k + 1) * P], raw[:, k, :], ident)
            last.then_inc(setup_filled, 1)
            pe.wait_ge(const_ready, 1)
            pe.wait_ge(setup_drained, 1)
            for k in range(2):
                last = nc.tensor.transpose(ps_g[:, k * P:(k + 1) * P], w_f[:, k, :], ident)
            last.then_inc(setup_filled, 1)
            pe.wait_ge(setup_drained, 2)
            for k in range(2):
                last = mm(ps_g[:, k * P:(k + 1) * P], rawT[:, k, :], const[:, C_ROT:C_ROT + P],
                          start=True, stop=True)
            last.then_inc(setup_filled, 1)
            pe.wait_ge(setup_drained, 3)

        def transposes(src, rows=P):
            for s in range(SUB):
                last = nc.tensor.transpose(ps_g[0:rows, s * P:(s + 1) * P], src[:, s, :], ident)
            return last

        def values(src, w, half):
            for b in range(SUB):
                col = (half * SUB + b) * SEQ
                for q in range(2):
                    last = mm(ps_g[SEQ * q:SEQ * q + SEQ, b * P:(b + 1) * P], src[:, col:col + SEQ], w,
                              start=True, stop=True)
            return last

        def use(n, name, i, j):
            kind = kind_of(j)
            r = j % 2
            if name == "xT":
                pe.wait_ge(normed, norm_index(i, j, "pre"))
            if name == "hT":
                pe.wait_ge(normed, norm_index(i, j, "post"))
            if name == "oT":
                pe.wait_ge(heads_ready, pair_no(i, j, SUB - 1) + 1)
            if name == "cT":
                pe.wait_ge(ctx_loaded[r], 16 * (tile_turn(i, j) + 1))
            wait(pe, glue_drained, n)
            if name == "xT":
                last = transposes(xh)
            elif name == "cT":
                last = transposes(cin[r], CE)
            elif name == "oT":
                last = transposes(att[r])
            elif name == "hT":
                last = transposes(hn)
            elif name == "wo":
                w = w_a[:, 3, :] if kind == 0 else w_f[:, 5, :]
                for s in range(SUB):
                    last = mm(ps_g[:, s * P:(s + 1) * P], oT[:, s * P:(s + 1) * P], w, start=True, stop=True)
            elif name in ("h0", "h1"):
                k = int(name[1])
                last = mm(ps_g[:], w1[:, k * P:(k + 1) * P], oT[:], start=True, stop=True)
            elif name == "ff":
                for s in range(SUB):
                    for k in range(2):
                        last = mm(ps_g[:, s * P:(s + 1) * P], h1T[:, k, s * P:(s + 1) * P], w2[:, k, :],
                                  start=(k == 0), stop=(k == 1))
            elif name == "lg":
                for s in range(SUB):
                    last = mm(ps_g[:, s * EXPERTS:(s + 1) * EXPERTS], hT[:, s * P:(s + 1) * P], w_r[:],
                              start=True, stop=True)
            elif name in ("v0", "v1"):
                src, w = {0: (xT, w_a[:, 2, :]), 1: (cT, w_x[0:CE, 2, :]), 2: (xT, w_f[:, 2, :])}[kind]
                last = values(src, w, int(name[1]))
            else:
                w = {(0, "q"): w_a[:, 0, :], (0, "k"): w_a[:, 1, :], (1, "q"): w_x[:, 0, :],
                     (1, "k"): w_x[0:CE, 1, :], (2, "q"): w_f[:, 0, :], (2, "k"): w_f[:, 1, :],
                     (2, "qr"): w_f[:, 3, :], (2, "kr"): w_f[:, 4, :]}[kind, name]
                last = mm(ps_g[:], w, (cT if kind == 1 and name == "k" else xT)[:], start=True, stop=True)
            last.then_inc(glue_filled, 1)

        def scores(i, j, p):
            n = pair_no(i, j, p)
            r, half = j % 2, p % 2
            if p == 0:
                pe.wait_ge(kbd_loaded[r], 16 * HEADS * (job_turn(i, j) + 1))
                pe.wait_ge(glue_drained, glue_before(i, j))
            wait(pe, centered, n - 1)
            causal = kind_of(j) != 1
            for g in range(2):
                for b in range(2):
                    rows = slice(SEQ * b, SEQ * b + SEQ)
                    o = ps_s[half][rows, 8 * g:8 * g + 8, :]
                    if causal:
                        mm(o, identb[:, rows], maskb[:].unsqueeze(1).broadcast_to([P, 8, SEQ]),
                           start=True, stop=False)
                for b in range(2):
                    rows = slice(SEQ * b, SEQ * b + SEQ)
                    o = ps_s[half][rows, 8 * g:8 * g + 8, :]
                    tok = (2 * p + b) * SEQ
                    last = mm(o, qT[r][:, tok:tok + SEQ], kbd[r][:, 8 * g:8 * g + 8, tok:tok + SEQ],
                              start=not causal, stop=True)
            last.then_inc(scores_ready, 1)

        def transpose_probs(i, j, p):
            n = pair_no(i, j, p)
            pe.wait_ge(probs_ready, n + 1)
            flat = probs[p % 2][:].rearrange("p h k -> p (h k)")
            for g in range(2):
                wait(pe, probsT_copied, 2 * n + g - 1)
                for k in range(4):
                    c = (4 * g + k) * P
                    last = nc.tensor.transpose(ps_t[g][:, k, :], flat[:, c:c + P], ident)
                last.then_inc(probsT_filled, 1)

        def attend(i, j, p):
            n = pair_no(i, j, p)
            r = j % 2
            wait(pe, heads_ready, n)
            pe.wait_ge(probsT_copied, 2 * n + 2)
            if p == 0:
                pe.wait_ge(glue_drained, glue_before(i, j))
            o = ps_o[:, 0:2 * (VW + PAD)].rearrange("p (b c) -> p b c", b=2)
            for k in range(HEADS // 2):
                c = 2 * (D + 1) * k
                v = vbd[r][:, 2 * p * VW + c:2 * p * VW + c + 2 * VW].rearrange("p (b c) -> p b c", b=2)
                last = mm(o[:, :, c:c + PAD], probsT[p % 2][:, k, :], v[:, :, 0:PAD], start=True, stop=True)
            last.then_inc(out_ready, 1)

        setup()
        for k, name in enumerate(PRE0):
            use(k, name, 0, 0)
        scores(0, 0, 0)

        def slot(i, j):
            for p in range(SUB):
                if p < SUB - 1:
                    scores(i, j, p + 1)
                transpose_probs(i, j, p)
                for n, name, jj in glue_uses(i, j, p):
                    use(n, name, i, jj)
                attend(i, j, p)
            if not is_last(i, j):
                scores(i, j + 1, 0)

        walk(pe, slot)
        for n, name, j in tail_uses():
            use(n, name, ITERS - 1, j)

        pe.wait_ge(sel_ready, 1)
        pe.wait_ge(glue_drained, glue_before(ITERS - 1, JOBS - 1) + 2 * len(POST[2]))
        mm(ps_g[:, 0:SUBS * EXPERTS], const[:, C_LOW:C_LOW + P], sel[:], start=True, stop=True)
        mm(ps_g[:, 256:512], ones[:], sel[:], start=True, stop=True).then_inc(ranks_ready, 1)

        experts_pe(pe)

    @block.scalar
    def _(act):
        def exps(i, j, p):
            n = pair_no(i, j, p)
            act.wait_ge(centered, n + 1)
            nc.scalar.activation(probs[p % 2][:], probs[p % 2][:], ACT.Exp, scale=SCALE).then_inc(probs_ready, 1)

        def copy_probsT(i, j, p):
            n = pair_no(i, j, p)
            wait(act, out_ready, n - 1)
            for g in range(2):
                act.wait_ge(probsT_filled, 2 * n + g + 1)
                nc.scalar.activation(probsT[p % 2][:, 4 * g:4 * g + 4, :], ps_t[g][:], ACT.Copy)\
                  .then_inc(probsT_copied, 1)

        def use(n, name, i, j):
            kind, r = kind_of(j), j % 2
            if name in ("wo", "ff", "lg", "v0", "v1", "qr", "kr") or (kind == 2 and name in ("q", "k")):
                return
            if name == "k":
                wait(act, kbd_loaded[r], 16 * HEADS * job_turn(i, j))
            act.wait_ge(glue_filled, n + 1)
            if name == "xT":
                ins = nc.scalar.activation(xT[:], ps_g[:], ACT.Copy)
            elif name == "cT":
                ins = nc.scalar.activation(cT[:], ps_g[0:CE, :], ACT.Copy)
            elif name == "oT" and kind == 1:
                ins = nc.scalar.activation(oT[:], ps_g[:], ACT.Identity, bias=cols[:, 2:3])
            elif name == "oT":
                ins = nc.scalar.activation(oT[:], ps_g[:], ACT.Copy)
            elif name == "hT":
                ins = nc.scalar.activation(hT[:], ps_g[:], ACT.Copy)
            elif name in ("h0", "h1"):
                k = int(name[1])
                ins = nc.scalar.activation(h1T[:, k, :], ps_g[:], ACT.Relu, bias=cols[:, 3 + k:4 + k])
            elif name == "q":
                ins = (nc.scalar.activation(qT[r][:], ps_g[:], ACT.Identity, bias=cols[:, 0:1]) if kind == 1
                       else nc.scalar.activation(qT[r][:], ps_g[:], ACT.Copy))
            elif name == "k":
                ins = (nc.scalar.activation(kS[r][:], ps_g[:], ACT.Identity, bias=cols[:, 1:2]) if kind == 1
                       else nc.scalar.activation(kS[r][:], ps_g[:], ACT.Copy))
            ins.then_inc(glue_drained, 1)

        act.wait_ge(weights_loaded, 16 * N_LOADS)
        act.wait_ge(setup_filled, 1)
        nc.scalar.activation(w_a[:].rearrange("p a b -> p (a b)"), ps_g[:], ACT.Copy).then_inc(setup_drained, 1)
        act.wait_ge(setup_filled, 2)
        nc.scalar.activation(rawT[:].rearrange("p a b -> p (a b)"), ps_g[:, 0:2 * P], ACT.Copy)\
          .then_inc(setup_drained, 1)
        act.wait_ge(setup_filled, 3)
        nc.scalar.activation(w_f[:, 3:5, :].rearrange("p a b -> p (a b)"), ps_g[:, 0:2 * P], ACT.Copy)\
          .then_inc(setup_drained, 1)
        for k, name in enumerate(PRE0):
            use(k, name, 0, 0)

        def slot(i, j):
            for p in range(SUB):
                exps(i, j, p)
                copy_probsT(i, j, p)
                for n, name, jj in glue_uses(i, j, p):
                    use(n, name, i, jj)

        walk(act, slot)
        for n, name, j in tail_uses():
            use(n, name, ITERS - 1, j)
        act.wait_ge(gap_ready, 1)
        nc.scalar.activation(w1st[:], gap[:], ACT.Exp).then_inc(weight_ready, 1)
        experts_act(act)

    @block.vector
    def _(dve):
        V = nc.vector

        def softmax_shift(i, j, p):
            n = pair_no(i, j, p)
            dve.wait_ge(scores_ready, n + 1)
            V.reduce_max(rmax[p % 2][:], ps_s[p % 2][:], AX.X).then_inc(rmax_ready, 1)
            wait(dve, probsT_filled, 2 * (n - 1))
            dve.wait_ge(rmax_ready, n + 1)
            V.tensor_tensor(probs[p % 2][:], ps_s[p % 2][:],
                            rmax[p % 2][:].unsqueeze(2).broadcast_to([P, HEADS, SEQ]), ALU.subtract)\
             .then_inc(centered, 1)

        def normalise(n, r, p):
            dve.wait_ge(out_ready, n + 1)
            halves = []
            for b in range(2):
                rows = slice(SEQ * b, SEQ * b + SEQ)
                o = ps_o[rows, b * (VW + PAD):b * (VW + PAD) + VW].rearrange("p (h c) -> p h c", h=HEADS)
                halves.append((rows, o))
                last = V.reciprocal(rden[rows, :], o[:, :, D])
            last.then_inc(rden_ready, 1)
            dve.wait_ge(rden_ready, n + 1)
            for rows, o in halves:
                last = V.tensor_tensor(att[r][rows, p, :].rearrange("p (h d) -> p h d", h=HEADS), o[:, :, 0:D],
                                       rden[rows, :].unsqueeze(2).broadcast_to([SEQ, HEADS, D]), ALU.mult)
            last.then_inc(heads_ready, 1)

        def norm(m, factors_at, src, pieces):
            for s in range(SUB):
                last = V.bn_stats(stats[:, s, :], src[:, s, :])
            last.then_inc(stats_ready, 1)
            wait_plain(stats_ready, m)
            for s in range(SUB):
                last = V.bn_aggr(mv[:, s, :], stats[:, s, :])
            last.then_inc(mv_ready, 1)
            dve.wait_ge(pool_step, factors_at)
            for dst, factor, centre in pieces:
                for s in range(SUB):
                    if centre:
                        last = V.tensor_scalar(dst[:, s, :], src[:, s, :], mv[:, s, 0:1], factor[:, s:s + 1],
                                               ALU.subtract, ALU.mult)
                    else:
                        last = V.tensor_scalar(dst[:, s, :], src[:, s, :], factor[:, s:s + 1], None, ALU.mult)
            last.then_inc(normed, 1)

        def wait_plain(sem_, value):
            dve.wait_ge(sem_, value)
            V.tensor_copy(turn[:], small[:, 0:1])

        def pre_norm(i, j):
            kind, r = kind_of(j), j % 2
            m = norm_index(i, j, "pre")
            at = 2 * (j + 1) if isinstance(i, int) and i == 0 and j <= 1 else steps_before(i, j - 1)
            if not (isinstance(i, int) and i == 0 and j <= 1):
                at = at + (7 if kind == 2 else 2)
            if kind == 0:
                dve.wait_ge(x_loaded[r], 16 * (tile_turn(i, j) + 1))
                norm(m, at, xin[r], ((xh, rstd, True),))
            elif kind == 1:
                norm(m, at, xres[r], ((xh, rstd, True),))
            else:
                norm(m, at, xres[r], ((fres[r], rstd, True), (xh, rboth, True)))

        def values_out(n, i, j, half):
            r = j % 2
            dve.wait_ge(glue_filled, n + 1)
            v = vbd[r][:, 4 * half * VW:4 * (half + 1) * VW].rearrange("p (b k c) -> p b k c", b=4, k=HEADS // 2)
            ps = ps_g[:].rearrange("p (b k c) -> p b k c", b=4, k=HEADS // 2)
            for q in range(2):
                rows = slice(SEQ * q, SEQ * q + SEQ)
                last = V.tensor_copy(v[rows, :, :, q * (D + 1):q * (D + 1) + D], ps[rows, :, :, q * D:q * D + D])
            last.then_inc(glue_drained, 1)

        def table(c):
            return const[:, c:c + SEQ].unsqueeze(1).broadcast_to([P, 2 * SUB, SEQ])

        def by_seq(ap):
            return ap.rearrange("p (b q) -> p b q", q=SEQ)

        def use(n, name, i, j):
            kind, r = kind_of(j), j % 2
            if name in ("v0", "v1"):
                values_out(n, i, j, int(name[1]))
            elif name == "wo" and kind == 0:
                dve.wait_ge(glue_filled, n + 1)
                V.tensor_tensor(xres[r][:], ps_g[:].rearrange("p (s e) -> p s e", s=SUB), xin[r][:], ALU.add)\
                 .then_inc(glue_drained, 1)
                dve.wait_ge(glue_drained, n + 1)
                pre_norm(i, j + 2)
            elif name == "ff":
                dve.wait_ge(b2_added, tile_no(i, j) + 1)
                dve.wait_ge(glue_filled, n + 1)
                V.tensor_tensor(xres[r][:], ps_g[:].rearrange("p (s e) -> p s e", s=SUB), xres[r][:], ALU.add)\
                 .then_inc(glue_drained, 1)
                dve.wait_ge(glue_drained, n + 1)
                pre_norm(i, j + 2)
            elif name == "wo":
                dve.wait_ge(glue_filled, n + 1)
                V.tensor_tensor(hres[:], ps_g[:].rearrange("p (s e) -> p s e", s=SUB), fres[r][:], ALU.add)\
                 .then_inc(glue_drained, 1)
            elif name == "lg":
                dve.wait_ge(glue_filled, n + 1)
                V.tensor_copy(lgs[:].rearrange("p s e -> p (s e)"), ps_g[:, 0:SUB * EXPERTS])\
                 .then_inc(glue_drained, 1)
                dve.wait_ge(glue_drained, n + 1)
                V.tensor_tensor(base[:], hres[:], xres[r][:], ALU.add).then_inc(export_ready, 1)
            elif kind == 2 and name in ("q", "k"):
                dve.wait_ge(glue_filled, n + 1)
                V.tensor_tensor(by_seq(rope[:, 0, :]), by_seq(ps_g[:]), table(C_COS), ALU.mult)\
                 .then_inc(glue_drained, 1)
            elif name in ("qr", "kr"):
                dve.wait_ge(glue_filled, n + 1)
                V.tensor_tensor(by_seq(rope[:, 1, :]), by_seq(ps_g[:]), table(C_SIN), ALU.mult)\
                 .then_inc(roped, 1)
                dve.wait_ge(roped, 2 * tile_no(i, j) + (1 if name == "kr" else 2))
                if name == "kr":
                    wait(dve, kbd_loaded[r], 16 * HEADS * job_turn(i, j))
                dst = (qT if name == "qr" else kS)[r]
                ins = V.tensor_tensor(dst[:], rope[:, 0, :], rope[:, 1, :], ALU.add)
                ins.then_inc(glue_drained, 1)

        def rms_norm(i, j):
            t = tile_no(i, j)
            dve.wait_ge(exported, EXPORT * (t + 1))
            m = norm_index(i, j, "post")
            if isinstance(i, int) and i == ITERS - 1:
                at = steps_before(i, JOBS - 1) + (4 if j == JOBS - 2 else 8)
            else:
                at = steps_before(i, j + 1) + 6
            norm(m, at, hres, ((hn, rstd, False),))

        dve.wait_ge(weights_loaded, 16 * N_LOADS)
        V.tensor_copy(identb[:], ident)
        V.tensor_copy(maskb[:], const[:, C_MASK:C_MASK + SEQ])
        for k in range(2):
            V.tensor_scalar(w_f[:, k, :], rawf[:, k, :], cols[:, 5:6], None, ALU.mult)
        V.tensor_scalar(w_f[:, 2, :], w_f[:, 2, :], cols[:, 5:6], None, ALU.mult)
        V.tensor_scalar(w_r[:], w_r[:], cols[:, 6:7], None, ALU.mult).then_inc(const_ready, 1)
        dve.wait_ge(pool_const, 1)
        pre_norm(0, 0)
        for k, name in enumerate(PRE0):
            use(k, name, 0, 0)
        pre_norm(0, 1)

        def slot(i, j):
            for p in range(SUB):
                softmax_shift(i, j, p)
                n = pair_no(i, j, p)
                if p > 0:
                    normalise(n - 1, j % 2, p - 1)
                elif j > 0:
                    normalise(n - 1, (j - 1) % 2, SUB - 1)
                if p == 0 and j in (5, 6) and not is_last(i, j):
                    pre_norm(i, j + 1)
                for m, name, jj in glue_uses(i, j, p):
                    use(m, name, i, jj)
                if p == 2 and j in (5, 6):
                    dve.wait_ge(glue_drained, glue_before(i, j) + 2)
                    rms_norm(i, j - 1)

        walk(dve, slot)
        normalise(pair_no(ITERS - 1, JOBS - 1, SUB - 1), (JOBS - 1) % 2, SUB - 1)
        for n, name, j in tail_uses():
            use(n, name, ITERS - 1, j)
            if name == "wo":
                dve.wait_ge(glue_drained, n + 1)
                rms_norm(ITERS - 1, j)
        route_dve(dve)
        experts_dve(dve)
        combine_dve(dve)

    @block.gpsimd
    def _(pool):
        G = nc.gpsimd
        var, mean = mv[:, :, 1], mv[:, :, 0]
        eps5, eps6, neg_half = small[:, 0:4], small[:, 4:8], small[:, 8:12]
        for r in range(2):
            G.memset(kbd[r][:], 0.0)
            G.memset(vbd[r][:], 0.0)
        G.memset(zrow[:], 0.0)
        G.memset(small[:, 0:4], 1e-5)
        G.memset(small[:, 4:8], 1e-6)
        G.memset(ones[:], 1.0)
        G.memset(small[:, 8:12], -0.5).then_inc(pool_clear, 1)
        pool.wait_ge(pool_clear, 1)
        for r in range(2):
            v = vbd[r][:, 0:2 * SUB * VW].rearrange("p (b k c) -> p b k c", b=2 * SUB, k=HEADS // 2)
            for q in range(2):
                rows = slice(SEQ * q, SEQ * q + SEQ)
                last = G.memset(v[rows, :, :, q * (D + 1) + D:q * (D + 1) + D + 1], 1.0)
        last.then_inc(pool_const, 1)

        def chain(k0):
            count = [k0]

            def step(out_, x, y, op):
                wait(pool, pool_step, count[0])
                G.tensor_tensor(out_, x, y, op).then_inc(pool_step, 1)
                count[0] = count[0] + 1
            return step

        def layer_norm(k0, m, both):
            step = chain(k0)
            pool.wait_ge(mv_ready, m)
            step(pt[:, 0, :], var, eps5, ALU.add)
            step(rstd[:], pt[:, 0, :], neg_half, ALU.pow)
            if both:
                step(pt[:, 1, :], rstd[:], rstd[:], ALU.mult)
                step(pt[:, 2, :], pt[:, 1, :], var, ALU.mult)
                step(pt[:, 3, :], pt[:, 2, :], eps6, ALU.add)
                step(pt[:, 1, :], pt[:, 3, :], neg_half, ALU.pow)
                step(rboth[:], rstd[:], pt[:, 1, :], ALU.mult)

        def rms(k0, m):
            step = chain(k0)
            pool.wait_ge(mv_ready, m)
            step(pt[:, 0, :], mean, mean, ALU.mult)
            step(pt[:, 1, :], pt[:, 0, :], var, ALU.add)
            step(pt[:, 2, :], pt[:, 1, :], eps6, ALU.add)
            step(rstd[:], pt[:, 2, :], neg_half, ALU.pow)

        layer_norm(0, 1, False)
        layer_norm(2, 2, False)
        pool.wait_ge(gate_up_loaded, 16 * (2 + HC))
        G.tensor_scalar(w_gu[:], w_gu[:], cols[:, 6:7], None, ALU.mult).then_inc(gate_up_ready, 1)

        def slot(i, j):
            if j == 0:
                return
            k0, m = steps_before(i, j), norms_before(i, j) + 1
            if j in (1, 2):
                layer_norm(k0, m, False)
                pool.wait_ge(normed, m)
                G.tensor_tensor(xres[j - 1][:], xres[j - 1][:], b2[:].unsqueeze(1).broadcast_to([P, SUB, E]),
                                ALU.add).then_inc(b2_added, 1)
            elif j in (3, 4):
                layer_norm(k0, m, True)
            elif is_last(i, j):
                rms(k0, m)
            else:
                layer_norm(k0, m, False)
                rms(k0 + 2, m + 1)

        walk(pool, slot)
        rms(steps_before(ITERS - 1, JOBS - 1) + 4, norms_before(ITERS - 1, JOBS - 1) + 2)
        dispatch_pool(pool)
        gather_pool(pool)


INPUTS = ["x", "ctx_768", "L0_attn_in_proj_weight", "L0_attn_out_proj_weight",
          "L0_xattn_Wq", "L0_xattn_bq", "L0_xattn_Wk", "L0_xattn_bk", "L0_xattn_Wv", "L0_xattn_bv",
          "L0_xattn_W1", "L0_xattn_b1", "L0_xattn_W2", "L0_xattn_b2",
          "L0_ffn_wq", "L0_ffn_wk", "L0_ffn_wv", "L0_ffn_wo", "L0_ffn_w_router",
          "L0_ffn_wg", "L0_ffn_wu", "L0_ffn_wd", "L0_ffn_g1", "L0_ffn_g2"]


def kernel(**inputs):
    import numpy as _np
    import concourse.bacc as _bacc
    from concourse import mybir as _mybir
    from concourse.bass_utils import run_bass_kernel_spmd as _run

    nc = _bacc.Bacc("TRN2", target_bir_lowering=False, num_devices=1)
    arrays = {f"in_{n}": _np.ascontiguousarray(inputs[n]) for n in INPUTS}
    arrays["in_const"] = constants()
    args = {n[3:]: nc.dram_tensor(n, v.shape, _mybir.dt.from_np(v.dtype), kind="ExternalInput").ap()
            for n, v in arrays.items()}
    out = nc.dram_tensor("out", (BATCH, SEQ, E), F32, kind="ExternalOutput").ap()
    build(nc, args, out)
    r = _run(nc, [arrays], core_ids=[0])
    return r.results[0]["out"]
```

```python
from contextlib import ExitStack

import numpy as np

import concourse.bass as bass
from concourse import mybir

F32 = mybir.dt.float32
BF16 = mybir.dt.bfloat16
I32 = mybir.dt.int32
U32 = mybir.dt.uint32
ALU = mybir.AluOpType
ACT = mybir.ActivationFunctionType
AX = mybir.AxisListType

P = 128
BATCH, SEQ, E, CE = 64, 64, 128, 96
HEADS, D = 16, 8
TOKENS = BATCH * SEQ
TILE, SUB = 512, 4
TILES = TOKENS // TILE
SUBS = TOKENS // P
EXPERTS, HIDDEN = 8, 384
HC = HIDDEN // P
FF = 256
BLOCKS = (2 * TOKENS + EXPERTS * (P - 1)) // P + 1
SCALE = float(D) ** -0.5
VW = HEADS * (D + 1)
PAD = 48

JOBS = 6
ITERS = TILES // 2

C_ID, C_ROT, C_LOW, C_COS, C_SIN, C_MASK, C_IOTA, C_BLK = 0, 128, 256, 384, 448, 512, 576, 584
C_ALL = C_BLK + BLOCKS
N_LOADS = 23
EXPORT = 3 * 16


def constants():
    c = np.zeros((P, C_ALL), np.float32)
    c[:, C_ID:C_ID + P] = np.eye(P)
    half = D // 2
    for o in range(P):
        d = o % D
        if d < half:
            c[o + half, C_ROT + o] = -1.0
        else:
            c[o - half, C_ROT + o] = 1.0
    c[:, C_LOW:C_LOW + P] = np.triu(np.ones((P, P)), 1)
    inv = 1.0 / 10000.0 ** (np.arange(0, D, 2, dtype=np.float32) / D)
    freqs = np.einsum("i,j->ij", np.arange(SEQ, dtype=np.float32), inv)
    emb = np.concatenate([freqs, freqs], axis=-1)
    c[:, C_COS:C_COS + SEQ] = np.tile(np.cos(emb).T, (HEADS, 1))
    c[:, C_SIN:C_SIN + SEQ] = np.tile(np.sin(emb).T, (HEADS, 1))
    q, k = np.arange(P)[:, None] % SEQ, np.arange(SEQ)[None, :]
    c[:, C_MASK:C_MASK + SEQ] = np.where(k > q, -1e30, 0.0)
    c[:, C_IOTA:C_IOTA + EXPERTS] = np.arange(EXPERTS)
    c[:, C_BLK:C_BLK + BLOCKS] = np.arange(BLOCKS)
    return c


SLOT_FIRST = ((("xT",), ("k",), ()), (("q",), ("v0",), ()), (("v1",), (), ()), ((), (), ()))
SLOT_A = ((("cT",), ("oT", "k"), ("wo", "st")), (("v0", "ap"), ("xT",), ("v1",)),
          (("q",), (), ()), ((), (), ()))
SLOT_B = (((), ("oT",), ("h0", "h1")), (("ff", "st"), (), ("ap",)),
          (("xT",), ("k",), ("kr",)), (("q",), ("qr",), ("v0", "v1")))
SLOT_C = ((("st",), ("oT",), ("ap",)), (("xT", "wo"), ("k", "st2"), ("q",)),
          (("v0", "ap2"), ("hT",), ("v1",)), (("lg",), (), ()))
SCORES_FIRST = (0, 1, 2, 5, 6)
SLOTS = {0: SLOT_FIRST, 1: SLOT_A, 2: SLOT_A, 3: SLOT_B, 4: SLOT_B, 5: SLOT_C, 6: SLOT_C}
PRE0 = ("xT", "k", "q", "v0", "v1")
POST = {0: ("oT", "wo"), 1: ("oT", "h0", "h1", "ff"), 2: ("oT", "wo", "st2", "ap2", "hT", "lg")}
TAIL = ("oT", "wo", "st2", "ap2", "hT", "lg")
ON_DVE_ONLY = ("st", "ap", "st2", "ap2")


def ring_uses(j, last=False):
    post = () if j == 0 else POST[((j - 1) % JOBS) // 2]
    for p in range(SUB):
        for place in range(3):
            if place == 1 and p > 0:
                yield p, place, "att"
            for name in SLOTS[j][p][place]:
                if name in post or not last:
                    yield p, place, name
    yield SUB - 1, 3, "att"


def count(uses):
    return sum(name not in ON_DVE_ONLY for _, _, name in uses)


N_SLOT = {j: count(ring_uses(j)) for j in SLOTS}
N_ITER = sum(N_SLOT[j] for j in range(1, JOBS + 1))
N_FIRST = len(PRE0) + N_SLOT[0]
assert N_ITER % 2 == 0
NORMS = {1: 1, 2: 1, 3: 1, 4: 1, 5: 2, 6: 2}
NORMS_ITER, NORMS_FIRST = sum(NORMS.values()), 2


class Use:

    def __init__(self, i, c):
        self.i, self.c, self.bank = i, c, c % 2

    def filled(self):
        return self.i * N_ITER + (self.c + 1)

    def before_in_bank(self):
        return self.i * (N_ITER // 2) + self.c // 2

    def drained(self):
        return self.i * (N_ITER // 2) + (self.c // 2 + 1)


def use_of(i, j, p, place, name, last=False):
    base = len(PRE0) if j == 0 else N_FIRST + sum(N_SLOT[x] for x in range(1, j))
    n = 0
    for step in ring_uses(j, last):
        if step == (p, place, name):
            return Use(i, base + n)
        n += step[2] not in ON_DVE_ONLY
    raise ValueError(name)


def named_use(i, j, name, last=False):
    p, place, _ = next(x for x in ring_uses(j, last) if x[2] == name)
    return use_of(i, j, p, place, name, last)


def norms_before(i, j):
    return NORMS_FIRST + i * NORMS_ITER + sum(NORMS[x] for x in range(1, j))


def kind_of(j):
    return (j % JOBS) // 2


def wait(eng, sem, value):
    if not (isinstance(value, int) and value <= 0):
        eng.wait_ge(sem, value)


def build(nc, a, out):
    with ExitStack() as ctx:
        _build(nc, ctx, a, out)


def _build(nc, ctx, a, out):
    def sb(name, shape, dt=F32):
        return ctx.enter_context(nc.sbuf_tensor(name, shape, dt))

    def sem(name):
        return ctx.enter_context(nc.semaphore(name))

    const = sb("const", [P, C_ALL])
    ident = const[:, C_ID:C_ID + P]
    identb = sb("identb", [P, P], BF16)
    maskb = sb("maskb", [P, SEQ], BF16)
    raw = sb("raw", [P, 4, P])
    rawf = sb("rawf", [P, 2, P])
    rawT = sb("rawT", [P, 2, P])
    w_a = sb("w_a", [P, 4, P])
    w_x = sb("w_x", [P, 3, P])
    w1 = sb("w1", [P, FF])
    w2 = sb("w2", [P, 2, P])
    w_f = sb("w_f", [P, 6, P])
    w_r = sb("w_r", [P, EXPERTS])
    cols = sb("cols", [P, 8])
    b2 = sb("b2", [P, E])
    w_gu = sb("w_gu", [P, EXPERTS * 2 * HIDDEN])
    w_d = sb("w_d", [P, HC, EXPERTS * P])
    small = sb("small", [P, 12])
    xin = [sb(f"xin{r}", [P, SUB, E]) for r in range(2)]
    cin = [sb(f"cin{r}", [P, SUB, CE]) for r in range(2)]
    xres = [sb(f"xres{r}", [P, SUB, E]) for r in range(2)]
    fres = [sb(f"fres{r}", [P, SUB, E]) for r in range(2)]
    xh = sb("xh", [P, SUB, E])
    hn = sb("hn", [P, SUB, E])
    hres = sb("hres", [P, SUB, E])
    base = sb("base", [P, SUB, E])
    lgs = sb("lgs", [P, SUB, EXPERTS])
    stats = sb("stats", [P, SUB, 6])
    mv = sb("mv", [P, SUB, 2])
    rstd = sb("rstd", [P, SUB])
    rboth = sb("rboth", [P, SUB])
    pt = sb("pt", [P, 4, SUB])
    xT = sb("xT", [P, TILE])
    cT = sb("cT", [CE, TILE])
    oT = sb("oT", [P, TILE])
    h1T = sb("h1T", [P, 2, TILE])
    hT = sb("hT", [P, TILE])
    rope = sb("rope", [P, 2, TILE])
    qT = [sb(f"qT{r}", [P, TILE]) for r in range(2)]
    kS = [sb(f"kS{r}", [P, TILE]) for r in range(2)]
    kbd = [sb(f"kbd{r}", [P, HEADS, TILE]) for r in range(2)]
    vbd = [sb(f"vbd{r}", [P, (2 * SUB + 1) * VW]) for r in range(2)]
    probs = [sb(f"probs{r}", [P, HEADS, SEQ]) for r in range(2)]
    probsT = [sb(f"probsT{r}", [P, HEADS // 2, P]) for r in range(2)]
    rmax = [sb(f"rmax{r}", [P, HEADS]) for r in range(2)]
    rden = [sb(f"rden{r}", [P, HEADS]) for r in range(2)]
    att = [sb(f"att{r}", [P, SUB, E]) for r in range(2)]
    lg_all = sb("lg_all", [P, SUBS, EXPERTS])
    ones = sb("ones", [P, P])
    zrow = sb("zrow", [P, E])
    turn = sb("turn", [P, 1])
    big = EXPERTS * SUBS
    route = kbd[1][:].rearrange("p h t -> p (h t)")
    spare = kbd[0][:].rearrange("p h t -> p (h t)")

    def grid(k):
        return route[:, k * big:(k + 1) * big].rearrange("p (s e) -> p s e", e=EXPERTS)

    oh0, oh1, sel3, less, keyed, second, scan0, scan1, rank = [grid(k) for k in range(9)]
    sel = route[:, 2 * big:3 * big]
    line = [route[:, 9 * big + k * SUBS:9 * big + (k + 1) * SUBS] for k in range(9)]
    top0, top1, idx0, idx1, gap, w1st, wsum, posf0, posf1 = line
    weight0, weight1 = sb("weight0", [P, SUBS]), sb("weight1", [P, SUBS])
    pos0, pos1 = sb("pos0", [P, SUBS], I32), sb("pos1", [P, SUBS], I32)
    counts_i = sb("counts_i", [P, EXPERTS], I32)
    blocks_i = sb("blocks_i", [P, EXPERTS], I32)
    blocks_f = sb("blocks_f", [P, 3, EXPERTS])
    first_row = sb("first_row", [P, EXPERTS])
    expert_of = sb("expert_of", [1, BLOCKS], I32)
    past = route[0:1, 12 * big:12 * big + BLOCKS * EXPERTS].rearrange("p (j e) -> p j e", e=EXPERTS)
    past_sum = route[0:1, 15 * big:15 * big + BLOCKS]

    def spare_pair(at, n):
        return [spare[:, at + r * n:at + (r + 1) * n] for r in range(2)]

    xb, xbT = spare_pair(0, P), spare_pair(2 * P, P)
    th, hh = spare_pair(512, HIDDEN), spare_pair(512 + 2 * HIDDEN, HIDDEN)
    hbT = spare_pair(512 + 4 * HIDDEN, HIDDEN)
    yb = spare_pair(512 + 6 * HIDDEN, P)
    RING = 4
    gy = [[spare[:, 4096 + (2 * r + k) * E:4096 + (2 * r + k + 1) * E] for k in range(2)] for r in range(RING)]
    hn_all = route[:, 16 * big:].rearrange("p (s e) -> p s e", e=E)
    hn_dram = nc.dram_tensor("hn_dram", [P, SUBS, E], F32).ap()
    base_dram = nc.dram_tensor("base_dram", [P, SUBS, E], F32).ap()
    xs_dram = nc.dram_tensor("xs_dram", [BLOCKS * P, E], F32).ap()
    ys_dram = nc.dram_tensor("ys_dram", [BLOCKS * P, E], F32).ap()

    ps_s = [ctx.enter_context(nc.psum_tensor(f"ps_s{r}", [P, HEADS, SEQ], F32)) for r in range(2)]
    ps_t = [ctx.enter_context(nc.psum_tensor(f"ps_t{r}", [P, 4, P], F32)) for r in range(2)]
    ring = [ctx.enter_context(nc.psum_tensor(f"ring{r}", [P, 512], F32)) for r in range(2)]
    ps_o, ps_g = ring

    weights_loaded = sem("weights_loaded")
    gate_up_loaded = sem("gate_up_loaded")
    pool_clear = sem("pool_clear")
    pool_const = sem("pool_const")
    const_ready = sem("const_ready")
    setup_filled = sem("setup_filled")
    setup_drained = sem("setup_drained")
    x_loaded = [sem(f"x_loaded{r}") for r in range(2)]
    ctx_loaded = [sem(f"ctx_loaded{r}") for r in range(2)]
    kbd_loaded = [sem(f"kbd_loaded{r}") for r in range(2)]
    scores_ready = sem("scores_ready")
    rmax_ready = sem("rmax_ready")
    centered = sem("centered")
    probs_ready = sem("probs_ready")
    probsT_filled = sem("probsT_filled")
    probsT_copied = sem("probsT_copied")
    rden_ready = sem("rden_ready")
    ring_filled = sem("ring_filled")
    ring_drained = [sem(f"ring_drained{r}") for r in range(2)]
    stats_ready = sem("stats_ready")
    mv_ready = sem("mv_ready")
    pool_step = sem("pool_step")
    normed = sem("normed")
    b2_added = sem("b2_added")
    rotated = sem("rotated")
    exported = sem("exported")
    export_ready = sem("export_ready")
    dve_chain = sem("dve_chain")
    sel_ready = sem("sel_ready")
    ranks_ready = sem("ranks_ready")
    gap_ready = sem("gap_ready")
    weight_ready = sem("weight_ready")
    xs_cleared = sem("xs_cleared")
    pos_ready = sem("pos_ready")
    scattered = sem("scattered")
    hn_loaded = sem("hn_loaded")
    gate_up_ready = sem("gate_up_ready")
    xb_loaded = [sem(f"xb_loaded{r}") for r in range(2)]
    ys_stored = [sem(f"ys_stored{r}") for r in range(2)]
    xbT_filled, xbT_copied = sem("xbT_filled"), sem("xbT_copied")
    gu_filled, tanh_ready, gated, h_ready = sem("gu_filled"), sem("tanh_ready"), sem("gated"), sem("h_ready")
    hbT_filled, hbT_copied = sem("hbT_filled"), sem("hbT_copied")
    y_filled, y_copied = sem("y_filled"), sem("y_copied")
    base_loaded = sem("base_loaded")
    fetched = [sem(f"fetched{r}") for r in range(RING)]
    first_added = sem("first_added")
    summed = sem("summed")
    stored = sem("stored")

    steps = {1: 2, 2: 2, 3: 5, 4: 5, 5: 6, 6: 6}

    def steps_before(i, j):
        return 4 + i * sum(steps.values()) + sum(steps[x] for x in range(1, j))

    def pair_no(i, j, p):
        return i * (JOBS * SUB) + j * SUB + p

    def tile_no(i, j):
        return 2 * i + 2 * (j // JOBS) + j % 2

    def tile_turn(i, j):
        return i + j // JOBS

    def job_turn(i, j):
        return 3 * i + j // 2

    def norm_index(i, j, which):
        if which == "pre":
            return j + 1 if isinstance(i, int) and i == 0 and j <= 1 else norms_before(i, j - 1) + 1
        if isinstance(i, int) and i == ITERS - 1:
            return norms_before(i, JOBS - 1) + (1 if j == JOBS - 2 else 2)
        return norms_before(i, j + 1) + 2

    def is_last(i, j):
        return isinstance(i, int) and i == ITERS - 1 and j == JOBS - 1

    def walk(eng, slot):
        slot(0, 0)
        with eng.Fori(0, ITERS - 1) as i:
            for j in range(1, JOBS + 1):
                slot(i, j)
        for j in range(1, JOBS):
            slot(ITERS - 1, j)

    def steps_at(i, j, p, place):
        post = () if j == 0 else POST[kind_of(j - 1)]
        last = is_last(i, j)
        for name in SLOTS[j][p][place]:
            if name in post:
                yield use_of(i, j, p, place, name, last), name, j - 1
            elif not last:
                yield use_of(i, j, p, place, name), name, j + 1

    def att_use(i, j, p):
        place = (p + 1, 1) if p < SUB - 1 else (p, 3)
        return use_of(i, j, *place, "att", is_last(i, j))

    def source(i, j, name):
        if name in TAIL[0:2] + ("h0", "h1", "hT", "ff", "lg"):
            if isinstance(i, int) and i == ITERS - 1 and j == JOBS - 1:
                return tail_use(name)
            return named_use(i, j + 1, name, is_last(i, j + 1))
        if isinstance(i, int) and i == 0 and j == 0:
            return Use(0, PRE0.index(name))
        return named_use(i, j - 1, name)

    def att_before(i, j, p):
        if p >= 2:
            return att_use(i, j, p - 2)
        if j == 1:
            return Use(i, N_FIRST - 2 + p)
        return att_use(i, j - 1, p + 2)

    def tail_use(name):
        names = [x for x in TAIL if x not in ON_DVE_ONLY]
        c = N_FIRST + sum(N_SLOT[x] for x in range(1, JOBS - 1)) + count(ring_uses(JOBS - 1, True))
        return Use(ITERS - 1, c + names.index(name))

    def route_dve(dve):
        V = nc.vector
        n = [0]

        def step(ins):
            n[0] += 1
            ins.then_inc(dve_chain, 1)
            dve.wait_ge(dve_chain, n[0])

        iota = const[:, C_IOTA:C_IOTA + EXPERTS].unsqueeze(1).broadcast_to([P, SUBS, EXPERTS])

        def wide(x):
            return x.unsqueeze(2).broadcast_to([P, SUBS, EXPERTS])

        dve.wait_ge(exported, EXPORT * (TILES + 1))
        for src, top, idx, oh in ((lg_all[:], top0, idx0, oh0), (second, top1, idx1, oh1)):
            step(V.reduce_max(top, src, AX.X))
            step(V.tensor_tensor(less, src, wide(top), ALU.is_lt))
            step(V.scalar_tensor_tensor(keyed, less, float(EXPERTS), iota, ALU.mult, ALU.add))
            step(V.tensor_reduce(idx, keyed, AX.X, ALU.min))
            step(V.tensor_tensor(oh, iota, wide(idx), ALU.is_equal))
            if src is not second:
                step(V.scalar_tensor_tensor(second, oh, -1e30, src, ALU.mult, ALU.add))
        V.tensor_tensor(sel3, oh0, oh1, ALU.add).then_inc(sel_ready, 1)
        V.tensor_tensor(gap, top1, top0, ALU.subtract).then_inc(gap_ready, 1)
        dve.wait_ge(ranks_ready, 1)
        within = ps_g[:, 0:big].rearrange("p (s e) -> p s e", e=EXPERTS)
        total = ps_g[:, big:2 * big].rearrange("p (s e) -> p s e", e=EXPERTS)
        step(V.tensor_copy(scan0, total))
        src, dst = scan0, scan1
        for k in (1, 2, 4, 8, 16):
            V.tensor_copy(dst[:, 0:k, :], src[:, 0:k, :])
            step(V.tensor_tensor(dst[:, k:, :], src[:, k:, :], src[:, 0:SUBS - k, :], ALU.add))
            src, dst = dst, src
        step(V.tensor_scalar(counts_i[:], src[:, SUBS - 1, :], float(P - 1), None, ALU.add))
        step(V.tensor_scalar(blocks_i[:], counts_i[:], 7, None, ALU.logical_shift_right))
        step(V.tensor_copy(blocks_f[:, 0, :], blocks_i[:]))
        a0, b0 = 0, 1
        for k in (1, 2, 4):
            V.tensor_copy(blocks_f[:, b0, 0:k], blocks_f[:, a0, 0:k])
            step(V.tensor_tensor(blocks_f[:, b0, k:], blocks_f[:, a0, k:], blocks_f[:, a0, 0:EXPERTS - k], ALU.add))
            a0, b0 = b0, (2 if k == 1 else a0)
        ends = blocks_f[:, a0, :]
        step(V.tensor_copy(blocks_f[:, b0, :], blocks_i[:]))
        step(V.tensor_tensor(first_row[:], ends, blocks_f[:, b0, :], ALU.subtract))
        step(V.tensor_scalar(first_row[:], first_row[:], float(P), None, ALU.mult))
        step(V.tensor_tensor(rank, src, total, ALU.subtract))
        step(V.tensor_tensor(rank, rank, within, ALU.add))
        step(V.tensor_tensor(rank, rank, first_row[:].unsqueeze(1).broadcast_to([P, SUBS, EXPERTS]), ALU.add))
        for oh, posf, pos in ((oh0, posf0, pos0), (oh1, posf1, pos1)):
            step(V.tensor_tensor(keyed, oh, rank, ALU.mult))
            step(V.reduce_sum(posf, keyed, AX.X))
            V.tensor_copy(pos[:], posf).then_inc(pos_ready, 1)
        step(V.tensor_tensor(past, const[0:1, C_BLK:C_BLK + BLOCKS].unsqueeze(2).broadcast_to([1, BLOCKS, EXPERTS]),
                             ends[0:1, :].unsqueeze(1).broadcast_to([1, BLOCKS, EXPERTS]), ALU.is_ge))
        step(V.reduce_sum(past_sum, past, AX.X))
        V.tensor_scalar(expert_of[:], past_sum, float(EXPERTS - 1), None, ALU.min).then_inc(pos_ready, 1)
        dve.wait_ge(weight_ready, 1)
        step(V.tensor_scalar(wsum, w1st, 1.0, None, ALU.add))
        step(V.reciprocal(weight0[:], wsum))
        step(V.tensor_tensor(weight1[:], w1st, weight0[:], ALU.mult))

    def dispatch_pool(pool):
        pool.wait_ge(xs_cleared, 16)
        pool.wait_ge(pos_ready, 2)
        pool.wait_ge(hn_loaded, 16)
        for s in range(SUBS):
            for pos in (pos0, pos1):
                nc.gpsimd.indirect_dma_start(
                    out=xs_dram, out_offset=bass.IndirectOffsetOnAxis(ap=pos[:, s:s + 1], axis=0),
                    in_=hn_all[:, s, :], in_offset=None).then_inc(scattered, 16)

    def blocks(eng, step):
        for j in range(3):
            step(j, j % 2)
        with eng.Fori(0, (BLOCKS - 6) // 2) as i:
            step(i * 2 + 3, 1)
            step(i * 2 + 4, 0)
        for j in range(BLOCKS - 3, BLOCKS):
            step(j, j % 2)

    def there(j):
        return not isinstance(j, int) or 0 <= j < BLOCKS

    g_bank = [ps_s[0][:].rearrange("p h k -> p (h k)")[:, 512 * r:512 * r + HIDDEN] for r in range(2)]
    u_bank = [ps_s[1][:].rearrange("p h k -> p (h k)")[:, 512 * r:512 * r + HIDDEN] for r in range(2)]
    h_bank = [ps_t[r][:].rearrange("p a b -> p (a b)")[:, 0:HIDDEN] for r in range(2)]
    x_bank, y_bank = ps_o[:, 0:P], ps_g[:, 0:E]

    def experts_sp(sp):
        sp.wait_ge(scattered, 16 * 2 * SUBS)
        xs_b = xs_dram.rearrange("(b p) e -> b p e", p=P)
        ys_b = ys_dram.rearrange("(b p) e -> b p e", p=P)

        def one(ap, j):
            return ap[j] if isinstance(j, int) else ap[bass.ds(j, 1)].rearrange("o p e -> (o p) e")

        def load(j, r):
            sp.dma_start(xb[r], one(xs_b, j)).then_inc(xb_loaded[r], 16)

        load(0, 0)
        load(1, 1)

        def step(j, r):
            if there(j + 2):
                sp.wait_ge(xbT_filled, j + 1)
                load(j + 2, r)
            if there(j - 1):
                sp.wait_ge(y_copied, j)
                sp.dma_start(one(ys_b, j - 1), yb[1 - r]).then_inc(ys_stored[1 - r], 16)

        blocks(sp, step)
        sp.wait_ge(y_copied, BLOCKS)
        sp.dma_start(one(ys_b, BLOCKS - 1), yb[(BLOCKS - 1) % 2]).then_inc(ys_stored[(BLOCKS - 1) % 2], 16)
        sp.dma_start(hn_all, base_dram).then_inc(base_loaded, 16)
        for t in range(TILES):
            sp.wait_ge(summed, (t + 1) * SUB)
            sp.dma_start(out_t[t], hn_all[:, t * SUB:(t + 1) * SUB, :]).then_inc(stored, 16)
        sp.wait_ge(stored, 16 * TILES)

    def experts_pe(pe):
        mm = nc.tensor.matmul
        pe.wait_ge(pos_ready, 3)
        pe.wait_ge(gate_up_ready, 1)
        pe.wait_ge(gate_up_loaded, 16 * (2 + HC))

        def expert(j):
            at = expert_of[0:1, j:j + 1] if isinstance(j, int) else expert_of[0:1, bass.ds(j, 1)]
            return pe.value_load(at, min_val=0, max_val=EXPERTS - 1)

        def rows_T(j, r, half):
            pe.wait_ge(xb_loaded[r], half * 16 + 16)
            wait(pe, xbT_copied, j)
            nc.tensor.transpose(x_bank, xb[r], ident).then_inc(xbT_filled, 1)

        def gate_up(j, r):
            pe.wait_ge(xbT_copied, j + 1)
            wait(pe, h_ready, j - 1)
            e = expert(j)
            for k, bank in ((0, g_bank), (1, u_bank)):
                w = w_gu[:, bass.ds(e * (2 * HIDDEN) + k * HIDDEN, HIDDEN)]
                last = mm(bank[r], xbT[r], w, start=True, stop=True)
            last.then_inc(gu_filled, 1)

        def hidden_T(j, r):
            pe.wait_ge(h_ready, j + 1)
            wait(pe, hbT_copied, j - 1)
            for c in range(HC):
                last = nc.tensor.transpose(h_bank[r][:, c * P:(c + 1) * P], hh[r][:, c * P:(c + 1) * P], ident)
            last.then_inc(hbT_filled, 1)

        def down(j, r):
            pe.wait_ge(hbT_copied, j + 1)
            wait(pe, y_copied, j)
            e = expert(j)
            for c in range(HC):
                last = mm(y_bank, hbT[r][:, c * P:(c + 1) * P], w_d[:, c, bass.ds(e * P, P)],
                          start=(c == 0), stop=(c == HC - 1))
            last.then_inc(y_filled, 1)

        rows_T(0, 0, 0)
        rows_T(1, 1, 0)
        gate_up(0, 0)

        def step(j, r):
            if there(j + 1):
                gate_up(j + 1, 1 - r)
            if there(j - 1):
                down(j - 1, 1 - r)
            if there(j + 2):
                rows_T(j + 2, r, (j + 2 - r) // 2 if isinstance(j, int) else half_of(j, r) + 1)
            hidden_T(j, r)

        blocks(pe, step)
        down(BLOCKS - 1, (BLOCKS - 1) % 2)

    def half_of(j, r):
        return (j - r) // 2

    def experts_act(act):
        def rows_out(j, r):
            act.wait_ge(xbT_filled, j + 1)
            wait(act, gu_filled, j - 1)
            nc.scalar.activation(xbT[r], x_bank, ACT.Copy).then_inc(xbT_copied, 1)

        rows_out(0, 0)
        rows_out(1, 1)

        def step(j, r):
            act.wait_ge(gu_filled, j + 1)
            wait(act, h_ready, j - 1)
            nc.scalar.activation(th[r], g_bank[r], ACT.Tanh, scale=0.5).then_inc(tanh_ready, 1)
            if there(j + 2):
                rows_out(j + 2, r)
            act.wait_ge(hbT_filled, j + 1)
            wait(act, y_filled, j - 1)
            nc.scalar.activation(hbT[r], h_bank[r], ACT.Copy, scale=0.5).then_inc(hbT_copied, 1)

        blocks(act, step)

    def experts_dve(dve):
        V = nc.vector

        def copy_y(j, r, half):
            dve.wait_ge(y_filled, j + 1)
            wait(dve, ys_stored[r], half * 16)
            V.tensor_scalar(yb[r], y_bank, 1.0, None, ALU.mult).then_inc(y_copied, 1)

        def step(j, r):
            dve.wait_ge(tanh_ready, j + 1)
            V.scalar_tensor_tensor(th[r], th[r], 1.0, g_bank[r], ALU.add, ALU.mult).then_inc(gated, 1)
            wait(dve, hbT_filled, j - 1)
            dve.wait_ge(gated, j + 1)
            V.tensor_tensor(hh[r], th[r], u_bank[r], ALU.mult).then_inc(h_ready, 1)
            if there(j - 1):
                copy_y(j - 1, 1 - r, half_of(j - 1, 1 - r))

        blocks(dve, step)
        copy_y(BLOCKS - 1, (BLOCKS - 1) % 2, (BLOCKS - 1) // 2)

    def gather_pool(pool):
        pool.wait_ge(ys_stored[0], 16 * (BLOCKS // 2))
        pool.wait_ge(ys_stored[1], 16 * (BLOCKS // 2))
        for s in range(SUBS):
            if s >= RING:
                pool.wait_ge(summed, s - RING + 1)
            for k, pos in enumerate((pos0, pos1)):
                nc.gpsimd.indirect_dma_start(
                    out=gy[s % RING][k], out_offset=None, in_=ys_dram,
                    in_offset=bass.IndirectOffsetOnAxis(ap=pos[:, s:s + 1], axis=0)).then_inc(fetched[s % RING], 16)

    def combine_dve(dve):
        V = nc.vector
        dve.wait_ge(base_loaded, 16)
        for s in range(SUBS):
            y0, y1 = gy[s % RING]
            dve.wait_ge(fetched[s % RING], 32 * (s // RING + 1))
            V.scalar_tensor_tensor(y0, y0, weight0[:, s:s + 1], hn_all[:, s, :], ALU.mult, ALU.add)\
             .then_inc(first_added, 1)
            dve.wait_ge(first_added, s + 1)
            V.scalar_tensor_tensor(hn_all[:, s, :], y1, weight1[:, s:s + 1], y0, ALU.mult, ALU.add)\
             .then_inc(summed, 1)

    block = ctx.enter_context(nc.Block())

    x_t = a["x"].rearrange("b q e -> (b q) e").rearrange("(t s p) e -> t p s e", s=SUB, p=P)
    c_t = a["ctx_768"].rearrange("b q e -> (b q) e").rearrange("(t s p) e -> t p s e", s=SUB, p=P)
    out_t = out.rearrange("b q e -> (b q) e").rearrange("(t s p) e -> t p s e", s=SUB, p=P)

    def dyn(ap, t):
        if isinstance(t, int):
            return ap[t]
        return ap[bass.ds(t, 1)].rearrange("o p s e -> (o p) s e")

    def column(name, lo=0):
        return a[name][lo:lo + P].rearrange("(p o) -> p o", o=1)

    @block.sync
    def _(sp):
        def load_tile(t, r):
            sp.dma_start(xin[r][:], dyn(x_t, t)).then_inc(x_loaded[r], 16)
            sp.dma_start(cin[r][:], dyn(c_t, t)).then_inc(ctx_loaded[r], 16)

        loads = [(const[:], a["const"])]
        loads += [(raw[:, k, :], a["L0_attn_in_proj_weight"][k * P:(k + 1) * P, :]) for k in range(3)]
        loads += [(raw[:, 3, :], a["L0_attn_out_proj_weight"])]
        loads += [(rawf[:, 0, :], a["L0_ffn_wq"]), (rawf[:, 1, :], a["L0_ffn_wk"]),
                  (w_f[:, 2, :], a["L0_ffn_wv"]), (w_f[:, 5, :], a["L0_ffn_wo"])]
        loads += [(cols[:, 5:6], column("L0_ffn_g1")), (cols[:, 6:7], column("L0_ffn_g2"))]
        loads += [(w_x[:, 0, :], a["L0_xattn_Wq"]), (w_x[0:CE, 1, :], a["L0_xattn_Wk"]),
                  (w_x[0:CE, 2, :], a["L0_xattn_Wv"]), (w1[:], a["L0_xattn_W1"]),
                  (w2[:], a["L0_xattn_W2"].rearrange("(k p) e -> p k e", p=P))]
        loads += [(cols[:, 0:1], column("L0_xattn_bq")), (cols[:, 1:2], column("L0_xattn_bk")),
                  (cols[:, 2:3], column("L0_xattn_bv")), (cols[:, 3:4], column("L0_xattn_b1")),
                  (cols[:, 4:5], column("L0_xattn_b1", P)),
                  (b2[:], a["L0_xattn_b2"].rearrange("(o e) -> o e", o=1).broadcast_to([P, E])),
                  (w_r[:], a["L0_ffn_w_router"])]
        assert len(loads) == N_LOADS
        for dst, src in loads:
            sp.dma_start(dst, src).then_inc(weights_loaded, 16)
        load_tile(0, 0)
        load_tile(1, 1)
        gu = w_gu[:].rearrange("p (e k h) -> p e k h", e=EXPERTS, k=2)
        sp.dma_start(gu[:, :, 0, :], a["L0_ffn_wg"].rearrange("x p h -> p x h")).then_inc(gate_up_loaded, 16)
        sp.dma_start(gu[:, :, 1, :], a["L0_ffn_wu"].rearrange("x p h -> p x h")).then_inc(gate_up_loaded, 16)
        wd_v = w_d[:].rearrange("p c (x e) -> p c x e", x=EXPERTS)
        for c in range(HC):
            sp.dma_start(wd_v[:, c], a["L0_ffn_wd"][:, c * P:(c + 1) * P, :].rearrange("x p e -> p x e"))\
              .then_inc(gate_up_loaded, 16)

        def spread_keys(i, j):
            r = j % 2
            if kind_of(j) == 2:
                sp.wait_ge(rotated, 2 * tile_no(i, j) + 1)
            else:
                u = source(i, j, "k")
                sp.wait_ge(ring_drained[u.bank], u.drained())

            for h in range(HEADS):
                sp.dma_start(kbd[r][D * h:D * h + D, h, :], kS[r][D * h:D * h + D, :]).then_inc(kbd_loaded[r], 16)

        def export(i, j):
            t = tile_no(i, j)
            wait(sp, export_ready, t + 1)
            sl = slice(t * SUB, t * SUB + SUB) if isinstance(t, int) else bass.ds(t * SUB, SUB)
            sp.dma_start(hn_dram[:, sl, :], hn[:]).then_inc(exported, 16)
            sp.dma_start(base_dram[:, sl, :], base[:]).then_inc(exported, 16)
            sp.dma_start(lg_all[:, sl, :], lgs[:]).then_inc(exported, 16)

        sp.wait_ge(pool_const, 1)
        sp.sem_inc(exported, EXPORT)
        sp.dma_start(xs_dram.rearrange("(b p) e -> p b e", p=P),
                     zrow[:].unsqueeze(1).broadcast_to([P, BLOCKS, E])).then_inc(xs_cleared, 16)
        spread_keys(0, 0)

        def slot(i, j):
            if j in (3, 4) and not (isinstance(i, int) and i == ITERS - 1):
                u = named_use(i, j - 2, "q")
                sp.wait_ge(ring_drained[u.bank], u.drained())
                load_tile(2 * i + 2 + (j - 3), j - 3)
            if not is_last(i, j):
                spread_keys(i, j + 1)
            if j in (5, 6):
                export(i, j - 1)

        walk(sp, slot)
        export(ITERS - 1, JOBS - 1)
        sp.wait_ge(exported, EXPORT * (TILES + 1))
        sp.wait_ge(scores_ready, TILES * 3 * SUB)
        sp.dma_start(hn_all, hn_dram).then_inc(hn_loaded, 16)
        experts_sp(sp)

    @block.tensor
    def _(pe):
        mm = nc.tensor.matmul

        def setup():
            pe.wait_ge(weights_loaded, 16 * N_LOADS)
            for k in range(4):
                last = nc.tensor.transpose(ps_g[:, k * P:(k + 1) * P], raw[:, k, :], ident)
            last.then_inc(setup_filled, 1)
            pe.wait_ge(const_ready, 1)
            pe.wait_ge(setup_drained, 1)
            for k in range(2):
                last = nc.tensor.transpose(ps_g[:, k * P:(k + 1) * P], w_f[:, k, :], ident)
            last.then_inc(setup_filled, 1)
            pe.wait_ge(setup_drained, 2)
            for k in range(2):
                last = mm(ps_g[:, k * P:(k + 1) * P], rawT[:, k, :], const[:, C_ROT:C_ROT + P],
                          start=True, stop=True)
            last.then_inc(setup_filled, 1)
            pe.wait_ge(setup_drained, 3)

        def transposes(ps_g, src, rows=P):
            for s in range(SUB):
                last = nc.tensor.transpose(ps_g[0:rows, s * P:(s + 1) * P], src[:, s, :], ident)
            return last

        def values(ps_g, src, w, half):
            for b in range(SUB):
                col = (half * SUB + b) * SEQ
                for q in range(2):
                    last = mm(ps_g[SEQ * q:SEQ * q + SEQ, b * P:(b + 1) * P], src[:, col:col + SEQ], w,
                              start=True, stop=True)
            return last

        def copied(uses, u=None):
            need = {}
            for x in uses:
                need[x.bank] = max(need.get(x.bank, 0), x.c // 2 + 1)
            if u is not None:
                need[u.bank] = max(need.get(u.bank, 0), u.c // 2)
            i = (u or uses[0]).i
            for bank, c in sorted(need.items()):
                wait(pe, ring_drained[bank], i * (N_ITER // 2) + c)

        def use(u, name, i, j):
            kind = kind_of(j)
            r = j % 2
            if name in ON_DVE_ONLY:
                return
            if name == "xT":
                pe.wait_ge(normed, norm_index(i, j, "pre"))
            elif name == "hT":
                pe.wait_ge(normed, norm_index(i, j, "post"))
            elif name == "cT":
                pe.wait_ge(ctx_loaded[r], 16 * (tile_turn(i, j) + 1))
            if name == "oT":
                needs = [att_use(i, j, SUB - 1)]
            elif name in ("xT", "hT", "cT"):
                needs = []
            else:
                names = {"wo": ("oT",), "h0": ("oT",), "h1": ("oT",), "ff": ("h0", "h1"), "lg": ("hT",)}
                names = names.get(name, ("cT",) if kind == 1 and name != "q" else ("xT",))
                needs = [source(i, j, x) for x in names]
            copied(needs, u)
            ps_g = ring[u.bank]
            if name == "xT":
                last = transposes(ps_g, xh)
            elif name == "cT":
                last = transposes(ps_g, cin[r], CE)
            elif name == "oT":
                last = transposes(ps_g, att[r])
            elif name == "hT":
                last = transposes(ps_g, hn)
            elif name == "wo":
                w = w_a[:, 3, :] if kind == 0 else w_f[:, 5, :]
                for s in range(SUB):
                    last = mm(ps_g[:, s * P:(s + 1) * P], oT[:, s * P:(s + 1) * P], w, start=True, stop=True)
            elif name in ("h0", "h1"):
                k = int(name[1])
                last = mm(ps_g[:], w1[:, k * P:(k + 1) * P], oT[:], start=True, stop=True)
            elif name == "ff":
                for s in range(SUB):
                    for k in range(2):
                        last = mm(ps_g[:, s * P:(s + 1) * P], h1T[:, k, s * P:(s + 1) * P], w2[:, k, :],
                                  start=(k == 0), stop=(k == 1))
            elif name == "lg":
                for s in range(SUB):
                    last = mm(ps_g[:, s * EXPERTS:(s + 1) * EXPERTS], hT[:, s * P:(s + 1) * P], w_r[:],
                              start=True, stop=True)
            elif name in ("v0", "v1"):
                src, w = {0: (xT, w_a[:, 2, :]), 1: (cT, w_x[0:CE, 2, :]), 2: (xT, w_f[:, 2, :])}[kind]
                last = values(ps_g, src, w, int(name[1]))
            else:
                w = {(0, "q"): w_a[:, 0, :], (0, "k"): w_a[:, 1, :], (1, "q"): w_x[:, 0, :],
                     (1, "k"): w_x[0:CE, 1, :], (2, "q"): w_f[:, 0, :], (2, "k"): w_f[:, 1, :],
                     (2, "qr"): w_f[:, 3, :], (2, "kr"): w_f[:, 4, :]}[kind, name]
                last = mm(ps_g[:], w, (cT if kind == 1 and name == "k" else xT)[:], start=True, stop=True)
            last.then_inc(ring_filled, 1)

        def scores(i, j, p):
            n = pair_no(i, j, p)
            r, half = j % 2, p % 2
            if p == 0:
                pe.wait_ge(kbd_loaded[r], 16 * HEADS * (job_turn(i, j) + 1))
                if kind_of(j) == 2:
                    pe.wait_ge(rotated, 2 * tile_no(i, j) + 2)
                else:
                    copied([source(i, j, "q")])
            wait(pe, centered, n - 1)
            causal = kind_of(j) != 1
            for g in range(2):
                for b in range(2):
                    rows = slice(SEQ * b, SEQ * b + SEQ)
                    o = ps_s[half][rows, 8 * g:8 * g + 8, :]
                    if causal:
                        mm(o, identb[:, rows], maskb[:].unsqueeze(1).broadcast_to([P, 8, SEQ]),
                           start=True, stop=False)
                for b in range(2):
                    rows = slice(SEQ * b, SEQ * b + SEQ)
                    o = ps_s[half][rows, 8 * g:8 * g + 8, :]
                    tok = (2 * p + b) * SEQ
                    last = mm(o, qT[r][:, tok:tok + SEQ], kbd[r][:, 8 * g:8 * g + 8, tok:tok + SEQ],
                              start=not causal, stop=True)
            last.then_inc(scores_ready, 1)

        def transpose_probs(i, j, p):
            n = pair_no(i, j, p)
            pe.wait_ge(probs_ready, n + 1)
            flat = probs[p % 2][:].rearrange("p h k -> p (h k)")
            for g in range(2):
                wait(pe, probsT_copied, 2 * n + g - 1)
                for k in range(4):
                    c = (4 * g + k) * P
                    last = nc.tensor.transpose(ps_t[g][:, k, :], flat[:, c:c + P], ident)
                last.then_inc(probsT_filled, 1)

        def attend(i, j, p):
            n = pair_no(i, j, p)
            r = j % 2
            u = att_use(i, j, p)
            pe.wait_ge(probsT_copied, 2 * n + 2)
            copied([source(i, j, x) for x in ("v0", "v1")] if p == 0 and j != 1 else [], u)
            o = ring[u.bank][:, 0:2 * (VW + PAD)].rearrange("p (b c) -> p b c", b=2)
            for k in range(HEADS // 2):
                c = 2 * (D + 1) * k
                v = vbd[r][:, 2 * p * VW + c:2 * p * VW + c + 2 * VW].rearrange("p (b c) -> p b c", b=2)
                last = mm(o[:, :, c:c + PAD], probsT[p % 2][:, k, :], v[:, :, 0:PAD], start=True, stop=True)
            last.then_inc(ring_filled, 1)

        setup()
        for k, name in enumerate(PRE0):
            use(Use(0, k), name, 0, 0)
        scores(0, 0, 0)

        def slot(i, j):
            for p in range(SUB):
                if p < SUB - 1:
                    scores(i, j, p + 1)
                for u, name, jj in steps_at(i, j, p, 0):
                    use(u, name, i, jj)
                if p > 0:
                    attend(i, j, p - 1)
                transpose_probs(i, j, p)
                for place in (1, 2):
                    for u, name, jj in steps_at(i, j, p, place):
                        use(u, name, i, jj)
            if j in SCORES_FIRST and not is_last(i, j):
                scores(i, j + 1, 0)
            attend(i, j, SUB - 1)
            if j not in SCORES_FIRST and not is_last(i, j):
                scores(i, j + 1, 0)

        walk(pe, slot)
        for name in TAIL:
            if name not in ON_DVE_ONLY:
                use(tail_use(name), name, ITERS - 1, JOBS - 1)

        pe.wait_ge(sel_ready, 1)
        for name in ("hT", "lg"):
            u = tail_use(name)
            pe.wait_ge(ring_drained[u.bank], u.drained())
        mm(ps_g[:, 0:SUBS * EXPERTS], const[:, C_LOW:C_LOW + P], sel[:], start=True, stop=True)
        mm(ps_g[:, 256:512], ones[:], sel[:], start=True, stop=True).then_inc(ranks_ready, 1)

        experts_pe(pe)

    @block.scalar
    def _(act):
        def exps(i, j, p):
            n = pair_no(i, j, p)
            act.wait_ge(centered, n + 1)
            nc.scalar.activation(probs[p % 2][:], probs[p % 2][:], ACT.Exp, scale=SCALE).then_inc(probs_ready, 1)

        def copy_probsT(i, j, p):
            n = pair_no(i, j, p)
            if not (isinstance(n, int) and n < 2):
                act.wait_ge(ring_filled, att_before(i, j, p).filled())
            for g in range(2):
                act.wait_ge(probsT_filled, 2 * n + g + 1)
                nc.scalar.activation(probsT[p % 2][:, 4 * g:4 * g + 4, :], ps_t[g][:], ACT.Copy)\
                  .then_inc(probsT_copied, 1)

        def use(u, name, i, j):
            kind, r = kind_of(j), j % 2
            if name in ("wo", "ff", "lg", "v0", "v1", "qr", "kr") + ON_DVE_ONLY or (kind == 2 and name in ("q", "k")):
                return
            if name == "k":
                wait(act, kbd_loaded[r], 16 * HEADS * job_turn(i, j))
            act.wait_ge(ring_filled, u.filled())
            ps_g = ring[u.bank]
            if name == "xT":
                ins = nc.scalar.activation(xT[:], ps_g[:], ACT.Copy)
            elif name == "cT":
                ins = nc.scalar.activation(cT[:], ps_g[0:CE, :], ACT.Copy)
            elif name == "oT" and kind == 1:
                ins = nc.scalar.activation(oT[:], ps_g[:], ACT.Identity, bias=cols[:, 2:3])
            elif name == "oT":
                ins = nc.scalar.activation(oT[:], ps_g[:], ACT.Copy)
            elif name == "hT":
                ins = nc.scalar.activation(hT[:], ps_g[:], ACT.Copy)
            elif name in ("h0", "h1"):
                k = int(name[1])
                ins = nc.scalar.activation(h1T[:, k, :], ps_g[:], ACT.Relu, bias=cols[:, 3 + k:4 + k])
            elif name == "q":
                ins = (nc.scalar.activation(qT[r][:], ps_g[:], ACT.Identity, bias=cols[:, 0:1]) if kind == 1
                       else nc.scalar.activation(qT[r][:], ps_g[:], ACT.Copy))
            elif name == "k":
                ins = (nc.scalar.activation(kS[r][:], ps_g[:], ACT.Identity, bias=cols[:, 1:2]) if kind == 1
                       else nc.scalar.activation(kS[r][:], ps_g[:], ACT.Copy))
            ins.then_inc(ring_drained[u.bank], 1)

        act.wait_ge(weights_loaded, 16 * N_LOADS)
        act.wait_ge(setup_filled, 1)
        nc.scalar.activation(w_a[:].rearrange("p a b -> p (a b)"), ps_g[:], ACT.Copy).then_inc(setup_drained, 1)
        act.wait_ge(setup_filled, 2)
        nc.scalar.activation(rawT[:].rearrange("p a b -> p (a b)"), ps_g[:, 0:2 * P], ACT.Copy)\
          .then_inc(setup_drained, 1)
        act.wait_ge(setup_filled, 3)
        nc.scalar.activation(w_f[:, 3:5, :].rearrange("p a b -> p (a b)"), ps_g[:, 0:2 * P], ACT.Copy)\
          .then_inc(setup_drained, 1)
        for k, name in enumerate(PRE0):
            use(Use(0, k), name, 0, 0)

        def slot(i, j):
            for p in range(SUB):
                exps(i, j, p)
                for u, name, jj in steps_at(i, j, p, 0):
                    use(u, name, i, jj)
                copy_probsT(i, j, p)
                for place in (1, 2):
                    for u, name, jj in steps_at(i, j, p, place):
                        use(u, name, i, jj)

        walk(act, slot)
        for name in TAIL:
            use(None if name in ON_DVE_ONLY else tail_use(name), name, ITERS - 1, JOBS - 1)
        act.wait_ge(gap_ready, 1)
        nc.scalar.activation(w1st[:], gap[:], ACT.Exp).then_inc(weight_ready, 1)
        experts_act(act)

    @block.vector
    def _(dve):
        V = nc.vector

        def softmax_shift(i, j, p):
            n = pair_no(i, j, p)
            dve.wait_ge(scores_ready, n + 1)
            V.reduce_max(rmax[p % 2][:], ps_s[p % 2][:], AX.X).then_inc(rmax_ready, 1)
            wait(dve, probsT_filled, 2 * (n - 1))
            dve.wait_ge(rmax_ready, n + 1)
            V.tensor_tensor(probs[p % 2][:], ps_s[p % 2][:],
                            rmax[p % 2][:].unsqueeze(2).broadcast_to([P, HEADS, SEQ]), ALU.subtract)\
             .then_inc(centered, 1)

        def normalise(i, j, p):
            n, r, u = pair_no(i, j, p), j % 2, att_use(i, j, p)
            dve.wait_ge(ring_filled, u.filled())
            halves = []
            for b in range(2):
                rows = slice(SEQ * b, SEQ * b + SEQ)
                at = b * (VW + PAD)
                o = ring[u.bank][rows, at:at + VW].rearrange("p (h c) -> p h c", h=HEADS)
                halves.append((rows, o))
                last = V.reciprocal(rden[p % 2][rows, :], o[:, :, D])
            last.then_inc(rden_ready, 1)
            dve.wait_ge(rden_ready, n + 1)
            for rows, o in halves:
                last = V.tensor_tensor(att[r][rows, p, :].rearrange("p (h d) -> p h d", h=HEADS), o[:, :, 0:D],
                                       rden[p % 2][rows, :].unsqueeze(2).broadcast_to([SEQ, HEADS, D]), ALU.mult)
            last.then_inc(ring_drained[u.bank], 1)

        def stats_of(m, src):
            for s in range(SUB):
                last = V.bn_stats(stats[:, s, :], src[:, s, :])
            last.then_inc(stats_ready, 1)
            wait_plain(stats_ready, m)
            for s in range(SUB):
                last = V.bn_aggr(mv[:, s, :], stats[:, s, :])
            last.then_inc(mv_ready, 1)

        def apply(factors_at, src, pieces):
            dve.wait_ge(pool_step, factors_at)
            for dst, factor, centre in pieces:
                for s in range(SUB):
                    if centre:
                        last = V.tensor_scalar(dst[:, s, :], src[:, s, :], mv[:, s, 0:1], factor[:, s:s + 1],
                                               ALU.subtract, ALU.mult)
                    else:
                        last = V.tensor_scalar(dst[:, s, :], src[:, s, :], factor[:, s:s + 1], None, ALU.mult)
            last.then_inc(normed, 1)

        def wait_plain(sem_, value):
            dve.wait_ge(sem_, value)
            V.tensor_copy(turn[:], small[:, 0:1])

        def pre_stats(i, j):
            kind, r = kind_of(j), j % 2
            if kind == 0:
                dve.wait_ge(x_loaded[r], 16 * (tile_turn(i, j) + 1))
            else:
                u = source(i, j - 2, "wo" if kind == 1 else "ff")
                dve.wait_ge(ring_drained[u.bank], u.drained())
            stats_of(norm_index(i, j, "pre"), (xin if kind == 0 else xres)[r])

        def pre_apply(i, j):
            kind, r = kind_of(j), j % 2
            if isinstance(i, int) and i == 0 and j <= 1:
                at = 2 * (j + 1)
            else:
                at = steps_before(i, j - 1) + (5 if kind == 2 else 2)
            src = (xin if kind == 0 else xres)[r]
            apply(at, src, ((fres[r], rstd, True), (xh, rboth, True)) if kind == 2 else ((xh, rstd, True),))

        def values_out(u, i, j, half):
            r = j % 2
            dve.wait_ge(ring_filled, u.filled())
            ps_g = ring[u.bank]
            v = vbd[r][:, 4 * half * VW:4 * (half + 1) * VW].rearrange("p (b k c) -> p b k c", b=4, k=HEADS // 2)
            ps = ps_g[:].rearrange("p (b k c) -> p b k c", b=4, k=HEADS // 2)
            for q in range(2):
                rows = slice(SEQ * q, SEQ * q + SEQ)
                last = V.tensor_copy(v[rows, :, :, q * (D + 1):q * (D + 1) + D], ps[rows, :, :, q * D:q * D + D])
            last.then_inc(ring_drained[u.bank], 1)

        def table(c):
            return const[:, c:c + SEQ].unsqueeze(1).broadcast_to([P, 2 * SUB, SEQ])

        def by_seq(ap):
            return ap.rearrange("p (b q) -> p b q", q=SEQ)

        def use(u, name, i, j):
            kind, r = kind_of(j), j % 2
            if name == "st":
                pre_stats(i, j)
            elif name == "ap":
                pre_apply(i, j)
            elif name == "st2":
                wo = source(i, j, "wo")
                dve.wait_ge(ring_drained[wo.bank], wo.drained())
                stats_of(norm_index(i, j, "post"), hres)
            elif name == "ap2":
                dve.wait_ge(exported, EXPORT * (tile_no(i, j) + 1))
                apply(rms_at(i, j), hres, ((hn, rstd, False),))
            elif name in ("v0", "v1"):
                values_out(u, i, j, int(name[1]))
            elif name in ("wo", "ff", "lg", "qr", "kr") or (kind == 2 and name in ("q", "k")):
                if name == "ff":
                    dve.wait_ge(b2_added, tile_no(i, j) + 1)
                dve.wait_ge(ring_filled, u.filled())
                ps_g = ring[u.bank]
                drained = ring_drained[u.bank]
                by_sub = ps_g[:].rearrange("p (s e) -> p s e", s=SUB)
                if name == "wo" and kind == 0:
                    V.tensor_tensor(xres[r][:], by_sub, xin[r][:], ALU.add).then_inc(drained, 1)
                elif name == "ff":
                    V.tensor_tensor(xres[r][:], by_sub, xres[r][:], ALU.add).then_inc(drained, 1)
                elif name == "wo":
                    V.tensor_tensor(hres[:], by_sub, fres[r][:], ALU.add).then_inc(drained, 1)
                elif name == "lg":
                    V.tensor_copy(lgs[:].rearrange("p s e -> p (s e)"), ps_g[:, 0:SUB * EXPERTS]).then_inc(drained, 1)
                    dve.wait_ge(drained, u.drained())
                    V.tensor_tensor(base[:], hres[:], xres[r][:], ALU.add).then_inc(export_ready, 1)
                elif name in ("q", "k"):
                    V.tensor_tensor(by_seq(rope[:, 0, :]), by_seq(ps_g[:]), table(C_COS), ALU.mult)\
                     .then_inc(drained, 1)
                else:
                    V.tensor_tensor(by_seq(rope[:, 1, :]), by_seq(ps_g[:]), table(C_SIN), ALU.mult)\
                     .then_inc(drained, 1)
                    dve.wait_ge(drained, u.drained())
                    if name == "kr":
                        wait(dve, kbd_loaded[r], 16 * HEADS * job_turn(i, j))
                    dst = (qT if name == "qr" else kS)[r]
                    V.tensor_tensor(dst[:], rope[:, 0, :], rope[:, 1, :], ALU.add).then_inc(rotated, 1)

        def rms_at(i, j):
            if isinstance(i, int) and i == ITERS - 1:
                return steps_before(i, JOBS - 1) + (4 if j == JOBS - 2 else 8)
            return steps_before(i, j + 1) + 6

        dve.wait_ge(weights_loaded, 16 * N_LOADS)
        V.tensor_copy(identb[:], ident)
        V.tensor_copy(maskb[:], const[:, C_MASK:C_MASK + SEQ])
        for k in range(2):
            V.tensor_scalar(w_f[:, k, :], rawf[:, k, :], cols[:, 5:6], None, ALU.mult)
        V.tensor_scalar(w_f[:, 2, :], w_f[:, 2, :], cols[:, 5:6], None, ALU.mult)
        V.tensor_scalar(w_r[:], w_r[:], cols[:, 6:7], None, ALU.mult).then_inc(const_ready, 1)
        dve.wait_ge(pool_const, 1)
        pre_stats(0, 0)
        pre_apply(0, 0)
        for k, name in enumerate(PRE0):
            use(Use(0, k), name, 0, 0)
        pre_stats(0, 1)
        pre_apply(0, 1)

        def slot(i, j):
            for p in range(SUB):
                softmax_shift(i, j, p)
                for u, name, jj in steps_at(i, j, p, 0):
                    use(u, name, i, jj)
                if p > 0:
                    normalise(i, j, p - 1)
                for place in (1, 2):
                    for u, name, jj in steps_at(i, j, p, place):
                        use(u, name, i, jj)
            normalise(i, j, SUB - 1)

        walk(dve, slot)
        for name in TAIL:
            use(None if name in ON_DVE_ONLY else tail_use(name), name, ITERS - 1, JOBS - 1)
        route_dve(dve)
        experts_dve(dve)
        combine_dve(dve)

    @block.gpsimd
    def _(pool):
        G = nc.gpsimd
        var, mean = mv[:, :, 1], mv[:, :, 0]
        eps5, eps6, neg_half = small[:, 0:4], small[:, 4:8], small[:, 8:12]
        for r in range(2):
            G.memset(kbd[r][:], 0.0)
            G.memset(vbd[r][:], 0.0)
        G.memset(zrow[:], 0.0)
        G.memset(small[:, 0:4], 1e-5)
        G.memset(small[:, 4:8], 1e-6)
        G.memset(ones[:], 1.0)
        G.memset(small[:, 8:12], -0.5).then_inc(pool_clear, 1)
        pool.wait_ge(pool_clear, 1)
        for r in range(2):
            v = vbd[r][:, 0:2 * SUB * VW].rearrange("p (b k c) -> p b k c", b=2 * SUB, k=HEADS // 2)
            for q in range(2):
                rows = slice(SEQ * q, SEQ * q + SEQ)
                last = G.memset(v[rows, :, :, q * (D + 1) + D:q * (D + 1) + D + 1], 1.0)
        last.then_inc(pool_const, 1)

        def chain(k0):
            count = [k0]

            def step(out_, x, y, op):
                wait(pool, pool_step, count[0])
                G.tensor_tensor(out_, x, y, op).then_inc(pool_step, 1)
                count[0] = count[0] + 1
            return step

        def layer_norm(k0, m, both):
            step = chain(k0)
            pool.wait_ge(mv_ready, m)
            step(pt[:, 0, :], var, eps5, ALU.add)
            step(rstd[:], pt[:, 0, :], neg_half, ALU.pow)
            if both:
                step(pt[:, 1, :], pt[:, 0, :], eps6, ALU.mult)
                step(pt[:, 2, :], pt[:, 1, :], var, ALU.add)
                step(rboth[:], pt[:, 2, :], neg_half, ALU.pow)

        def rms(k0, m):
            step = chain(k0)
            pool.wait_ge(mv_ready, m)
            step(pt[:, 0, :], mean, mean, ALU.mult)
            step(pt[:, 1, :], pt[:, 0, :], var, ALU.add)
            step(pt[:, 2, :], pt[:, 1, :], eps6, ALU.add)
            step(rstd[:], pt[:, 2, :], neg_half, ALU.pow)

        layer_norm(0, 1, False)
        layer_norm(2, 2, False)
        pool.wait_ge(gate_up_loaded, 16 * (2 + HC))
        G.tensor_scalar(w_gu[:], w_gu[:], cols[:, 6:7], None, ALU.mult).then_inc(gate_up_ready, 1)

        def slot(i, j):
            if j == 0:
                return
            k0, m = steps_before(i, j), norms_before(i, j) + 1
            if j in (1, 2):
                layer_norm(k0, m, False)
                pool.wait_ge(normed, m)
                G.tensor_tensor(xres[j - 1][:], xres[j - 1][:], b2[:].unsqueeze(1).broadcast_to([P, SUB, E]),
                                ALU.add).then_inc(b2_added, 1)
            elif j in (3, 4):
                layer_norm(k0, m, True)
            elif is_last(i, j):
                rms(k0, m)
            else:
                layer_norm(k0, m, False)
                rms(k0 + 2, m + 1)

        walk(pool, slot)
        rms(steps_before(ITERS - 1, JOBS - 1) + 4, norms_before(ITERS - 1, JOBS - 1) + 2)
        dispatch_pool(pool)
        gather_pool(pool)


INPUTS = ["x", "ctx_768", "L0_attn_in_proj_weight", "L0_attn_out_proj_weight",
          "L0_xattn_Wq", "L0_xattn_bq", "L0_xattn_Wk", "L0_xattn_bk", "L0_xattn_Wv", "L0_xattn_bv",
          "L0_xattn_W1", "L0_xattn_b1", "L0_xattn_W2", "L0_xattn_b2",
          "L0_ffn_wq", "L0_ffn_wk", "L0_ffn_wv", "L0_ffn_wo", "L0_ffn_w_router",
          "L0_ffn_wg", "L0_ffn_wu", "L0_ffn_wd", "L0_ffn_g1", "L0_ffn_g2"]


def kernel(**inputs):
    import numpy as _np
    import concourse.bacc as _bacc
    from concourse import mybir as _mybir
    from concourse.bass_utils import run_bass_kernel_spmd as _run

    nc = _bacc.Bacc("TRN2", target_bir_lowering=False, num_devices=1)
    arrays = {f"in_{n}": _np.ascontiguousarray(inputs[n]) for n in INPUTS}
    arrays["in_const"] = constants()
    args = {n[3:]: nc.dram_tensor(n, v.shape, _mybir.dt.from_np(v.dtype), kind="ExternalInput").ap()
            for n, v in arrays.items()}
    out = nc.dram_tensor("out", (BATCH, SEQ, E), F32, kind="ExternalOutput").ap()
    build(nc, args, out)
    r = _run(nc, [arrays], core_ids=[0])
    return r.results[0]["out"]
```

```python
from contextlib import ExitStack

import numpy as np

import concourse.bass as bass
from concourse import mybir

F32 = mybir.dt.float32
BF16 = mybir.dt.bfloat16
I32 = mybir.dt.int32
ALU = mybir.AluOpType
ACT = mybir.ActivationFunctionType
AX = mybir.AxisListType

P = 128
BATCH, SEQ, E, CE = 64, 64, 128, 96
HEADS, D = 16, 8
TOKENS = BATCH * SEQ
TILE, SUB = 512, 4
TILES = TOKENS // TILE
SUBS = TOKENS // P
EXPERTS, HIDDEN = 8, 384
HC = HIDDEN // P
FF = 256
W_GATE, W_UP, W_DOWN = 0, HIDDEN, 2 * HIDDEN
W_ALL = W_DOWN + HC * E
BLOCKS = (2 * TOKENS + EXPERTS * (P - 1)) // P + 1
CHOICES = 2 * SUBS
CHUNK = 16
UNROLL = 8
TURNS = BLOCKS // UNROLL
assert BLOCKS == TURNS * UNROLL
SCALE = float(D) ** -0.5
VW = HEADS * (D + 1)
PAD = 48

HEADS_ACT = 6
JOBS = 6
ITERS = TILES // 2

C_ID, C_ROT, C_LOW, C_COS, C_SIN, C_MASK, C_IOTA, C_BLK = 0, 128, 256, 384, 448, 512, 576, 584
C_COL = C_BLK + BLOCKS
C_SPARE = C_COL + 1
C_WIDE = C_SPARE + BLOCKS
C_HEAD = C_WIDE + P
C_ALL = C_HEAD + HEADS
N_FIRST_LOADS, N_LOADS = 3, 18
EXPORT = 2 * 16


def constants():
    c = np.zeros((P, C_ALL), np.float32)
    c[:, C_ID:C_ID + P] = np.eye(P)
    half = D // 2
    for o in range(P):
        d = o % D
        if d < half:
            c[o + half, C_ROT + o] = -1.0
        else:
            c[o - half, C_ROT + o] = 1.0
    c[:, C_LOW:C_LOW + P] = np.triu(np.ones((P, P)), 1)
    inv = 1.0 / 10000.0 ** (np.arange(0, D, 2, dtype=np.float32) / D)
    freqs = np.einsum("i,j->ij", np.arange(SEQ, dtype=np.float32), inv)
    emb = np.concatenate([freqs, freqs], axis=-1)
    c[:, C_COS:C_COS + SEQ] = np.tile(np.cos(emb).T, (HEADS, 1))
    c[:, C_SIN:C_SIN + SEQ] = np.tile(np.sin(emb).T, (HEADS, 1))
    q, k = np.arange(P)[:, None] % SEQ, np.arange(SEQ)[None, :]
    c[:, C_MASK:C_MASK + SEQ] = np.where(k > q, -1e30, 0.0)
    c[:, C_IOTA:C_IOTA + EXPERTS] = np.arange(EXPERTS)
    c[:, C_BLK:C_BLK + BLOCKS] = np.arange(BLOCKS)
    c[:, C_COL] = np.arange(P)
    c[:, C_SPARE:C_SPARE + BLOCKS] = 2 * TOKENS + P * np.arange(BLOCKS)[None, :] + np.arange(P)[:, None]
    c[:, C_WIDE:C_WIDE + P] = np.arange(P)
    c[:, C_HEAD:C_HEAD + HEADS] = np.arange(P)[:, None] // D == np.arange(HEADS)[None, :]
    return c


SLOT_FIRST = ((("xT",), ("k",), ()),
              (("q",), ("v0",), ()),
              (("v1",), (), ()),
              ((), (), ()))
SLOT_A = ((("cT", "oT"), ("k",), ("wo", "st")),
          (("v0", "ap"), (), ("v1",)),
          ((), ("xT", "q"), ()),
          ((), (), ()))
SLOT_B = ((("oT",), (), ("h0", "h1")),
          (("ff", "st"), (), ("ap",)),
          ((), ("xT", "k"), ("kr",)),
          (("ks",), ("q", "qr"), ("v0", "v1")))
SLOT_C = ((("st", "oT"), (), ("ap",)),
          (("wo", "xT", "st2"), ("q", "k"), ()),
          (("ap2", "v0"), ("hT",), ()),
          (("v1",), ("lg",), ()))
SCORES_FIRST = (0, 1, 2, 5, 6)
SHIFT_FIRST = (1, 2, 5, 6)
SHIFT_AT = ((1, 1, 1),
            (3, 3, 2),
            (3, 3, 2),
            (1, 1, 2),
            (1, 1, 2),
            (3, 3, 3),
            (3, 3, 3))
SLOTS = {0: SLOT_FIRST, 1: SLOT_A, 2: SLOT_A, 3: SLOT_B, 4: SLOT_B, 5: SLOT_C, 6: SLOT_C}
PRE0 = ("xT", "k", "q", "v0", "v1")
POST = {0: ("oT", "wo"), 1: ("oT", "h0", "h1", "ff"), 2: ("oT", "wo", "st2", "ap2", "hT", "lg")}
TAIL = ("oT", "wo", "st2", "ap2", "hT", "lg")
NOT_ON_PE = ("st", "ap", "st2", "ap2", "ks")
DVE_DRAINS = ("wo", "ff", "lg", "v0", "v1", "qr", "kr")


def ring_uses(j, last=False):
    post = () if j == 0 else POST[((j - 1) % JOBS) // 2]
    for p in range(SUB):
        for place in range(3):
            if place == 1 and p > 0:
                yield p, place, "att"
            for name in SLOTS[j][p][place]:
                if name in post or not last:
                    yield p, place, name
    yield SUB - 1, 3, "att"


def count(uses):
    return sum(name not in NOT_ON_PE for _, _, name in uses)


N_SLOT = {j: count(ring_uses(j)) for j in SLOTS}
N_ITER = sum(N_SLOT[j] for j in range(1, JOBS + 1))
N_FIRST = len(PRE0) + N_SLOT[0]
assert N_ITER % 2 == 0
NORMS = {1: 1, 2: 1, 3: 1, 4: 1, 5: 2, 6: 2}
NORMS_ITER, NORMS_FIRST = sum(NORMS.values()), 2


class Use:

    def __init__(self, i, c):
        self.i, self.c, self.bank = i, c, c % 2

    def filled(self):
        return self.i * N_ITER + (self.c + 1)

    def drained(self):
        return self.i * (N_ITER // 2) + (self.c // 2 + 1)


def use_of(i, j, p, place, name, last=False):
    base = len(PRE0) if j == 0 else N_FIRST + sum(N_SLOT[x] for x in range(1, j))
    n = 0
    for step in ring_uses(j, last):
        if step == (p, place, name):
            return Use(i, base + n)
        n += step[2] not in NOT_ON_PE
    raise ValueError(name)


def named_use(i, j, name, last=False):
    p, place, _ = next(x for x in ring_uses(j, last) if x[2] == name)
    return use_of(i, j, p, place, name, last)


def norms_before(i, j):
    return NORMS_FIRST + i * NORMS_ITER + sum(NORMS[x] for x in range(1, j))


def kind_of(j):
    return (j % JOBS) // 2


def wait(eng, sem, value):
    if not (isinstance(value, int) and value <= 0):
        eng.wait_ge(sem, value)


def build(nc, a, out):
    with ExitStack() as ctx:
        _build(nc, ctx, a, out)


def _build(nc, ctx, a, out):
    def sb(name, shape, dt=F32):
        return ctx.enter_context(nc.sbuf_tensor(name, shape, dt))

    def sem(name):
        return ctx.enter_context(nc.semaphore(name))

    const = sb("const", [P, C_ALL])
    ident = const[:, C_ID:C_ID + P]
    identb = sb("identb", [P, P], BF16)
    maskb = sb("maskb", [P, SEQ], BF16)
    w_given = sb("w_given", [P, 4, P])
    w_given_f = sb("w_given_f", [P, 2, P])
    w_turned = sb("w_turned", [P, 2, P])
    w_a = sb("w_a", [P, 4, P])
    w_x = sb("w_x", [P, 3, P])
    w1 = sb("w1", [P, FF])
    w2 = sb("w2", [P, 2, P])
    w_f = sb("w_f", [P, 6, P])
    w_r = sb("w_r", [P, EXPERTS])
    cols = sb("cols", [P, 8])
    b2 = sb("b2", [P, E])
    w_exp = sb("w_exp", [P, EXPERTS, W_ALL])
    small = sb("small", [P, 12])
    xin = [sb(f"xin{r}", [P, SUB, E]) for r in range(2)]
    cin = [sb(f"cin{r}", [P, SUB, CE]) for r in range(2)]
    xres = [sb(f"xres{r}", [P, SUB, E]) for r in range(2)]
    fres = [sb(f"fres{r}", [P, SUB, E]) for r in range(2)]
    xh = sb("xh", [P, SUB, E])
    hn = sb("hn", [P, SUB, E])
    hres = sb("hres", [P, SUB, E])
    base = sb("base", [P, SUB, E])
    stats = sb("stats", [P, SUB, 6])
    mv = sb("mv", [P, SUB, 2])
    rstd = sb("rstd", [P, SUB])
    rboth = sb("rboth", [P, SUB])
    pt = sb("pt", [P, 4, SUB])
    xT = sb("xT", [P, TILE])
    cT = sb("cT", [CE, TILE])
    oT = sb("oT", [P, TILE])
    h1T = sb("h1T", [P, 2, TILE])
    hT = sb("hT", [P, TILE])
    rope = sb("rope", [P, 2, TILE])
    qT = [sb(f"qT{r}", [P, TILE]) for r in range(2)]
    kS = [sb(f"kS{r}", [P, TILE]) for r in range(2)]
    kbd = [sb(f"kbd{r}", [P, HEADS, TILE]) for r in range(2)]
    vbd = [sb(f"vbd{r}", [P, (2 * SUB + 1) * VW]) for r in range(2)]
    probs = [sb(f"probs{r}", [P, HEADS, SEQ]) for r in range(2)]
    probsT = [sb(f"probsT{r}", [P, HEADS // 2, P]) for r in range(2)]
    rmax = [sb(f"rmax{r}", [P, HEADS]) for r in range(2)]
    rden = [sb(f"rden{r}", [P, HEADS]) for r in range(2)]
    att = [sb(f"att{r}", [P, SUB, E]) for r in range(2)]
    lg_all = sb("lg_all", [P, SUBS, EXPERTS])
    ones = sb("ones", [P, P])
    wide_b = sb("wide_b", [P, P], BF16)
    carrier = sb("carrier", [P, 1])
    warm = sb("warm", [P, 1])
    big = EXPERTS * SUBS
    route = kbd[1][:].rearrange("p h t -> p (h t)")
    spare = kbd[0][:].rearrange("p h t -> p (h t)")

    def grid(k):
        return route[:, k * big:(k + 1) * big].rearrange("p (s e) -> p s e", e=EXPERTS)

    oh0, oh1, sel3, less, keyed, second, scan0, scan1, rank = [grid(k) for k in range(9)]
    sel = route[:, 2 * big:3 * big]
    line = [route[:, 9 * big + k * SUBS:9 * big + (k + 1) * SUBS] for k in range(9)]
    top0, top1, idx0, idx1, gap, w1st, wsum = line[:7]
    weight0, weight1 = sb("weight0", [P, SUBS]), sb("weight1", [P, SUBS])
    pos_f = sb("pos_f", [P, CHOICES])
    pos_i = sb("pos_i", [P, 3, CHOICES], I32)
    row_f, blk_f = sb("row_f", [P, CHOICES]), sb("blk_f", [P, CHOICES])
    found = sb("found", [P, 7, BLOCKS])
    gather_rows = sb("gather_rows", [P, BLOCKS], I32)
    scatter_rows = sb("scatter_rows", [P, BLOCKS], I32)
    counts_i = sb("counts_i", [P, EXPERTS], I32)
    blocks_i = sb("blocks_i", [P, EXPERTS], I32)
    blocks_f = sb("blocks_f", [P, 3, EXPERTS])
    first_row = sb("first_row", [P, EXPERTS])
    expert_at = sb("expert_at", [1, BLOCKS], I32)
    past = route[0:1, 12 * big:12 * big + BLOCKS * EXPERTS].rearrange("p (j e) -> p j e", e=EXPERTS)
    past_sum = route[0:1, 15 * big:15 * big + BLOCKS]

    def spare_pair(at, n):
        return [spare[:, at + r * n:at + (r + 1) * n] for r in range(2)]

    xb = [spare[:, r * P:(r + 1) * P] for r in range(UNROLL)]
    yb = [spare[:, (UNROLL + r) * P:(UNROLL + r + 1) * P] for r in range(UNROLL)]
    xbT = spare_pair(2 * UNROLL * P, P)
    th, hh, hbT = [spare_pair(2 * (UNROLL + 1) * P + 2 * k * HIDDEN, HIDDEN) for k in range(3)]
    y_both = [spare[:, k * SUBS * E:(k + 1) * SUBS * E].rearrange("p (s e) -> p s e", e=E) for k in range(2)]
    residual = route[:, 16 * big:].rearrange("p (s e) -> p s e", e=E)
    row_hot = route[:, 16 * big:].bitcast(BF16).rearrange("p (m r) -> p m r", r=P)
    half_blk = CHOICES * BLOCKS // 2
    blk_hot = spare[:, 0:half_blk].bitcast(BF16).rearrange("p (m j) -> p m j", j=BLOCKS)
    blk_code = spare[:, half_blk:3 * half_blk].bitcast(BF16).rearrange("p (m t j) -> p m t j", t=2, j=BLOCKS)
    hn_dram = nc.dram_tensor("hn_dram", [P, SUBS, E], F32).ap()
    base_dram = nc.dram_tensor("base_dram", [P, SUBS, E], F32).ap()
    y_dram = nc.dram_tensor("y_dram", [2 * TOKENS + BLOCKS * P, E], F32).ap()

    ps_s = [ctx.enter_context(nc.psum_tensor(f"ps_s{r}", [P, HEADS, SEQ], F32)) for r in range(2)]
    ps_t = [ctx.enter_context(nc.psum_tensor(f"ps_t{r}", [P, 4, P], F32)) for r in range(2)]
    ring = [ctx.enter_context(nc.psum_tensor(f"ring{r}", [P, 512], F32)) for r in range(2)]
    ps_o, ps_g = ring

    first_loaded = sem("first_loaded")
    weights_loaded = sem("weights_loaded")
    experts_loaded = sem("experts_loaded")
    small_ready = sem("small_ready")
    pool_clear = sem("pool_clear")
    pool_const = sem("pool_const")
    keys_cleared = [sem(f"keys_cleared{r}") for r in range(2)]
    casts_ready = sem("casts_ready")
    const_ready = sem("const_ready")
    setup_filled = sem("setup_filled")
    setup_drained = sem("setup_drained")
    x_loaded = [sem(f"x_loaded{r}") for r in range(2)]
    ctx_loaded = [sem(f"ctx_loaded{r}") for r in range(2)]
    kbd_loaded = [[sem(f"kbd_loaded{r}{g}") for g in range(2)] for r in range(2)]
    scores_ready = sem("scores_ready")
    rmax_ready = sem("rmax_ready")
    centered = sem("centered")
    probs_ready = sem("probs_ready")
    probsT_filled = sem("probsT_filled")
    probsT_copied = sem("probsT_copied")
    rden_ready = sem("rden_ready")
    ring_filled = sem("ring_filled")
    ring_drained = [sem(f"ring_drained{r}") for r in range(2)]
    stats_ready = sem("stats_ready")
    mv_ready = sem("mv_ready")
    pool_step = sem("pool_step")
    normed = sem("normed")
    b2_added = sem("b2_added")
    rotated = sem("rotated")
    exported = sem("exported")
    export_ready = sem("export_ready")
    dve_chain = sem("dve_chain")
    sel_ready = sem("sel_ready")
    ranks_ready = sem("ranks_ready")
    gap_ready = sem("gap_ready")
    weight_ready = sem("weight_ready")
    experts_known = sem("experts_known")
    rows_known = sem("rows_known")
    blocks_hot = [sem(f"blocks_hot{c}") for c in range(CHOICES // CHUNK)]
    rows_hot = sem("rows_hot")
    coded = sem("coded")
    inverted = sem("inverted")
    addresses_ready = sem("addresses_ready")
    gate_up_ready = sem("gate_up_ready")
    xb_loaded = [sem(f"xb_loaded{r}") for r in range(UNROLL)]
    y_stored = [sem(f"y_stored{r}") for r in range(UNROLL)]
    xbT_filled, xbT_copied = sem("xbT_filled"), sem("xbT_copied")
    gu_filled, tanh_ready, gated, h_ready = sem("gu_filled"), sem("tanh_ready"), sem("gated"), sem("h_ready")
    hbT_filled, hbT_copied = sem("hbT_filled"), sem("hbT_copied")
    y_filled, y_copied = sem("y_filled"), sem("y_copied")
    PARTS = 8
    base_loaded = sem("base_loaded")
    y_loaded = [sem(f"y_loaded{t}") for t in range(PARTS)]
    weights_known = sem("weights_known")
    weighed = sem("weighed")
    first_added = sem("first_added")
    summed = sem("summed")
    stored = sem("stored")

    steps = {1: 2, 2: 2, 3: 5, 4: 5, 5: 6, 6: 6}

    def steps_before(i, j):
        return 4 + i * sum(steps.values()) + sum(steps[x] for x in range(1, j))

    def pair_no(i, j, p):
        return i * (JOBS * SUB) + j * SUB + p

    def tile_no(i, j):
        return 2 * i + 2 * (j // JOBS) + j % 2

    def tile_turn(i, j):
        return i + j // JOBS

    def job_turn(i, j):
        return 3 * i + j // 2

    def norm_index(i, j, which):
        if which == "pre":
            return j + 1 if isinstance(i, int) and i == 0 and j <= 1 else norms_before(i, j - 1) + 1
        if isinstance(i, int) and i == ITERS - 1:
            return norms_before(i, JOBS - 1) + (1 if j == JOBS - 2 else 2)
        return norms_before(i, j + 1) + 2

    def is_last(i, j):
        return isinstance(i, int) and i == ITERS - 1 and j == JOBS - 1

    def walk(eng, slot):
        slot(0, 0)
        with eng.Fori(0, ITERS - 1) as i:
            for j in range(1, JOBS + 1):
                slot(i, j)
        for j in range(1, JOBS):
            slot(ITERS - 1, j)

    def steps_at(i, j, p, place):
        post = () if j == 0 else POST[kind_of(j - 1)]
        last = is_last(i, j)
        for name in SLOTS[j][p][place]:
            if name in post:
                yield use_of(i, j, p, place, name, last), name, j - 1
            elif not last:
                yield use_of(i, j, p, place, name), name, j + 1

    def att_use(i, j, p):
        place = (p + 1, 1) if p < SUB - 1 else (p, 3)
        return use_of(i, j, *place, "att", is_last(i, j))

    def source(i, j, name):
        if name in TAIL[0:2] + ("h0", "h1", "hT", "ff", "lg"):
            if isinstance(i, int) and i == ITERS - 1 and j == JOBS - 1:
                return tail_use(name)
            return named_use(i, j + 1, name, is_last(i, j + 1))
        if isinstance(i, int) and i == 0 and j == 0:
            return Use(0, PRE0.index(name))
        return named_use(i, j - 1, name)

    def att_before(i, j, p):
        if p >= 2:
            return att_use(i, j, p - 2)
        if j == 1:
            return Use(i, N_FIRST - 2 + p)
        return att_use(i, j - 1, p + 2)

    def tail_use(name):
        names = [x for x in TAIL if x not in NOT_ON_PE]
        c = N_FIRST + sum(N_SLOT[x] for x in range(1, JOBS - 1)) + count(ring_uses(JOBS - 1, True))
        return Use(ITERS - 1, c + names.index(name))

    def route_dve(dve):
        V = nc.vector
        n = [0]

        def step(ins):
            n[0] += 1
            ins.then_inc(dve_chain, 1)
            dve.wait_ge(dve_chain, n[0])

        iota = const[:, C_IOTA:C_IOTA + EXPERTS].unsqueeze(1).broadcast_to([P, SUBS, EXPERTS])

        def wide(x):
            return x.unsqueeze(2).broadcast_to([P, SUBS, EXPERTS])

        for src, top, idx, oh in ((lg_all[:], top0, idx0, oh0), (second, top1, idx1, oh1)):
            step(V.reduce_max(top, src, AX.X))
            step(V.tensor_tensor(less, src, wide(top), ALU.is_lt))
            step(V.scalar_tensor_tensor(keyed, less, float(EXPERTS), iota, ALU.mult, ALU.add))
            step(V.tensor_reduce(idx, keyed, AX.X, ALU.min))
            step(V.tensor_tensor(oh, iota, wide(idx), ALU.is_equal))
            if src is not second:
                step(V.scalar_tensor_tensor(second, oh, -1e30, src, ALU.mult, ALU.add))
        V.tensor_tensor(sel3, oh0, oh1, ALU.add).then_inc(sel_ready, 1)
        V.tensor_tensor(gap, top1, top0, ALU.subtract).then_inc(gap_ready, 1)
        dve.wait_ge(ranks_ready, 1)
        within = ps_g[:, 0:big].rearrange("p (s e) -> p s e", e=EXPERTS)
        total = ps_g[:, big:2 * big].rearrange("p (s e) -> p s e", e=EXPERTS)
        step(V.tensor_copy(scan0, total))
        src, dst = scan0, scan1
        for k in (1, 2, 4, 8, 16):
            V.tensor_copy(dst[:, 0:k, :], src[:, 0:k, :])
            step(V.tensor_tensor(dst[:, k:, :], src[:, k:, :], src[:, 0:SUBS - k, :], ALU.add))
            src, dst = dst, src
        step(V.tensor_scalar(counts_i[:], src[:, SUBS - 1, :], float(P - 1), None, ALU.add))
        step(V.tensor_scalar(blocks_i[:], counts_i[:], 7, None, ALU.logical_shift_right))
        step(V.tensor_copy(blocks_f[:, 0, :], blocks_i[:]))
        a0, b0 = 0, 1
        for k in (1, 2, 4):
            V.tensor_copy(blocks_f[:, b0, 0:k], blocks_f[:, a0, 0:k])
            step(V.tensor_tensor(blocks_f[:, b0, k:], blocks_f[:, a0, k:], blocks_f[:, a0, 0:EXPERTS - k], ALU.add))
            a0, b0 = b0, (2 if k == 1 else a0)
        ends = blocks_f[:, a0, :]
        step(V.tensor_copy(blocks_f[:, b0, :], blocks_i[:]))
        step(V.tensor_tensor(first_row[:], ends, blocks_f[:, b0, :], ALU.subtract))
        step(V.tensor_scalar(first_row[:], first_row[:], float(P), None, ALU.mult))
        step(V.tensor_tensor(rank, src, total, ALU.subtract))
        step(V.tensor_tensor(rank, rank, within, ALU.add))
        step(V.tensor_tensor(rank, rank, first_row[:].unsqueeze(1).broadcast_to([P, SUBS, EXPERTS]), ALU.add))
        for k, oh in enumerate((oh0, oh1)):
            step(V.tensor_tensor(keyed, oh, rank, ALU.mult))
            step(V.reduce_sum(pos_f[:, k * SUBS:(k + 1) * SUBS], keyed, AX.X))
        step(V.tensor_copy(pos_i[:, 0, :], pos_f[:]))
        step(V.tensor_scalar(pos_i[:, 1, :], pos_i[:, 0, :], 7, None, ALU.logical_shift_right))
        step(V.tensor_scalar(pos_i[:, 2, :], pos_i[:, 0, :], P - 1, None, ALU.bitwise_and))
        step(V.tensor_copy(blk_f[:], pos_i[:, 1, :]))
        V.tensor_copy(row_f[:], pos_i[:, 2, :]).then_inc(rows_known, 1)
        dve.wait_ge(rows_known, 1)
        for c in range(CHOICES // CHUNK):
            ms = range(c * CHUNK, (c + 1) * CHUNK)
            if c < CHOICES // CHUNK // 2:
                for m in ms:
                    last = V.tensor_scalar(blk_hot[:, m, :], wide_b[:, 0:BLOCKS], blk_f[:, m:m + 1], None, ALU.is_equal)
                last.then_inc(blocks_hot[c], 1)
            for m in ms:
                V.tensor_scalar(row_hot[:, m, :], wide_b[:], row_f[:, m:m + 1], None, ALU.is_equal)
            dve.wait_ge(blocks_hot[c], 1)
            V.tensor_scalar(blk_code[:, ms[0]:ms[-1] + 1, 0, :], blk_hot[:, ms[0]:ms[-1] + 1, :],
                            const[:, C_COL:C_COL + 1], None, ALU.mult).then_inc(rows_hot, 1)
        step(V.tensor_tensor(past, const[0:1, C_BLK:C_BLK + BLOCKS].unsqueeze(2).broadcast_to([1, BLOCKS, EXPERTS]),
                             ends[0:1, :].unsqueeze(1).broadcast_to([1, BLOCKS, EXPERTS]), ALU.is_ge))
        step(V.reduce_sum(past_sum, past, AX.X))
        V.tensor_scalar(expert_at[:], past_sum, float(EXPERTS - 1), float(W_ALL), ALU.min, ALU.mult)\
         .then_inc(experts_known, 1)
        dve.wait_ge(inverted, 1)
        partition, code = ps_o[:, 0:BLOCKS], ps_o[:, BLOCKS:2 * BLOCKS]
        unused, second_choice, subtile, sub_f, gather_f, target, extra = [found[:, k, :] for k in range(7)]
        V.tensor_scalar(unused, code, 0.0, None, ALU.is_equal)
        V.tensor_scalar(second_choice, code, float(SUBS), None, ALU.is_gt)
        step(V.tensor_scalar(subtile, code, -1.0, 0.0, ALU.add, ALU.max))
        V.tensor_tensor(extra, unused, const[:, C_SPARE:C_SPARE + BLOCKS], ALU.mult)
        step(V.scalar_tensor_tensor(sub_f, second_choice, -float(SUBS), subtile, ALU.mult, ALU.add))
        step(V.scalar_tensor_tensor(gather_f, partition, float(SUBS), sub_f, ALU.mult, ALU.add))
        V.tensor_copy(gather_rows[:], gather_f).then_inc(addresses_ready, 1)
        step(V.scalar_tensor_tensor(target, second_choice, float(TOKENS), gather_f, ALU.mult, ALU.add))
        V.tensor_tensor(scatter_rows[:], target, extra, ALU.add).then_inc(addresses_ready, 1)
        dve.wait_ge(weight_ready, 1)
        step(V.tensor_scalar(wsum, w1st, 1.0, None, ALU.add))
        step(V.reciprocal(weight0[:], wsum))
        V.tensor_tensor(weight1[:], w1st, weight0[:], ALU.mult).then_inc(weights_known, 1)

    def invert_act(act):
        for c in range(CHOICES // CHUNK):
            act.wait_ge(blocks_hot[c], 1)
            for m in range(c * CHUNK, (c + 1) * CHUNK):
                last = nc.scalar.activation(blk_code[:, m, 1, :], blk_hot[:, m, :], ACT.Copy, scale=float(m + 1))
            last.then_inc(coded, 1)

    def invert_pe(pe):
        for c in range(CHOICES // CHUNK):
            pe.wait_ge(rows_hot, c + 1)
            pe.wait_ge(coded, c + 1)
            for m in range(c * CHUNK, (c + 1) * CHUNK):
                last = nc.tensor.matmul(ps_o[:, 0:2 * BLOCKS], row_hot[:, m, :],
                                        blk_code[:, m].rearrange("p t j -> p (t j)"),
                                        start=(m == 0), stop=(m == CHOICES - 1))
        last.then_inc(inverted, 1)

    def blocks(eng, step):
        for c in range(UNROLL):
            step(0, c)
        with eng.Fori(0, TURNS - 2) as n:
            for c in range(UNROLL):
                step(n + 1, c)
        for c in range(UNROLL):
            step(TURNS - 1, c)

    def there(i, c):
        return not isinstance(i, int) or 0 <= i * UNROLL + c < BLOCKS

    g_bank = [ps_s[0][:].rearrange("p h k -> p (h k)")[:, 512 * r:512 * r + HIDDEN] for r in range(2)]
    u_bank = [ps_s[1][:].rearrange("p h k -> p (h k)")[:, 512 * r:512 * r + HIDDEN] for r in range(2)]
    h_bank = [ps_t[r][:].rearrange("p a b -> p (a b)")[:, 0:HIDDEN] for r in range(2)]
    x_bank, y_bank = ps_o[:, 0:P], ps_g[:, 0:E]

    def experts_sp(sp):
        sp.wait_ge(exported, EXPORT * (TILES + 1))
        sp.wait_ge(inverted, 1)
        sp.dma_start(residual, base_dram).then_inc(base_loaded, 16)
        for r in range(UNROLL):
            sp.wait_ge(y_stored[r], 16 * TURNS)
        for t in range(PARTS):
            sl = slice(t * SUBS // PARTS, (t + 1) * SUBS // PARTS)
            for k in range(2):
                y_k = y_dram[k * TOKENS:(k + 1) * TOKENS].rearrange("(p s) e -> p s e", p=P)
                sp.dma_start(y_both[k][:, sl, :], y_k[:, sl, :]).then_inc(y_loaded[t], 16)
        for t in range(TILES):
            sp.wait_ge(summed, t + 1)
            sp.dma_start(out_t[t], residual[:, t * SUB:(t + 1) * SUB, :]).then_inc(stored, 16)
        sp.wait_ge(stored, 16 * TILES)

    def invert_pool(pool):
        pool.wait_ge(rows_known, 1)
        for c in range(CHOICES // CHUNK // 2, CHOICES // CHUNK):
            for m in range(c * CHUNK, (c + 1) * CHUNK):
                last = nc.gpsimd.tensor_scalar(blk_hot[:, m, :], wide_b[:, 0:BLOCKS], blk_f[:, m:m + 1], None,
                                               ALU.is_equal)
            last.then_inc(blocks_hot[c], 1)

    def experts_pool(pool):
        G = nc.gpsimd
        hn_rows = hn_dram.rearrange("p s e -> (p s) e")

        def column(table, i, c):
            j = i * UNROLL + c
            return table[:, j:j + 1] if isinstance(j, int) else table[:, bass.ds(j, 1)]

        def gather(i, c):
            r = c % UNROLL
            G.indirect_dma_start(out=xb[r], out_offset=None, in_=hn_rows,
                                 in_offset=bass.IndirectOffsetOnAxis(ap=column(gather_rows, i, c), axis=0))\
             .then_inc(xb_loaded[r], 16)

        def scatter(i, c):
            r = c % UNROLL
            G.indirect_dma_start(out=y_dram, in_=yb[r], in_offset=None,
                                 out_offset=bass.IndirectOffsetOnAxis(ap=column(scatter_rows, i, c), axis=0))\
            .then_inc(y_stored[r], 16)

        pool.wait_ge(exported, EXPORT * (TILES + 1))
        pool.wait_ge(addresses_ready, 2)
        for c in range(UNROLL):
            gather(0, c)
        for j in range(BLOCKS):
            i, c = divmod(j, UNROLL)
            if there(i, c + UNROLL):
                pool.wait_ge(xbT_filled, j + 1)
                gather(i, c + UNROLL)
            if there(i, c - 1):
                pool.wait_ge(y_copied, j)
                scatter(i, c - 1)
        pool.wait_ge(y_copied, BLOCKS)
        scatter(TURNS - 1, UNROLL - 1)

    def experts_pe(pe):
        mm = nc.tensor.matmul
        pe.wait_ge(experts_known, 1)
        pe.wait_ge(gate_up_ready, 1)
        pe.wait_ge(experts_loaded, 16 * (2 + HC))

        def expert(i, c):
            j = i * UNROLL + c
            at = expert_at[0:1, j:j + 1] if isinstance(j, int) else expert_at[0:1, bass.ds(j, 1)]
            return pe.value_load(at, min_val=0, max_val=(EXPERTS - 1) * W_ALL)

        def weights(at, column, n):
            span = (EXPERTS - 1) * W_ALL + n
            return w_exp[:].rearrange("p x c -> p (x c)")[:, column:column + span][:, bass.ds(at, n)]

        def rows_T(i, c):
            r = c % UNROLL
            pe.wait_ge(xb_loaded[r], (i + c // UNROLL) * 16 + 16)
            wait(pe, xbT_copied, i * UNROLL + c)
            nc.tensor.transpose(x_bank, xb[r], ident).then_inc(xbT_filled, 1)

        def gate_up(i, c, e):
            j, r = i * UNROLL + c, c % 2
            pe.wait_ge(xbT_copied, j + 1)
            wait(pe, h_ready, j - 1)
            for bank, column in ((g_bank, W_GATE), (u_bank, W_UP)):
                last = mm(bank[r], xbT[r], weights(e, column, HIDDEN), start=True, stop=True)
            last.then_inc(gu_filled, 1)

        def hidden_T(i, c):
            j, r = i * UNROLL + c, c % 2
            pe.wait_ge(h_ready, j + 1)
            wait(pe, hbT_copied, j - 1)
            for k in range(HC):
                last = nc.tensor.transpose(h_bank[r][:, k * P:(k + 1) * P], hh[r][:, k * P:(k + 1) * P], ident)
            last.then_inc(hbT_filled, 1)

        def down(i, c, e):
            j, r = i * UNROLL + c, c % 2
            pe.wait_ge(hbT_copied, j + 1)
            wait(pe, y_copied, j)
            for k in range(HC):
                last = mm(y_bank, hbT[r][:, k * P:(k + 1) * P], weights(e, W_DOWN + k * E, E),
                          start=(k == 0), stop=(k == HC - 1))
            last.then_inc(y_filled, 1)

        rows_T(0, 0)
        rows_T(0, 1)
        gate_up(0, 0, expert(0, 0))
        rows_T(0, 2)
        gate_up(0, 1, expert(0, 1))
        e = {}

        def know(i, c):
            if there(i, c):
                e[c] = expert(i, c)

        def step(i, c):
            know(i, c + 2)
            hidden_T(i, c)
            if there(i, c + 3):
                rows_T(i, c + 3)
            if there(i, c + 2):
                gate_up(i, c + 2, e[c + 2])
            if c < 2:
                know(i, c)
            down(i, c, e[c])

        blocks(pe, step)

    def experts_act(act):
        def rows_out(i, c):
            j = i * UNROLL + c
            act.wait_ge(xbT_filled, j + 1)
            wait(act, gu_filled, j - 1)
            nc.scalar.activation(xbT[c % 2], x_bank, ACT.Copy).then_inc(xbT_copied, 1)

        def tanh(i, c):
            j, r = i * UNROLL + c, c % 2
            act.wait_ge(gu_filled, j + 1)
            wait(act, h_ready, j - 1)
            nc.scalar.activation(th[r], g_bank[r], ACT.Tanh, scale=0.5).then_inc(tanh_ready, 1)

        rows_out(0, 0)
        rows_out(0, 1)
        tanh(0, 0)
        rows_out(0, 2)
        tanh(0, 1)

        def step(i, c):
            j, r = i * UNROLL + c, c % 2
            act.wait_ge(hbT_filled, j + 1)
            wait(act, y_filled, j - 1)
            nc.scalar.activation(hbT[r], h_bank[r], ACT.Copy, scale=0.5).then_inc(hbT_copied, 1)
            if there(i, c + 3):
                rows_out(i, c + 3)
            if there(i, c + 2):
                tanh(i, c + 2)

        blocks(act, step)

    def experts_dve(dve):
        V = nc.vector

        def gate(i, c):
            j, r = i * UNROLL + c, c % 2
            dve.wait_ge(tanh_ready, j + 1)
            V.scalar_tensor_tensor(th[r], th[r], 1.0, g_bank[r], ALU.add, ALU.mult).then_inc(gated, 1)
            wait(dve, hbT_filled, j - 1)
            dve.wait_ge(gated, j + 1)
            V.tensor_tensor(hh[r], th[r], u_bank[r], ALU.mult).then_inc(h_ready, 1)

        def copy_y(i, c):
            r = c % UNROLL
            dve.wait_ge(y_filled, i * UNROLL + c + 1)
            wait(dve, y_stored[r], (i + c // UNROLL) * 16)
            V.tensor_scalar(yb[r], y_bank, 1.0, None, ALU.mult).then_inc(y_copied, 1)

        gate(0, 0)
        gate(0, 1)

        def step(i, c):
            if there(i, c + 2):
                gate(i, c + 2)
            copy_y(i, c)

        blocks(dve, step)

    def weigh_act(act):
        y1 = y_both[1]
        act.wait_ge(weights_known, 1)
        for s in range(SUBS):
            if s % (SUBS // PARTS) == 0:
                act.wait_ge(y_loaded[s // (SUBS // PARTS)], 32)
            nc.scalar.activation(y1[:, s, :], y1[:, s, :], ACT.Copy, scale=weight1[:, s:s + 1]).then_inc(weighed, 1)

    def combine_dve(dve):
        V = nc.vector
        dve.wait_ge(base_loaded, 16)
        y0, y1 = y_both
        for t in range(TILES):
            for s in range(t * SUB, (t + 1) * SUB):
                if s % (SUBS // PARTS) == 0:
                    dve.wait_ge(y_loaded[s // (SUBS // PARTS)], 32)
                V.scalar_tensor_tensor(y0[:, s, :], y0[:, s, :], weight0[:, s:s + 1], residual[:, s, :],
                                       ALU.mult, ALU.add).then_inc(first_added, 1)
            dve.wait_ge(weighed, (t + 1) * SUB)
            dve.wait_ge(first_added, (t + 1) * SUB)
            sl = slice(t * SUB, (t + 1) * SUB)
            V.tensor_tensor(residual[:, sl, :], y0[:, sl, :], y1[:, sl, :], ALU.add).then_inc(summed, 1)

    block = ctx.enter_context(nc.Block())

    x_t = a["x"].rearrange("b q e -> (b q) e").rearrange("(t s p) e -> t p s e", s=SUB, p=P)
    c_t = a["ctx_768"].rearrange("b q e -> (b q) e").rearrange("(t s p) e -> t p s e", s=SUB, p=P)
    out_t = out.rearrange("b q e -> (b q) e").rearrange("(t s p) e -> t p s e", s=SUB, p=P)

    def dyn(ap, t):
        if isinstance(t, int):
            return ap[t]
        return ap[bass.ds(t, 1)].rearrange("o p s e -> (o p) s e")

    def column(name, lo=0):
        return a[name][lo:lo + P].rearrange("(p o) -> p o", o=1)

    @block.sync
    def _(sp):
        def load_tile(t, r):
            sp.dma_start(xin[r][:], dyn(x_t, t)).then_inc(x_loaded[r], 16)
            sp.dma_start(cin[r][:], dyn(c_t, t)).then_inc(ctx_loaded[r], 16)

        first = [(w_given[:, 0:3, :], a["L0_attn_in_proj_weight"].rearrange("(k p) e -> p k e", p=P)),
                 (const[:], a["const"]), (w_given[:, 3, :], a["L0_attn_out_proj_weight"])]
        assert len(first) == N_FIRST_LOADS
        load_tile(0, 0)
        for dst, src in first:
            sp.dma_start(dst, src).then_inc(first_loaded, 16)
        loads = [(w_given_f[:, 0, :], a["L0_ffn_wq"]), (w_given_f[:, 1, :], a["L0_ffn_wk"]),
                 (w_f[:, 2, :], a["L0_ffn_wv"]), (w_f[:, 5, :], a["L0_ffn_wo"])]
        loads += [(cols[:, 5:6], column("L0_ffn_g1")), (cols[:, 6:7], column("L0_ffn_g2"))]
        loads += [(w_x[:, 0, :], a["L0_xattn_Wq"]), (w_x[0:CE, 1, :], a["L0_xattn_Wk"]),
                  (w_x[0:CE, 2, :], a["L0_xattn_Wv"]), (w1[:], a["L0_xattn_W1"]),
                  (w2[:], a["L0_xattn_W2"].rearrange("(k p) e -> p k e", p=P))]
        loads += [(cols[:, 0:1], column("L0_xattn_bq")), (cols[:, 1:2], column("L0_xattn_bk")),
                  (cols[:, 2:3], column("L0_xattn_bv")), (cols[:, 3:4], column("L0_xattn_b1")),
                  (cols[:, 4:5], column("L0_xattn_b1", P)),
                  (b2[:], a["L0_xattn_b2"].rearrange("(o e) -> o e", o=1).broadcast_to([P, E])),
                  (w_r[:], a["L0_ffn_w_router"])]
        assert len(loads) == N_LOADS
        for dst, src in loads:
            sp.dma_start(dst, src).then_inc(weights_loaded, 16)
        load_tile(1, 1)
        def spread_keys(i, j):
            r = j % 2
            if isinstance(i, int) and j == i == 0:
                sp.wait_ge(keys_cleared[0], 2)
            elif j == 1:
                sp.wait_ge(keys_cleared[1], 1)
            if kind_of(j) == 2:
                sp.wait_ge(rotated, 2 * tile_no(i, j) + 1)
            else:
                u = source(i, j, "k")
                sp.wait_ge(ring_drained[u.bank], u.drained())

            for h in range(HEADS - (HEADS_ACT if kind_of(j) == 2 else 0)):
                sp.dma_start(kbd[r][D * h:D * h + D, h, :], kS[r][D * h:D * h + D, :])\
                  .then_inc(kbd_loaded[r][2 * h // HEADS], 16)

        def export(i, j):
            t = tile_no(i, j)
            wait(sp, export_ready, t + 1)
            sl = slice(t * SUB, t * SUB + SUB) if isinstance(t, int) else bass.ds(t * SUB, SUB)
            sp.dma_start(hn_dram[:, sl, :], hn[:]).then_inc(exported, 16)
            sp.dma_start(base_dram[:, sl, :], base[:]).then_inc(exported, 16)

        sp.sem_inc(exported, EXPORT)
        spread_keys(0, 0)
        sp.dma_start(w_exp[:, :, W_GATE:W_UP], a["L0_ffn_wg"].rearrange("x p h -> p x h")).then_inc(experts_loaded, 16)
        sp.dma_start(w_exp[:, :, W_UP:W_DOWN], a["L0_ffn_wu"].rearrange("x p h -> p x h")).then_inc(experts_loaded, 16)
        for k in range(HC):
            sp.dma_start(w_exp[:, :, W_DOWN + k * E:W_DOWN + (k + 1) * E],
                         a["L0_ffn_wd"][:, k * P:(k + 1) * P, :].rearrange("x p e -> p x e"))\
              .then_inc(experts_loaded, 16)

        def slot(i, j):
            if j in (3, 4) and not (isinstance(i, int) and i == ITERS - 1):
                u = named_use(i, j - 2, "q")
                sp.wait_ge(ring_drained[u.bank], u.drained())
                load_tile(2 * i + 2 + (j - 3), j - 3)
            if not is_last(i, j):
                spread_keys(i, j + 1)
            if j in (5, 6):
                export(i, j - 1)

        walk(sp, slot)
        export(ITERS - 1, JOBS - 1)
        experts_sp(sp)

    @block.tensor
    def _(pe):
        mm = nc.tensor.matmul

        def setup_first():
            pe.wait_ge(first_loaded, 16 * N_FIRST_LOADS)
            for k in range(4):
                last = nc.tensor.transpose(ps_t[0][:, k, :], w_given[:, k, :], ident)
            last.then_inc(setup_filled, 1)
            pe.wait_ge(setup_drained, 1)

        def setup_rotated():
            pe.wait_ge(weights_loaded, 16 * N_LOADS)
            pe.wait_ge(const_ready, 1)
            for k in range(2):
                last = nc.tensor.transpose(ps_t[1][:, k, :], w_f[:, k, :], ident)
            last.then_inc(setup_filled, 1)
            pe.wait_ge(setup_drained, 2)
            for k in range(2):
                last = mm(ps_t[1][:, k, :], w_turned[:, k, :], const[:, C_ROT:C_ROT + P],
                          start=True, stop=True)
            last.then_inc(setup_filled, 1)
            pe.wait_ge(setup_drained, 3)

        def transposes(ps_g, src, rows=P):
            for s in range(SUB):
                last = nc.tensor.transpose(ps_g[0:rows, s * P:(s + 1) * P], src[:, s, :], ident)
            return last

        def values(ps_g, src, w, half):
            for b in range(SUB):
                col = (half * SUB + b) * SEQ
                for q in range(2):
                    last = mm(ps_g[SEQ * q:SEQ * q + SEQ, b * P:(b + 1) * P], src[:, col:col + SEQ], w,
                              start=True, stop=True)
            return last

        def copied(uses, u=None):
            need = {}
            for x in uses:
                need[x.bank] = max(need.get(x.bank, 0), x.c // 2 + 1)
            if u is not None:
                need[u.bank] = max(need.get(u.bank, 0), u.c // 2)
            i = (u or uses[0]).i
            for bank, c in sorted(need.items()):
                wait(pe, ring_drained[bank], i * (N_ITER // 2) + c)

        def use(u, name, i, j):
            kind = kind_of(j)
            r = j % 2
            if name in NOT_ON_PE:
                return
            if name == "xT":
                pe.wait_ge(normed, norm_index(i, j, "pre"))
            elif name == "hT":
                pe.wait_ge(normed, norm_index(i, j, "post"))
            elif name == "cT":
                pe.wait_ge(ctx_loaded[r], 16 * (tile_turn(i, j) + 1))
            if name == "oT":
                needs = [att_use(i, j, SUB - 1)]
            elif name in ("xT", "hT", "cT"):
                needs = []
            else:
                names = {"wo": ("oT",), "h0": ("oT",), "h1": ("oT",), "ff": ("h0", "h1"), "lg": ("hT",)}
                names = names.get(name, ("cT",) if kind == 1 and name != "q" else ("xT",))
                needs = [source(i, j, x) for x in names]
            copied(needs, u)
            ps_g = ring[u.bank]
            if name == "xT":
                last = transposes(ps_g, xh)
            elif name == "cT":
                last = transposes(ps_g, cin[r], CE)
            elif name == "oT":
                last = transposes(ps_g, att[r])
            elif name == "hT":
                last = transposes(ps_g, hn)
            elif name == "wo":
                w = w_a[:, 3, :] if kind == 0 else w_f[:, 5, :]
                for s in range(SUB):
                    last = mm(ps_g[:, s * P:(s + 1) * P], oT[:, s * P:(s + 1) * P], w, start=True, stop=True)
            elif name in ("h0", "h1"):
                k = int(name[1])
                last = mm(ps_g[:], w1[:, k * P:(k + 1) * P], oT[:], start=True, stop=True)
            elif name == "ff":
                for s in range(SUB):
                    for k in range(2):
                        last = mm(ps_g[:, s * P:(s + 1) * P], h1T[:, k, s * P:(s + 1) * P], w2[:, k, :],
                                  start=(k == 0), stop=(k == 1))
            elif name == "lg":
                for s in range(SUB):
                    last = mm(ps_g[:, s * EXPERTS:(s + 1) * EXPERTS], hT[:, s * P:(s + 1) * P], w_r[:],
                              start=True, stop=True)
            elif name in ("v0", "v1"):
                src, w = {0: (xT, w_a[:, 2, :]), 1: (cT, w_x[0:CE, 2, :]), 2: (xT, w_f[:, 2, :])}[kind]
                last = values(ps_g, src, w, int(name[1]))
            else:
                w = {(0, "q"): w_a[:, 0, :], (0, "k"): w_a[:, 1, :], (1, "q"): w_x[:, 0, :],
                     (1, "k"): w_x[0:CE, 1, :], (2, "q"): w_f[:, 0, :], (2, "k"): w_f[:, 1, :],
                     (2, "qr"): w_f[:, 3, :], (2, "kr"): w_f[:, 4, :]}[kind, name]
                last = mm(ps_g[:], w, (cT if kind == 1 and name == "k" else xT)[:], start=True, stop=True)
            last.then_inc(ring_filled, 1)

        def scores(i, j, p):
            n = pair_no(i, j, p)
            r, half = j % 2, p % 2
            if p == 0:
                if kind_of(j) == 2:
                    pe.wait_ge(rotated, 2 * tile_no(i, j) + 2)
                else:
                    copied([source(i, j, "q")])
            wait(pe, centered, n - 1)
            causal = kind_of(j) != 1
            for g in range(2):
                if p == 0:
                    pe.wait_ge(kbd_loaded[r][g], 8 * HEADS * (job_turn(i, j) + 1))
                if causal:
                    mm(ps_s[half][:, 8 * g:8 * g + 8, :], identb[:],
                       maskb[:].unsqueeze(1).broadcast_to([P, 8, SEQ]), start=True, stop=False)
                for b in range(2):
                    rows = slice(SEQ * b, SEQ * b + SEQ)
                    o = ps_s[half][rows, 8 * g:8 * g + 8, :]
                    tok = (2 * p + b) * SEQ
                    last = mm(o, qT[r][:, tok:tok + SEQ], kbd[r][:, 8 * g:8 * g + 8, tok:tok + SEQ],
                              start=not causal, stop=True)
            last.then_inc(scores_ready, 1)

        def transpose_probs(i, j, p):
            n = pair_no(i, j, p)
            pe.wait_ge(probs_ready, n + 1)
            flat = probs[p % 2][:].rearrange("p h k -> p (h k)")
            for g in range(2):
                wait(pe, probsT_copied, 2 * n + g - 1)
                for k in range(4):
                    c = (4 * g + k) * P
                    last = nc.tensor.transpose(ps_t[g][:, k, :], flat[:, c:c + P], ident)
                last.then_inc(probsT_filled, 1)

        def attend(i, j, p):
            n = pair_no(i, j, p)
            r = j % 2
            u = att_use(i, j, p)
            pe.wait_ge(probsT_copied, 2 * n + 2)
            copied([source(i, j, x) for x in ("v0", "v1")] if p == 0 and j != 1 else [], u)
            o = ring[u.bank][:, 0:2 * (VW + PAD)].rearrange("p (b c) -> p b c", b=2)
            for k in range(HEADS // 2):
                c = 2 * (D + 1) * k
                v = vbd[r][:, 2 * p * VW + c:2 * p * VW + c + 2 * VW].rearrange("p (b c) -> p b c", b=2)
                last = mm(o[:, :, c:c + PAD], probsT[p % 2][:, k, :], v[:, :, 0:PAD], start=True, stop=True)
            last.then_inc(ring_filled, 1)

        setup_first()
        for k, name in enumerate(PRE0):
            use(Use(0, k), name, 0, 0)
        pe.wait_ge(casts_ready, 1)
        scores(0, 0, 0)
        setup_rotated()

        def slot(i, j):
            for p in range(SUB):
                if p < SUB - 1:
                    scores(i, j, p + 1)
                for u, name, jj in steps_at(i, j, p, 0):
                    use(u, name, i, jj)
                if p > 0:
                    attend(i, j, p - 1)
                transpose_probs(i, j, p)
                for place in (1, 2):
                    for u, name, jj in steps_at(i, j, p, place):
                        use(u, name, i, jj)
            if j in SCORES_FIRST and not is_last(i, j):
                scores(i, j + 1, 0)
            attend(i, j, SUB - 1)
            if j not in SCORES_FIRST and not is_last(i, j):
                scores(i, j + 1, 0)

        walk(pe, slot)
        for name in TAIL:
            if name not in NOT_ON_PE:
                use(tail_use(name), name, ITERS - 1, JOBS - 1)

        pe.wait_ge(sel_ready, 1)
        for name in ("hT", "lg"):
            u = tail_use(name)
            pe.wait_ge(ring_drained[u.bank], u.drained())
        mm(ps_g[:, 0:SUBS * EXPERTS], const[:, C_LOW:C_LOW + P], sel[:], start=True, stop=True)
        mm(ps_g[:, 256:512], ones[:], sel[:], start=True, stop=True).then_inc(ranks_ready, 1)

        invert_pe(pe)
        experts_pe(pe)

    @block.scalar
    def _(act):
        def exps(i, j, p):
            n = pair_no(i, j, p)
            act.wait_ge(centered, n + 1)
            nc.scalar.activation(probs[p % 2][:], probs[p % 2][:], ACT.Exp, scale=SCALE).then_inc(probs_ready, 1)

        def copy_probsT(i, j, p):
            n = pair_no(i, j, p)
            if not (isinstance(n, int) and n < 2):
                act.wait_ge(ring_filled, att_before(i, j, p).filled())
            for g in range(2):
                act.wait_ge(probsT_filled, 2 * n + g + 1)
                nc.scalar.activation(probsT[p % 2][:, 4 * g:4 * g + 4, :], ps_t[g][:], ACT.Copy)\
                  .then_inc(probsT_copied, 1)

        def use(u, name, i, j):
            kind, r = kind_of(j), j % 2
            if name in DVE_DRAINS + ("st", "ap", "st2", "ap2") or (kind == 2 and name in ("q", "k")):
                return
            if name == "ks":
                act.wait_ge(rotated, 2 * tile_no(i, j) + 1)
                for h in range(HEADS - HEADS_ACT, HEADS):
                    rows_of_head = const[:, C_HEAD + h:C_HEAD + h + 1]
                    nc.scalar.activation(kbd[r][:, h, :], kS[r][:], ACT.Copy, scale=rows_of_head)\
                      .then_inc(kbd_loaded[r][1], 16)
                return
            if name == "k":
                for g in range(2):
                    wait(act, kbd_loaded[r][g], 8 * HEADS * job_turn(i, j))
            act.wait_ge(ring_filled, u.filled())
            ps_g = ring[u.bank]
            if name == "xT":
                ins = nc.scalar.activation(xT[:], ps_g[:], ACT.Copy)
            elif name == "cT":
                ins = nc.scalar.activation(cT[:], ps_g[0:CE, :], ACT.Copy)
            elif name == "oT" and kind == 1:
                ins = nc.scalar.activation(oT[:], ps_g[:], ACT.Identity, bias=cols[:, 2:3])
            elif name == "oT":
                ins = nc.scalar.activation(oT[:], ps_g[:], ACT.Copy)
            elif name == "hT":
                ins = nc.scalar.activation(hT[:], ps_g[:], ACT.Copy)
            elif name in ("h0", "h1"):
                k = int(name[1])
                ins = nc.scalar.activation(h1T[:, k, :], ps_g[:], ACT.Relu, bias=cols[:, 3 + k:4 + k])
            elif name == "q":
                ins = (nc.scalar.activation(qT[r][:], ps_g[:], ACT.Identity, bias=cols[:, 0:1]) if kind == 1
                       else nc.scalar.activation(qT[r][:], ps_g[:], ACT.Copy))
            elif name == "k":
                ins = (nc.scalar.activation(kS[r][:], ps_g[:], ACT.Identity, bias=cols[:, 1:2]) if kind == 1
                       else nc.scalar.activation(kS[r][:], ps_g[:], ACT.Copy))
            ins.then_inc(ring_drained[u.bank], 1)

        act.wait_ge(small_ready, 1)
        nc.scalar.activation(warm[:], small[:, 0:1], ACT.Exp)
        act.wait_ge(setup_filled, 1)
        nc.scalar.activation(w_a[:], ps_t[0][:], ACT.Copy).then_inc(setup_drained, 1)
        for k, name in enumerate(PRE0):
            use(Use(0, k), name, 0, 0)
        act.wait_ge(weights_loaded, 16 * N_LOADS)
        act.wait_ge(setup_filled, 2)
        nc.scalar.activation(w_turned[:], ps_t[1][:, 0:2, :], ACT.Copy).then_inc(setup_drained, 1)
        act.wait_ge(setup_filled, 3)
        nc.scalar.activation(w_f[:, 3:5, :], ps_t[1][:, 0:2, :], ACT.Copy).then_inc(setup_drained, 1)

        def slot(i, j):
            for p in range(SUB):
                for u, name, jj in steps_at(i, j, p, 0):
                    use(u, name, i, jj)
                copy_probsT(i, j, p)
                for place in (1, 2):
                    for u, name, jj in steps_at(i, j, p, place):
                        use(u, name, i, jj)
                if p < SUB - 1:
                    exps(i, j, p + 1)
            if not is_last(i, j):
                exps(i, j + 1, 0)

        exps(0, 0, 0)
        walk(act, slot)
        for name in TAIL:
            use(None if name in NOT_ON_PE else tail_use(name), name, ITERS - 1, JOBS - 1)
        act.wait_ge(experts_loaded, 16 * (2 + HC))
        nc.scalar.activation(w_exp[:, :, 0:W_DOWN], w_exp[:, :, 0:W_DOWN], ACT.Copy, scale=cols[:, 6:7])\
          .then_inc(gate_up_ready, 1)
        act.wait_ge(gap_ready, 1)
        nc.scalar.activation(w1st[:], gap[:], ACT.Exp).then_inc(weight_ready, 1)
        invert_act(act)
        experts_act(act)
        weigh_act(act)

    @block.vector
    def _(dve):
        V = nc.vector

        def softmax_shift(i, j, p):
            n = pair_no(i, j, p)
            dve.wait_ge(scores_ready, n + 1)
            V.reduce_max(rmax[p % 2][:], ps_s[p % 2][:], AX.X).then_inc(rmax_ready, 1)
            wait(dve, probsT_filled, 2 * (n - 1))
            dve.wait_ge(rmax_ready, n + 1)
            V.tensor_tensor(probs[p % 2][:], ps_s[p % 2][:],
                            rmax[p % 2][:].unsqueeze(2).broadcast_to([P, HEADS, SEQ]), ALU.subtract)\
             .then_inc(centered, 1)

        def normalise(i, j, p):
            n, r, u = pair_no(i, j, p), j % 2, att_use(i, j, p)
            dve.wait_ge(ring_filled, u.filled())
            halves = []
            for b in range(2):
                rows = slice(SEQ * b, SEQ * b + SEQ)
                at = b * (VW + PAD)
                o = ring[u.bank][rows, at:at + VW].rearrange("p (h c) -> p h c", h=HEADS)
                halves.append((rows, o))
                last = V.reciprocal(rden[p % 2][rows, :], o[:, :, D])
            last.then_inc(rden_ready, 1)
            dve.wait_ge(rden_ready, n + 1)
            for rows, o in halves:
                last = V.tensor_tensor(att[r][rows, p, :].rearrange("p (h d) -> p h d", h=HEADS), o[:, :, 0:D],
                                       rden[p % 2][rows, :].unsqueeze(2).broadcast_to([SEQ, HEADS, D]), ALU.mult)
            last.then_inc(ring_drained[u.bank], 1)

        def stats_of(m, src):
            for s in range(SUB):
                last = V.bn_stats(stats[:, s, :], src[:, s, :])
            last.then_inc(stats_ready, 1)
            wait_plain(stats_ready, m)
            for s in range(SUB):
                last = V.bn_aggr(mv[:, s, :], stats[:, s, :])
            last.then_inc(mv_ready, 1)

        def apply(factors_at, src, pieces):
            dve.wait_ge(pool_step, factors_at)
            for dst, factor, centre in pieces:
                for s in range(SUB):
                    if centre:
                        last = V.tensor_scalar(dst[:, s, :], src[:, s, :], mv[:, s, 0:1], factor[:, s:s + 1],
                                               ALU.subtract, ALU.mult)
                    else:
                        last = V.tensor_scalar(dst[:, s, :], src[:, s, :], factor[:, s:s + 1], None, ALU.mult)
            last.then_inc(normed, 1)

        def wait_plain(sem_, value):
            dve.wait_ge(sem_, value)
            V.tensor_copy(carrier[:], small[:, 0:1])

        def pre_stats(i, j):
            kind, r = kind_of(j), j % 2
            if kind == 0:
                dve.wait_ge(x_loaded[r], 16 * (tile_turn(i, j) + 1))
            else:
                u = source(i, j - 2, "wo" if kind == 1 else "ff")
                dve.wait_ge(ring_drained[u.bank], u.drained())
            stats_of(norm_index(i, j, "pre"), (xin if kind == 0 else xres)[r])

        def pre_apply(i, j):
            kind, r = kind_of(j), j % 2
            if isinstance(i, int) and i == 0 and j <= 1:
                at = 2 * (j + 1)
            else:
                at = steps_before(i, j - 1) + (5 if kind == 2 else 2)
            src = (xin if kind == 0 else xres)[r]
            apply(at, src, ((fres[r], rstd, True), (xh, rboth, True)) if kind == 2 else ((xh, rstd, True),))

        def values_out(u, i, j, half):
            r = j % 2
            dve.wait_ge(ring_filled, u.filled())
            ps_g = ring[u.bank]
            v = vbd[r][:, 4 * half * VW:4 * (half + 1) * VW].rearrange("p (b k c) -> p b k c", b=4, k=HEADS // 2)
            ps = ps_g[:].rearrange("p (b k c) -> p b k c", b=4, k=HEADS // 2)
            for q in range(2):
                rows = slice(SEQ * q, SEQ * q + SEQ)
                last = V.tensor_copy(v[rows, :, :, q * (D + 1):q * (D + 1) + D], ps[rows, :, :, q * D:q * D + D])
            last.then_inc(ring_drained[u.bank], 1)

        def table(c):
            return const[:, c:c + SEQ].unsqueeze(1).broadcast_to([P, 2 * SUB, SEQ])

        def by_seq(ap):
            return ap.rearrange("p (b q) -> p b q", q=SEQ)

        def use(u, name, i, j):
            kind, r = kind_of(j), j % 2
            if name == "st":
                pre_stats(i, j)
            elif name == "ap":
                pre_apply(i, j)
            elif name == "st2":
                wo = source(i, j, "wo")
                dve.wait_ge(ring_drained[wo.bank], wo.drained())
                stats_of(norm_index(i, j, "post"), hres)
            elif name == "ap2":
                dve.wait_ge(exported, EXPORT * (tile_no(i, j) + 1))
                apply(rms_at(i, j), hres, ((hn, rstd, False),))
            elif name in ("v0", "v1"):
                values_out(u, i, j, int(name[1]))
            elif name in ("wo", "ff", "lg", "qr", "kr") or (kind == 2 and name in ("q", "k")):
                if name == "ff":
                    dve.wait_ge(b2_added, tile_no(i, j) + 1)
                dve.wait_ge(ring_filled, u.filled())
                ps_g = ring[u.bank]
                drained = ring_drained[u.bank]
                by_sub = ps_g[:].rearrange("p (s e) -> p s e", s=SUB)
                if name == "wo" and kind == 0:
                    V.tensor_tensor(xres[r][:], by_sub, xin[r][:], ALU.add).then_inc(drained, 1)
                elif name == "ff":
                    V.tensor_tensor(xres[r][:], by_sub, xres[r][:], ALU.add).then_inc(drained, 1)
                elif name == "wo":
                    V.tensor_tensor(hres[:], by_sub, fres[r][:], ALU.add).then_inc(drained, 1)
                elif name == "lg":
                    t = tile_no(i, j)
                    sl = slice(t * SUB, t * SUB + SUB) if isinstance(t, int) else bass.ds(t * SUB, SUB)
                    V.tensor_copy(lg_all[:, sl, :], ps_g[:, 0:SUB * EXPERTS].rearrange("p (s e) -> p s e", s=SUB))\
                     .then_inc(drained, 1)
                    dve.wait_ge(drained, u.drained())
                    V.tensor_tensor(base[:], hres[:], xres[r][:], ALU.add).then_inc(export_ready, 1)
                elif name in ("q", "k"):
                    V.tensor_tensor(by_seq(rope[:, 0, :]), by_seq(ps_g[:]), table(C_COS), ALU.mult)\
                     .then_inc(drained, 1)
                else:
                    V.tensor_tensor(by_seq(rope[:, 1, :]), by_seq(ps_g[:]), table(C_SIN), ALU.mult)\
                     .then_inc(drained, 1)
                    dve.wait_ge(drained, u.drained())
                    if name == "kr":
                        for g in range(2):
                            wait(dve, kbd_loaded[r][g], 8 * HEADS * job_turn(i, j))
                    dst = (qT if name == "qr" else kS)[r]
                    V.tensor_tensor(dst[:], rope[:, 0, :], rope[:, 1, :], ALU.add).then_inc(rotated, 1)

        def rms_at(i, j):
            if isinstance(i, int) and i == ITERS - 1:
                return steps_before(i, JOBS - 1) + (4 if j == JOBS - 2 else 8)
            return steps_before(i, j + 1) + 6

        V.memset(kbd[0][:, 0:HEADS // 2, :], 0.0).then_inc(keys_cleared[0], 1)
        dve.wait_ge(small_ready, 1)
        pre_stats(0, 0)
        pre_apply(0, 0)
        dve.wait_ge(first_loaded, 16 * N_FIRST_LOADS)
        V.tensor_copy(identb[:], ident)
        V.tensor_copy(wide_b[:], const[:, C_WIDE:C_WIDE + P])
        V.tensor_copy(maskb[:], const[:, C_MASK:C_MASK + SEQ]).then_inc(casts_ready, 1)
        dve.wait_ge(pool_const, 1)
        for k, name in enumerate(PRE0):
            use(Use(0, k), name, 0, 0)
        dve.wait_ge(weights_loaded, 16 * N_LOADS)
        for k in range(2):
            V.tensor_scalar(w_f[:, k, :], w_given_f[:, k, :], cols[:, 5:6], None, ALU.mult)
        V.tensor_scalar(w_f[:, 2, :], w_f[:, 2, :], cols[:, 5:6], None, ALU.mult)
        V.tensor_scalar(w_r[:], w_r[:], cols[:, 6:7], None, ALU.mult).then_inc(const_ready, 1)
        pre_stats(0, 1)
        pre_apply(0, 1)

        def slot(i, j):
            for p in range(SUB):
                for k in range(5):
                    if p < SUB - 1 and k == SHIFT_AT[j][p]:
                        softmax_shift(i, j, p + 1)
                    if k == 1 and p > 0:
                        normalise(i, j, p - 1)
                    if k < 4:
                        for u, name, jj in steps_at(i, j, p, k - (k > 1)) if k != 1 else ():
                            use(u, name, i, jj)
            if j in SHIFT_FIRST and not is_last(i, j):
                softmax_shift(i, j + 1, 0)
            normalise(i, j, SUB - 1)
            if j not in SHIFT_FIRST and not is_last(i, j):
                softmax_shift(i, j + 1, 0)

        softmax_shift(0, 0, 0)
        walk(dve, slot)
        for name in TAIL:
            use(None if name in NOT_ON_PE else tail_use(name), name, ITERS - 1, JOBS - 1)
        route_dve(dve)
        experts_dve(dve)
        combine_dve(dve)

    @block.gpsimd
    def _(pool):
        G = nc.gpsimd
        var, mean = mv[:, :, 1], mv[:, :, 0]
        eps5, eps6, neg_half = small[:, 0:4], small[:, 4:8], small[:, 8:12]
        G.memset(small[:, 0:4], 1e-5)
        G.memset(small[:, 4:8], 1e-6)
        G.memset(small[:, 8:12], -0.5).then_inc(small_ready, 1)
        G.memset(ones[:], 1.0)
        for r in range(2):
            last = G.memset(vbd[r][:], 0.0)
        last.then_inc(pool_clear, 1)
        pool.wait_ge(pool_clear, 1)
        for r in range(2):
            v = vbd[r][:, 0:2 * SUB * VW].rearrange("p (b k c) -> p b k c", b=2 * SUB, k=HEADS // 2)
            for q in range(2):
                rows = slice(SEQ * q, SEQ * q + SEQ)
                last = G.memset(v[rows, :, :, q * (D + 1) + D:q * (D + 1) + D + 1], 1.0)
        last.then_inc(pool_const, 1)

        def chain(k0):
            count = [k0]

            def step(out_, x, y, op):
                wait(pool, pool_step, count[0])
                G.tensor_tensor(out_, x, y, op).then_inc(pool_step, 1)
                count[0] = count[0] + 1
            return step

        def layer_norm(k0, m, both):
            step = chain(k0)
            pool.wait_ge(mv_ready, m)
            step(pt[:, 0, :], var, eps5, ALU.add)
            step(rstd[:], pt[:, 0, :], neg_half, ALU.pow)
            if both:
                step(pt[:, 1, :], pt[:, 0, :], eps6, ALU.mult)
                step(pt[:, 2, :], pt[:, 1, :], var, ALU.add)
                step(rboth[:], pt[:, 2, :], neg_half, ALU.pow)

        def rms(k0, m):
            step = chain(k0)
            pool.wait_ge(mv_ready, m)
            step(pt[:, 0, :], mean, mean, ALU.mult)
            step(pt[:, 1, :], pt[:, 0, :], var, ALU.add)
            step(pt[:, 2, :], pt[:, 1, :], eps6, ALU.add)
            step(rstd[:], pt[:, 2, :], neg_half, ALU.pow)

        pool.wait_ge(pool_const, 1)
        layer_norm(0, 1, False)
        G.memset(kbd[0][:, HEADS // 2:, :], 0.0).then_inc(keys_cleared[0], 1)
        G.memset(kbd[1][:], 0.0).then_inc(keys_cleared[1], 1)
        layer_norm(2, 2, False)

        def slot(i, j):
            if j == 0:
                return
            k0, m = steps_before(i, j), norms_before(i, j) + 1
            if j in (1, 2):
                layer_norm(k0, m, False)
                pool.wait_ge(normed, m)
                G.tensor_tensor(xres[j - 1][:], xres[j - 1][:], b2[:].unsqueeze(1).broadcast_to([P, SUB, E]),
                                ALU.add).then_inc(b2_added, 1)
            elif j in (3, 4):
                layer_norm(k0, m, True)
            elif is_last(i, j):
                rms(k0, m)
            else:
                layer_norm(k0, m, False)
                rms(k0 + 2, m + 1)

        walk(pool, slot)
        rms(steps_before(ITERS - 1, JOBS - 1) + 4, norms_before(ITERS - 1, JOBS - 1) + 2)
        invert_pool(pool)
        experts_pool(pool)


INPUTS = ["x", "ctx_768", "L0_attn_in_proj_weight", "L0_attn_out_proj_weight",
          "L0_xattn_Wq", "L0_xattn_bq", "L0_xattn_Wk", "L0_xattn_bk", "L0_xattn_Wv", "L0_xattn_bv",
          "L0_xattn_W1", "L0_xattn_b1", "L0_xattn_W2", "L0_xattn_b2",
          "L0_ffn_wq", "L0_ffn_wk", "L0_ffn_wv", "L0_ffn_wo", "L0_ffn_w_router",
          "L0_ffn_wg", "L0_ffn_wu", "L0_ffn_wd", "L0_ffn_g1", "L0_ffn_g2"]


def kernel(**inputs):
    import numpy as _np
    import concourse.bacc as _bacc
    from concourse import mybir as _mybir
    from concourse.bass_utils import run_bass_kernel_spmd as _run

    nc = _bacc.Bacc("TRN2", target_bir_lowering=False, num_devices=1)
    arrays = {f"in_{n}": _np.ascontiguousarray(inputs[n]) for n in INPUTS}
    arrays["in_const"] = constants()
    args = {n[3:]: nc.dram_tensor(n, v.shape, _mybir.dt.from_np(v.dtype), kind="ExternalInput").ap()
            for n, v in arrays.items()}
    out = nc.dram_tensor("out", (BATCH, SEQ, E), F32, kind="ExternalOutput").ap()
    build(nc, args, out)
    r = _run(nc, [arrays], core_ids=[0])
    return r.results[0]["out"]
```
